# Optimizing a Trainium2 kernel written in Bass

```python
import numpy as np
import jax
import jax.numpy as jnp

def _softmax(x, axis=-1):
    return jax.nn.softmax(x, axis=axis)

def _gelu(x):
    return jax.nn.gelu(x, approximate=True)

def _silu(x):
    return jax.nn.silu(x)

def _sigmoid(x):
    return jax.nn.sigmoid(x)

def _layernorm(x, axis=-1, eps=1e-05):
    m = jnp.mean(x, axis=axis, keepdims=True)
    v = jnp.var(x, axis=axis, keepdims=True)
    return (x - m) / jnp.sqrt(v + eps)

def _scatter_add(tgt, idx, src, axis=0):
    return tgt.at[idx].add(src)

def _segment_sum(src, seg, n):
    return jax.ops.segment_sum(src, seg, n)
kernel_name = 'mk_audio_tower_d2_tok_audfeat512_r4_73eaf7'

def setup_inputs(seed: int=0):
    np.random.seed(seed)
    _w = jnp.asarray

    def _rec_inputs():
        import jax
        import jax.numpy as jnp
        _rk = jax.random.key(seed)
        x = 3.78913e-05 + 1.00016 * jax.random.normal(jax.random.fold_in(_rk, 1), (8, 375, 64), jnp.float32)
        return x
    x = _rec_inputs()

    def _L0_tok_setup():
        import jax, jax.numpy as jnp
        import numpy as np
        CONTEXT = 5
        DILATION = 1
        EPS = 1e-05
        key = jax.random.key(seed)
        k1, k2, k3 = jax.random.split(key, 3)
        B, T, D, O = (64, 500, 64, 128)
        x = jax.random.normal(k1, (B, T, D), dtype=jnp.float32)
        K = D * CONTEXT
        W = jax.random.normal(k2, (O, K), dtype=jnp.float32) / np.sqrt(K).astype(np.float32)
        b = jax.random.normal(k3, (O,), dtype=jnp.float32) * 0.01
        gamma = jnp.ones((O,), dtype=jnp.float32)
        beta = jnp.zeros((O,), dtype=jnp.float32)
        return {'x': x, 'W': W, 'b': b, 'gamma': gamma, 'beta': beta}
    _L0_tok_all = _L0_tok_setup()
    _L0_tok_in = {k: v for k, v in _L0_tok_all.items() if k in ('W', 'b', 'gamma', 'beta')}
    del _L0_tok_all

    def _L0_attn_setup():
        import jax, jax.numpy as jnp
        import numpy as np
        D_MODEL, D_STATE, D_CONV, EXPAND = (128, 16, 4, 2)
        D_INNER = EXPAND * D_MODEL
        DT_RANK = (D_MODEL + 15) // 16
        B, L = (4, 512)
        key = jax.random.key(seed)
        ks = jax.random.split(key, 12)
        s = lambda k, shape, sc: jax.random.normal(k, shape, jnp.float32) * sc
        inp = {'x': s(ks[0], (B, L, D_MODEL), 1.0), 'ln_g': jnp.ones((D_MODEL,), jnp.float32), 'ln_b': jnp.zeros((D_MODEL,), jnp.float32), 'W_in': s(ks[1], (2 * D_INNER, D_MODEL), D_MODEL ** (-0.5)), 'conv_w': s(ks[2], (D_INNER, 1, D_CONV), D_CONV ** (-0.5)), 'conv_b': s(ks[3], (D_INNER,), 0.02), 'W_x': s(ks[4], (DT_RANK + 2 * D_STATE, D_INNER), D_INNER ** (-0.5)), 'W_dt': s(ks[5], (D_INNER, DT_RANK), DT_RANK ** (-0.5)), 'b_dt': jnp.full((D_INNER,), -4.6, jnp.float32), 'A_log': jnp.log(jnp.broadcast_to(jnp.arange(1, D_STATE + 1, dtype=jnp.float32), (D_INNER, D_STATE))), 'D': jnp.ones((D_INNER,), jnp.float32), 'W_out': s(ks[6], (D_MODEL, D_INNER), D_INNER ** (-0.5))}
        return inp
    _L0_attn_all = _L0_attn_setup()
    _L0_attn_in = {k: v for k, v in _L0_attn_all.items() if k in ('ln_g', 'ln_b', 'W_in', 'conv_w', 'conv_b', 'W_x', 'W_dt', 'b_dt', 'A_log', 'D', 'W_out')}
    del _L0_attn_all

    def _L0_ffn_setup():
        import jax, jax.numpy as jnp
        import numpy as np
        B, S, D = (16, 512, 128)
        E, TOP_K = (8, 2)
        H = 4 * D
        key = jax.random.key(seed)
        ks = jax.random.split(key, 8)
        x = jax.random.normal(ks[0], (B, S, D), dtype=jnp.float32)
        gate_w = jax.random.normal(ks[1], (D, E), dtype=jnp.float32) * 0.02
        gate_b = jnp.zeros((E,), dtype=jnp.float32)
        w1 = jax.random.normal(ks[2], (E, D, H), dtype=jnp.float32) * 0.02
        b1 = jnp.zeros((E, H), dtype=jnp.float32)
        w2 = jax.random.normal(ks[3], (E, H, D), dtype=jnp.float32) * 0.02
        b2 = jnp.zeros((E, D), dtype=jnp.float32)
        return {'x': x, 'gate_w': gate_w, 'gate_b': gate_b, 'w1': w1, 'b1': b1, 'w2': w2, 'b2': b2}
    _L0_ffn_all = _L0_ffn_setup()
    _L0_ffn_in = {k: v for k, v in _L0_ffn_all.items() if k in ('gate_w', 'gate_b', 'w1', 'b1', 'w2', 'b2')}
    del _L0_ffn_all

    def _L1_attn_setup():
        import jax, jax.numpy as jnp
        import numpy as np
        SCALE = 64 ** 0.5
        key = jax.random.key(seed)
        kx, kw = jax.random.split(key)
        B, S, D, O = (8, 512, 128, 128)
        x = jax.random.normal(kx, (B, S, D), dtype=jnp.float32)
        kernel = jax.random.normal(kw, (3, D, O), dtype=jnp.float32) * 0.02
        return {'x': x, 'kernel': kernel}
    _L1_attn_all = _L1_attn_setup()
    _L1_attn_in = {k: v for k, v in _L1_attn_all.items() if k in ('kernel',)}
    del _L1_attn_all

    def _L1_ffn_setup():
        import jax, jax.numpy as jnp
        import numpy as np
        B, L, H, E, F, C = (8, 2048, 128, 8, 256, 2)
        key = jax.random.key(seed)
        ks = jax.random.split(key, 4)
        x = jax.random.normal(ks[0], (B, L, H), jnp.float32)
        Wg = jax.random.normal(ks[1], (H, E), jnp.float32) * H ** (-0.5)
        W1 = jax.random.normal(ks[2], (E, H, F), jnp.float32) * H ** (-0.5)
        b1 = jnp.zeros((E, F), jnp.float32)
        W2 = jax.random.normal(ks[3], (E, F, H), jnp.float32) * F ** (-0.5)
        b2 = jnp.zeros((E, H), jnp.float32)
        return {'x': x, 'Wg': Wg, 'W1': W1, 'b1': b1, 'W2': W2, 'b2': b2}
    _L1_ffn_all = _L1_ffn_setup()
    _L1_ffn_in = {k: v for k, v in _L1_ffn_all.items() if k in ('Wg', 'W1', 'b1', 'W2', 'b2')}
    del _L1_ffn_all
    return {'x': x, 'L0_tok_W': _L0_tok_in['W'], 'L0_tok_b': _L0_tok_in['b'], 'L0_tok_gamma': _L0_tok_in['gamma'], 'L0_tok_beta': _L0_tok_in['beta'], 'L0_attn_ln_g': _L0_attn_in['ln_g'], 'L0_attn_ln_b': _L0_attn_in['ln_b'], 'L0_attn_W_in': _L0_attn_in['W_in'], 'L0_attn_conv_w': _L0_attn_in['conv_w'], 'L0_attn_conv_b': _L0_attn_in['conv_b'], 'L0_attn_W_x': _L0_attn_in['W_x'], 'L0_attn_W_dt': _L0_attn_in['W_dt'], 'L0_attn_b_dt': _L0_attn_in['b_dt'], 'L0_attn_A_log': _L0_attn_in['A_log'], 'L0_attn_D': _L0_attn_in['D'], 'L0_attn_W_out': _L0_attn_in['W_out'], 'L0_ffn_gate_w': _L0_ffn_in['gate_w'], 'L0_ffn_gate_b': _L0_ffn_in['gate_b'], 'L0_ffn_w1': _L0_ffn_in['w1'], 'L0_ffn_b1': _L0_ffn_in['b1'], 'L0_ffn_w2': _L0_ffn_in['w2'], 'L0_ffn_b2': _L0_ffn_in['b2'], 'L1_attn_kernel': _L1_attn_in['kernel'], 'L1_ffn_Wg': _L1_ffn_in['Wg'], 'L1_ffn_W1': _L1_ffn_in['W1'], 'L1_ffn_b1': _L1_ffn_in['b1'], 'L1_ffn_W2': _L1_ffn_in['W2'], 'L1_ffn_b2': _L1_ffn_in['b2']}

def reference(x, L0_tok_W, L0_tok_b, L0_tok_gamma, L0_tok_beta, L0_attn_ln_g, L0_attn_ln_b, L0_attn_W_in, L0_attn_conv_w, L0_attn_conv_b, L0_attn_W_x, L0_attn_W_dt, L0_attn_b_dt, L0_attn_A_log, L0_attn_D, L0_attn_W_out, L0_ffn_gate_w, L0_ffn_gate_b, L0_ffn_w1, L0_ffn_b1, L0_ffn_w2, L0_ffn_b2, L1_attn_kernel, L1_ffn_Wg, L1_ffn_W1, L1_ffn_b1, L1_ffn_W2, L1_ffn_b2):
    import jax
    import jax.numpy as jnp

    def _L0_tok_ref(x, W, b, gamma, beta):
        import jax, jax.numpy as jnp
        import numpy as np
        CONTEXT = 5
        DILATION = 1
        EPS = 1e-05
        B, T, D = x.shape
        new_T = T - DILATION * (CONTEXT - 1)
        win = jnp.concatenate([x[:, i * DILATION:i * DILATION + new_T, :] for i in range(CONTEXT)], axis=-1)
        y = jnp.einsum('btk,ok->bto', win, W) + b
        y = jax.nn.relu(y)
        mean = jnp.mean(y, axis=(0, 1))
        var = jnp.mean(jnp.square(y - mean), axis=(0, 1))
        y = (y - mean) * jax.lax.rsqrt(var + EPS) * gamma + beta
        return y

    def _L0_attn_ref(x, ln_g, ln_b, W_in, conv_w, conv_b, W_x, W_dt, b_dt, A_log, D, W_out):
        import jax, jax.numpy as jnp
        import numpy as np
        D_MODEL, D_STATE, D_CONV, EXPAND = (128, 16, 4, 2)
        D_INNER = EXPAND * D_MODEL
        DT_RANK = (D_MODEL + 15) // 16
        B, L = (4, 512)
        mu = x.mean(-1, keepdims=True)
        var = x.var(-1, keepdims=True)
        xn = (x - mu) * jax.lax.rsqrt(var + 1e-05) * ln_g + ln_b
        xz = jnp.einsum('bld,ed->ble', xn, W_in)
        xi, z = (xz[..., :D_INNER], xz[..., D_INNER:])
        xc = jax.lax.conv_general_dilated(xi.transpose(0, 2, 1), conv_w, (1,), [(D_CONV - 1, 0)], dimension_numbers=('NCH', 'OIH', 'NCH'), feature_group_count=D_INNER)
        xc = jax.nn.silu(xc.transpose(0, 2, 1) + conv_b)
        x_dbl = jnp.einsum('bld,rd->blr', xc, W_x)
        dt = jax.nn.softplus(jnp.einsum('blr,dr->bld', x_dbl[..., :DT_RANK], W_dt) + b_dt)
        Bm = x_dbl[..., DT_RANK:DT_RANK + D_STATE]
        Cm = x_dbl[..., DT_RANK + D_STATE:]
        A = -jnp.exp(A_log)

        def step(h, ins):
            dt_t, B_t, C_t, u_t = ins
            dA = jnp.exp(dt_t[..., None] * A)
            h = dA * h + dt_t[..., None] * B_t[:, None, :] * u_t[..., None]
            y = jnp.einsum('bds,bs->bd', h, C_t)
            return (h, y)
        h0 = jnp.zeros((x.shape[0], D_INNER, D_STATE), xc.dtype)
        xs = (dt.transpose(1, 0, 2), Bm.transpose(1, 0, 2), Cm.transpose(1, 0, 2), xc.transpose(1, 0, 2))
        _, ys = jax.lax.scan(step, h0, xs)
        y = ys.transpose(1, 0, 2) + xc * D
        y = y * jax.nn.silu(z)
        return jnp.einsum('bld,od->blo', y, W_out)

    def _L0_ffn_ref(x, gate_w, gate_b, w1, b1, w2, b2):
        import jax, jax.numpy as jnp
        import numpy as np
        B, S, D = (16, 512, 128)
        E, TOP_K = (8, 2)
        H = 4 * D
        b, s, d = x.shape
        e = gate_b.shape[0]
        pooled = x.mean(axis=1)
        logits = pooled @ gate_w + gate_b
        top_v, top_i = jax.lax.top_k(logits, TOP_K)
        weights = jax.nn.softmax(top_v, axis=-1)
        w_full = jnp.zeros((b, e), dtype=x.dtype).at[jnp.arange(b)[:, None], top_i].add(weights)
        out = jnp.zeros_like(x)
        for ex in range(e):
            h = jax.nn.gelu(x @ w1[ex] + b1[ex], approximate=False)
            y = h @ w2[ex] + b2[ex]
            out = out + y * w_full[:, ex][:, None, None]
        return out

    def _L1_attn_ref(x, kernel):
        import jax, jax.numpy as jnp
        import numpy as np
        SCALE = 64 ** 0.5
        WQ = jnp.einsum('bsd,do->bso', x, kernel[0])
        WK = jnp.einsum('bsd,do->bso', x, kernel[1])
        WV = jnp.einsum('bsd,do->bso', x, kernel[2])
        QK = jnp.einsum('bso,bto->bst', WQ, WK)
        row_sums = jnp.sum(QK, axis=2)
        c0 = jnp.argmin(row_sums[0])
        A = jax.nn.softmax(QK / SCALE, axis=-1)
        row_mask = (jnp.arange(QK.shape[1]) == c0)[None, :, None]
        A = jnp.where(row_mask, jnp.zeros((), A.dtype), A)
        V = jnp.einsum('bst,bto->bso', A, WV)
        return V

    def _L1_ffn_ref(x, Wg, W1, b1, W2, b2):
        import jax, jax.numpy as jnp
        import numpy as np
        B, L, H, E, F, C = (8, 2048, 128, 8, 256, 2)
        b, l, h = x.shape
        e = Wg.shape[1]
        k = min(max(int(l * C / e), 1), l)
        S = jax.nn.softmax(x @ Wg, axis=-1)
        St = jnp.swapaxes(S, 1, 2)
        G, I = jax.lax.top_k(St, k)
        ex = jnp.take_along_axis(x[:, None], I[..., None], axis=2)
        hmid = jax.nn.gelu(jnp.einsum('bekh,ehf->bekf', ex, W1) + b1[None, :, None, :], approximate=False)
        out = jnp.einsum('bekf,efh->bekh', hmid, W2) + b2[None, :, None, :]
        vals = G[..., None] * out
        new_x = jnp.zeros_like(x).at[jnp.arange(b)[:, None, None], I].add(vals)
        return new_x
    h = _L0_tok_ref(x, L0_tok_W, L0_tok_b, L0_tok_gamma, L0_tok_beta)
    h = h + _L0_attn_ref(_layernorm(h, axis=-1), L0_attn_ln_g, L0_attn_ln_b, L0_attn_W_in, L0_attn_conv_w, L0_attn_conv_b, L0_attn_W_x, L0_attn_W_dt, L0_attn_b_dt, L0_attn_A_log, L0_attn_D, L0_attn_W_out)
    h = h + _L0_ffn_ref(_layernorm(h, axis=-1), L0_ffn_gate_w, L0_ffn_gate_b, L0_ffn_w1, L0_ffn_b1, L0_ffn_w2, L0_ffn_b2)
    h = h + _L1_attn_ref(_layernorm(h, axis=-1), L1_attn_kernel)
    h = h + _L1_ffn_ref(_layernorm(h, axis=-1), L1_ffn_Wg, L1_ffn_W1, L1_ffn_b1, L1_ffn_W2, L1_ffn_b2)
    return h

_drawn_inputs = setup_inputs


def setup_inputs(seed=0):
    import zlib

    import numpy as np

    out = dict(_drawn_inputs(seed))
    spreads = {'L0_tok_gamma': (1.0, 0.2),
     'L0_tok_beta': (0.0, 0.1),
     'L0_attn_ln_g': (1.0, 0.2),
     'L0_attn_ln_b': (0.0, 0.1),
     'L0_attn_b_dt': (-4.599999904632568, 0.553),
     'L0_attn_D': (1.0, 0.2),
     'L0_ffn_gate_b': (0.0, 0.1),
     'L0_ffn_b1': (0.0, 0.39),
     'L0_ffn_b2': (0.0, 0.1),
     'L1_ffn_b1': (0.0, 0.308),
     'L1_ffn_b2': (0.0, 0.1)}
    factors = {'L0_tok_b': 4.198, 'L0_attn_conv_b': 4.324, 'L0_ffn_gate_w': 2.746}
    for name, (base, spread) in spreads.items():
        noise = np.random.default_rng([zlib.crc32(name.encode()), seed]).standard_normal(out[name].shape)
        drawn = base * np.exp(spread * noise) if base else spread * noise
        out[name] = jnp.asarray(drawn.astype(out[name].dtype))
    for name, factor in factors.items():
        out[name] = (out[name] * factor).astype(out[name].dtype)
    return out
```

```python
from contextlib import ExitStack

import concourse.bass as bass
from concourse import mybir

F32 = mybir.dt.float32
BF16 = mybir.dt.bfloat16
U32 = mybir.dt.uint32
I32 = mybir.dt.int32
ALU = mybir.AluOpType
ACT = mybir.ActivationFunctionType
AX_X = mybir.AxisListType.X
LN_EXP = "natural_log_exp_and_others"

P = 128
BANK = 512
EPS = 1e-5

TOK_B, GAMMA, BETA, LN_G, LN_B, CONV_B, B_DT, D_SKIP, A_LOG, MOE1_B1, N_VEC = 0, 1, 2, 3, 4, 5, 7, 9, 11, 43, 59


class Signal:

    def __init__(self, sem, per_batch, head):
        self.sem, self.per_batch, self.head = sem, per_batch, head

    def at(self, b, n):
        return b * self.per_batch + (n + self.head)


def audio_tower(nc, x_t, tok_w, vec_in, conv_w, w_in, w_x, w_dt, w_out, gate_w, gate_b, moe0, qkv_w,
                router_w, moe1_w1, moe1_w2, moe1_b2, out, gates_dram, mask_dram, b_dram):
    B, T_IN = x_t.shape[1:]
    TAPS = 5
    T = T_IN - TAPS + 1
    TP = 3 * P
    TILES = [(0, P), (P, P), (2 * P, T - 2 * P)]
    HALVES = 2
    STATES = 16
    GROUP = 4
    GROUPS = STATES // GROUP
    RANK = 8
    CONV = 4
    E = 8
    H0T = 4
    TOP_TOKENS = max(T * 2 // E, 1)
    TOP_ROUNDS = -(-TOP_TOKENS // 8)
    SCORE_SCALE = 1.0 / 8.0
    BT = B * T
    W1_AT, W2_AT, B1_AT, B2_AT, PACK = 0, 512, 1024, 1028, 1029

    with ExitStack() as ctx:
        def sb(name, shape, dt=F32):
            return ctx.enter_context(nc.sbuf_tensor(name, shape, dt))

        def sem(name):
            return ctx.enter_context(nc.semaphore(name))

        def signal(name, per_batch=1, head=0):
            return Signal(sem(name), per_batch, head)

        c_rows = ctx.enter_context(nc.psum_tensor("c_rows", [P, 4, BANK], F32))
        y_bank = ctx.enter_context(nc.psum_tensor("y_bank", [P, BANK], F32))
        f_bank = ctx.enter_context(nc.psum_tensor("f_bank", [P, BANK], F32))
        p_bank = ctx.enter_context(nc.psum_tensor("p_bank", [P, 2, BANK], F32))

        mean_mat = sb("mean_mat", [P, P])
        ident = sb("ident", [P, P])
        ones_row = sb("ones_row", [1, P])
        pick = sb("pick", [96, STATES], BF16)
        token_index = sb("token_index", [1, T])
        vecs = sb("vecs", [P, N_VEC])
        neg_a = sb("neg_a", [P, HALVES * STATES])
        eps_col = sb("eps_col", [P, 3])
        w_in_sb = sb("w_in_sb", [P, 512])
        w_conv = sb("w_conv", [P, CONV, 256])
        w_x_sb = sb("w_x_sb", [P, HALVES, RANK + 2 * STATES])
        w_bc = sb("w_bc", [P, HALVES, 96])
        w_dt_sb = sb("w_dt_sb", [RANK, 256])
        w_out_sb = sb("w_out_sb", [P, HALVES, P])
        gate_w_sb = sb("gate_w_sb", [P, E])
        gate_b_sb = sb("gate_b_sb", [1, E])
        qkv_sb = sb("qkv_sb", [P, 3, P])
        router_sb = sb("router_sb", [P, E])
        moe1_w1_sb = sb("moe1_w1_sb", [P, E, 256])
        moe1_w2_sb = sb("moe1_w2_sb", [P, E, 2, P])
        moe1_b2_sb = sb("moe1_b2_sb", [E, P])

        x_area = sb("x_area", [P, B * T_IN])
        x2 = x_area[:, :].rearrange("p (b t) -> p b t", b=B)
        xn4_all = x_area[:, 0:BT]
        tok_y = sb("tok_y", [P, BT])
        h3_all = tok_y
        bn_parts = sb("bn_parts", [P, B, 6])
        bn = sb("bn", [P, 2])
        tok_rs = sb("tok_rs", [P, 6])

        h0 = [sb(f"h0_{i}", [P, T]) for i in range(2)]
        f_centered = sb("f_centered", [P, T])
        ssm_in = sb("ssm_in", [P, CONV - 1 + T])
        xc = [sb(f"xc{i}", [P, HALVES, T]) for i in range(2)]
        zs = [sb(f"zs{i}", [P, HALVES, T]) for i in range(2)]
        bc_rest = sb("bc_rest", [96, T])
        bc_f32 = sb("bc_f32", [32, T])
        bc_mid = sb("bc_mid", [96, T], BF16)
        bc_parts = [sb(f"bc_parts{i}", [96, T], BF16) for i in range(2)]
        dt_low = sb("dt_low", [RANK, T])
        dt_soft = sb("dt_soft", [P, HALVES, T])
        f_square, f_rs = dt_soft[:, 0, :], dt_soft[:, 1, :]
        dt = [sb(f"dt{i}", [P, HALVES, T]) for i in range(2)]
        dtu = [sb(f"dtu{i}", [P, HALVES, T]) for i in range(2)]

        b_area = sb("b_area", [P, STATES * T])
        b_rows = b_area[:, :].rearrange("p (s t) -> p s t", s=STATES)
        tok_w_sb = b_area[:, 0:3 * P].rearrange("p (k o) -> p k o", k=3)
        scan_area = sb("scan_area", [P, 8, GROUP * T])
        decay, drive, state, read = ([scan_area[:, 2 * k + i, :] for i in range(2)] for k in range(4))
        y_gated = sb("y_gated", [P, HALVES, T])
        h1 = h0
        conv_rows = scan_area[:, 0, 0:CONV * 256].rearrange("p (j d) -> p j d", j=CONV)

        def by_state(area):
            return area.rearrange("p (s t) -> p s t", s=GROUP)

        centered = sb("centered", [P, T])
        square = sb("square", [P, T])
        rs = sb("rs", [P, T])
        spare = sb("spare", [1, 1])
        pooled = sb("pooled", [P, 1])
        gate_row = sb("gate_row", [1, E])
        top_v = sb("top_v", [1, 8])
        top_i = sb("top_i", [1, 8], U32)
        gate_tmp = sb("gate_tmp", [1, 4])
        w_pair = sb("w_pair", [1, 2])
        w_col = sb("w_col", [P, 2])
        expert = [sb(f"expert{j}", [P, PACK]) for j in range(2)]
        b2_mix = sb("b2_mix", [P, 2])
        h2 = sb("h2", [P, T])
        hid0 = sb("hid0", [P, H0T, T])
        probs = hid0
        xn3 = sb("xn3", [P, TP])
        xn2 = xn3[:, 0:T]
        q_t = sb("q_t", [P, TP])
        k_t = sb("k_t", [P, T])
        k_sum = sb("k_sum", [P, 1])
        v_sb = sb("v_sb", [P, 3, P])
        low_row = square[0:1, :]
        low_v = sb("low_v", [1, 8])
        low_i = sb("low_i", [1, 8], U32)
        low_f = sb("low_f", [1, 1])
        keep_row = sb("keep_row", [1, TP])
        keep = sb("keep", [P, 3])
        s_max = sb("s_max", [P, 3])
        s_bias = sb("s_bias", [P, 3])
        s_sum = sb("s_sum", [P, 3])
        s_inv = sb("s_inv", [P, 3])
        s_scale = sb("s_scale", [P, 3])
        probs_t = sb("probs_t", [P, 3, TP])
        xn4 = sb("xn4", [P, TP])
        r_max = sb("r_max", [P, 3])
        r_cent = sb("r_cent", [P, 3, E])
        r_exp = sb("r_exp", [P, 3, E])
        r_sum = sb("r_sum", [P, 3])
        r_inv = sb("r_inv", [P, 3])
        r_prob = sb("r_prob", [P, 3, E])
        gates_t = sb("gates_t", [E, T])

        gates_e = scan_area[0:96, 0:2, :].rearrange("p a n -> p (a n)")
        gates_rest = scan_area[0:96, 2:4, :].rearrange("p a n -> p (a n)")
        gates_parts = scan_area[0:96, 4, :].bitcast(BF16)
        gates_mid = scan_area[0:96, 5, :].bitcast(BF16)
        top_in = scan_area[0:B * E, 6, 0:T]
        top_work = [scan_area[0:B * E, 6, T * (1 + i):T * (2 + i)] for i in range(2)]
        gates_masked = scan_area[0:B * E, 6, 3 * T:4 * T]
        top_8 = sb("top_8", [B * E, 8])
        hid1 = [b_area[:, 2 * T * i:2 * T * (i + 1)].rearrange("p (f t) -> p f t", f=2) for i in range(2)]
        hid1_g = [b_area[:, 2 * T * i:2 * T * (i + 1)].rearrange("p (f t) -> p f t", f=2) for i in (2, 3)]
        out_sb = [b_area[:, T * i:T * (i + 1)] for i in (8, 9)]

        x_loaded, tokw_loaded, vec_loaded, ssm_loaded, gate_loaded, moe1_loaded = (
            sem(n) for n in ("x_loaded", "tokw_loaded", "vec_loaded", "ssm_loaded", "gate_loaded", "moe1_loaded"))
        ident_step, pick_step, index_step, pads_ready, granted = (
            sem(n) for n in ("ident_step", "pick_step", "index_step", "pads_ready", "granted"))
        tok_mm, tok_relu, bn_part, tok_step, tok_act = (
            sem(n) for n in ("tok_mm", "tok_relu", "bn_part", "tok_step", "tok_act"))
        a_exp, a_ready, weights_made = sem("a_exp"), sem("a_ready"), sem("weights_made")

        F_MEAN, F_VAR, F_XI, F_Z, F_BC, F_DT_LOW, F_DT, NF = 0, 1, 2, 4, 6, 7, 8, 10
        f_mm = signal("f_mm", NF)
        f_read = signal("f_read", NF, head=1)
        h0_ready = signal("h0_ready")
        f_squared = signal("f_squared")
        f_rs_ready = signal("f_rs_ready")
        f_scaled = signal("f_scaled")
        ssm_in_ready = signal("ssm_in_ready")
        bc_hi = signal("bc_hi")
        bc_copied = signal("bc_copied")
        bc_mids = signal("bc_mids")
        bc_ready = signal("bc_ready")
        b_stored = signal("b_stored", 16)
        b_loaded = [signal(f"b_loaded{g}", 16) for g in range(GROUPS)]
        dt_abs_ready = signal("dt_abs_ready", 2)
        dt_exp_ready = signal("dt_exp_ready")
        dt_ln_ready = signal("dt_ln_ready")
        dt_ready = signal("dt_ready")
        dtu_ready = signal("dtu_ready")

        NG = HALVES * GROUPS
        decay_ready = signal("decay_ready", NG)
        drive_ready = signal("drive_ready", NG, head=4)
        state_ready = signal("state_ready", NG, head=2)
        c_ready = signal("c_ready", 2 * NG)
        read_ready = signal("read_ready", 2 * NG, head=3)
        read_summed = signal("read_summed", NG, head=2)
        y_mm = signal("y_mm", 3)
        y_read = signal("y_read", 3, head=1)
        y_gated_ready = signal("y_gated_ready", 2)

        P_MEAN2, P_VAR2, P_GATE, P_WCOL, P_UP0, P_DOWN0 = 0, 1, 2, 3, (4, 9), (8, 13)
        P_MEAN3, P_VAR3, P_Q, P_K, P_V, P_LOW, P_KEEP = 14, 15, 16, 17, 18, 19, 20
        P_SCORE, P_PROBS, P_ATTN, P_MEAN4, P_VAR4, P_ROUTER, P_GATES, NPT = 21, 24, 27, 28, 29, 30, 31, 32
        p_mm = signal("p_mm", NPT)
        p_read = [signal(f"p_read{i}", NPT // 2, head=1) for i in range(2)]
        squared = signal("squared", 3)
        rs_ready = signal("rs_ready", 3)
        xn2_ready = signal("xn2_ready")
        gate_step = signal("gate_step", 5)
        gate_exp_ready = signal("gate_exp_ready")
        experts_known = sem("experts_known")
        expert_loaded = [signal(f"expert_loaded{j}", 16) for j in range(2)]
        b2_step = signal("b2_step", 3)
        xn3_ready = signal("xn3_ready")
        low_step = sem("low_step")
        max_ready = signal("max_ready", 3)
        bias_ready = signal("bias_ready", 3)
        scale_step = signal("scale_step", 2)
        probs_scaled = signal("probs_scaled", 3)
        xn4_ready = signal("xn4_ready")
        router_step = signal("router_step", 4)
        router_exp_ready = signal("router_exp_ready")
        xn4_kept = signal("xn4_kept", 16, head=16)
        gates_kept = signal("gates_kept", 16, head=16)

        gates_loaded, top_step, mask_stored, mask_loaded, zeroed = (
            sem(n) for n in ("gates_loaded", "top_step", "mask_stored", "mask_loaded", "zeroed"))
        gates_hi, gates_left, gates_mids, gates_split = (
            sem(n) for n in ("gates_hi", "gates_left", "gates_mids", "gates_split"))
        up_mm = signal("up_mm", E)
        gate_rows_mm = signal("gate_rows_mm", E)
        hid1_ready = signal("hid1_ready", E, head=2)
        hid1_gated = signal("hid1_gated", E, head=2)
        down_mm = signal("down_mm", E, head=2)
        out_ready = signal("out_ready", 1, head=2)
        out_stored = signal("out_stored", 16, head=16)

        def wait(eng, s, b, n):
            eng.wait_ge(s.sem, s.at(b, n))

        def grant(eng, s):
            eng.sem_inc(s.sem, s.head)

        def per_batch(eng, run):
            with eng.Fori(0, B // 2) as pair:
                run(pair * 2, 0)
                run(pair * 2 + 1, 1)

        def cols(area, b):
            return area[:, bass.ds(b * T, T)]

        def vec(k):
            return vecs[:, k:k + 1]

        def p_tile(n):
            return p_bank[:, n % 2, :]

        def wait_p_read(eng, b, n):
            wait(eng, p_read[n % 2], b, n // 2 + 1)

        def then_p_read(ins, n):
            ins.then_inc(p_read[n % 2].sem, 1)

        block = ctx.enter_context(nc.Block())

        @block.sync
        def _(sp):
            sp.dma_start(x2[0:64, :, :], x_t).then_inc(x_loaded, 16)
            sp.dma_start(x2[64:P, :, 0:T_IN - 1], x_t[:, :, 1:T_IN]).then_inc(x_loaded, 16)
            sp.dma_start(w_in_sb[:, :], w_in).then_inc(ssm_loaded, 16)
            sp.dma_start(conv_rows, conv_w.partition_broadcast(P)).then_inc(ssm_loaded, 16)
            sp.dma_start(w_x_sb[:, :, :], w_x).then_inc(ssm_loaded, 16)
            sp.dma_start(w_dt_sb[:, :], w_dt).then_inc(ssm_loaded, 16)
            sp.dma_start(w_out_sb[:, :, :], w_out).then_inc(ssm_loaded, 16)
            sp.dma_start(gate_w_sb[:, :], gate_w).then_inc(gate_loaded, 16)
            sp.dma_start(gate_b_sb[:, :], gate_b).then_inc(gate_loaded, 16)
            sp.dma_start(qkv_sb[:, :, :], qkv_w).then_inc(gate_loaded, 16)
            sp.dma_start(router_sb[:, :], router_w).then_inc(gate_loaded, 16)
            sp.dma_start(moe1_w1_sb[:, :, :], moe1_w1).then_inc(moe1_loaded, 16)
            sp.dma_start(moe1_w2_sb[:, :, :, :], moe1_w2).then_inc(moe1_loaded, 16)
            sp.dma_start(moe1_b2_sb[:, :], moe1_b2).then_inc(moe1_loaded, 16)
            grant(sp, xn4_kept)
            grant(sp, gates_kept)
            grant(sp, out_stored)

            def front(b, i):
                wait(sp, bc_copied, b, 1)
                sp.dma_start(b_dram[i], bc_f32[16:32, :]).then_inc(b_stored.sem, 16)
                wait(sp, b_stored, b, 16)
                for g in range(GROUPS):
                    wait(sp, drive_ready, b - 1, GROUPS + g + 1)
                    sp.dma_start(b_rows[:, GROUP * g:GROUP * (g + 1), :],
                                 b_dram[i, GROUP * g:GROUP * (g + 1), :].partition_broadcast(P))\
                      .then_inc(b_loaded[g].sem, 16)

            def post(b, i):
                sp.wait_ge(experts_known, 1)
                chosen = [sp.value_load(top_i[0:1, j:j + 1], min_val=0, max_val=E - 1) for j in range(2)]
                sp.sem_clear(experts_known)
                for j, e in enumerate(chosen):
                    sp.dma_start(expert[j][:, :], moe0[bass.ds(e, 1), :, :].rearrange("a p n -> p (a n)"))\
                      .then_inc(expert_loaded[j].sem, 16)
                wait(sp, xn4_ready, b, 1)
                sp.dma_start(cols(xn4_all, b), xn4[:, 0:T]).then_inc(xn4_kept.sem, 16)
                wait_p_read(sp, b, P_GATES)
                sp.dma_start(gates_dram[bass.ds(b, 1), :, :].rearrange("a e t -> e (a t)"), gates_t[:, :])\
                  .then_inc(gates_kept.sem, 16)

            def batch(b, i):
                front(b, i)
                post(b, i)

            per_batch(sp, batch)

            wait(sp, gates_kept, B - 1, 16)
            sp.dma_start(top_in, gates_dram.rearrange("b e t -> (b e) t")).then_inc(gates_loaded, 16)
            sp.wait_ge(top_step, 2 * TOP_ROUNDS + (2 if TOP_TOKENS % 8 else 1))
            sp.dma_start(mask_dram.rearrange("b e t -> (b e) t"), gates_masked).then_inc(mask_stored, 16)
            sp.wait_ge(mask_stored, 16)
            sp.wait_ge(zeroed, 1)
            for k in range(3):
                sp.dma_start(gates_e[32 * k:32 * k + E, :].rearrange("e (b t) -> e b t", b=B),
                             mask_dram.rearrange("b e t -> e b t")).then_inc(mask_loaded, 16)

            def result(b, i):
                wait(sp, out_ready, b, 1)
                sp.dma_start(cols(out, b), out_sb[i]).then_inc(out_stored.sem, 16)

            per_batch(sp, result)
            wait(sp, out_stored, B - 1, 16)
            wait(sp, xn4_kept, B - 1, 16)

        @block.gpsimd
        def _(pool):
            pool.memset(ident[:, :], 0.0).then_inc(ident_step, 1)
            pool.wait_ge(ident_step, 1)
            pool.affine_select(out=ident[:, :], in_=ident[:, :], compare_op=ALU.not_equal, fill=1.0, base=0,
                               pattern=[[-1, P]], channel_multiplier=1).then_inc(ident_step, 1)
            pool.memset(mean_mat[:, :], 1.0 / P).then_inc(ident_step, 1)
            pool.memset(pick[:, :], 0.0).then_inc(pick_step, 1)
            for k in range(3):
                pool.wait_ge(pick_step, k + 1)
                pool.affine_select(out=pick[:, :], in_=pick[:, :], compare_op=ALU.not_equal, fill=1.0,
                                   base=-32 * k, pattern=[[-1, STATES]], channel_multiplier=1).then_inc(pick_step, 1)
            pool.iota(token_index[:, :], pattern=[[1, T]], base=0, channel_multiplier=0,
                      allow_small_or_imprecise_dtypes=True).then_inc(index_step, 1)
            grant(pool, drive_ready)

            def front(b, i):
                wait(pool, dt_ready, b, 1)
                wait(pool, f_read, b, F_XI + 2)
                pool.tensor_tensor(dtu[i][:, :, :], dt[i][:, :, :], xc[i][:, :, :], ALU.mult)\
                    .then_inc(dtu_ready.sem, 1)

            def scan(b, i):
                wait(pool, dtu_ready, b, 1)
                for g in range(NG):
                    half, states = g // GROUPS, g % GROUPS
                    if half == 0:
                        wait(pool, b_loaded[states], b, 16)
                    wait(pool, state_ready, b, g - 1)
                    pool.tensor_tensor(by_state(drive[g % 2]),
                                       dtu[i][:, half:half + 1, :].to_broadcast([P, GROUP, T]),
                                       b_rows[:, GROUP * states:GROUP * (states + 1), :], ALU.mult)\
                        .then_inc(drive_ready.sem, 1)

            def batch(b, i):
                front(b, i)
                scan(b, i)

            per_batch(pool, batch)
            wait(pool, y_read, B - 1, 3)
            pool.memset(gates_e, 0.0).then_inc(zeroed, 1)

        @block.scalar
        def _(act):
            act.dma_start(tok_w_sb, tok_w).then_inc(tokw_loaded, 16)
            act.dma_start(vecs[:, :], vec_in).then_inc(vec_loaded, 16)
            grant(act, hid1_ready)
            act.preload_act_table_set(LN_EXP)
            act.wait_ge(vec_loaded, 16)
            act.activation(neg_a[:, :], vecs[:, A_LOG:A_LOG + HALVES * STATES], ACT.Exp).then_inc(a_exp, 1)
            for b in range(B):
                act.wait_ge(tok_mm, b + 1)
                act.activation(tok_y[:, b * T:(b + 1) * T], c_rows[:, b % 4, 0:T], ACT.Relu, bias=vec(TOK_B))\
                   .then_inc(tok_relu, 1)
            act.wait_ge(tok_step, 2)
            act.activation(tok_rs[:, 1:2], tok_rs[:, 0:1], ACT.Ln).then_inc(tok_act, 1)
            act.wait_ge(tok_act, 1)
            act.activation(tok_rs[:, 2:3], tok_rs[:, 1:2], ACT.Exp, scale=-0.5).then_inc(tok_act, 1)

            def front(b, i):
                act.preload_act_table_set(LN_EXP)
                wait(act, f_read, b, F_MEAN + 1)
                act.activation(f_square, f_centered[:, :], ACT.Square).then_inc(f_squared.sem, 1)
                wait(act, f_mm, b, F_VAR + 1)
                act.activation(f_rs, f_bank[:, 0:T], ACT.Ln, scale=1.0 + EPS, bias=eps_col[:, 1:2])\
                   .then_inc(f_read.sem, 1)
                wait(act, f_read, b, F_VAR + 1)
                act.activation(f_rs, f_rs, ACT.Exp, scale=-0.5).then_inc(f_rs_ready.sem, 1)
                for half in range(HALVES):
                    wait(act, f_mm, b, F_XI + half + 1)
                    act.activation(xc[i][:, half, :], f_bank[:, 0:T], ACT.Silu, bias=vec(CONV_B + half))\
                       .then_inc(f_read.sem, 1)
                for half in range(HALVES):
                    wait(act, f_mm, b, F_Z + half + 1)
                    act.activation(zs[i][:, half, :], f_bank[:, 0:T], ACT.Silu).then_inc(f_read.sem, 1)
                wait(act, f_mm, b, F_BC + 1)
                act.activation(bc_parts[i][:, :], f_bank[0:96, 0:T], ACT.Copy).then_inc(bc_hi.sem, 1)
                wait(act, f_read, b, F_BC + 1)
                act.activation(bc_parts[i][32:64, :], bc_rest[32:64, :], ACT.Copy)
                act.activation(bc_mid[64:96, :], bc_rest[64:96, :], ACT.Copy).then_inc(bc_mids.sem, 1)
                wait(act, f_mm, b, F_DT_LOW + 1)
                act.activation(dt_low[:, :], f_bank[0:RANK, 0:T], ACT.Copy).then_inc(f_read.sem, 1)
                for half in range(HALVES):
                    wait(act, f_mm, b, F_DT + half + 1)
                    act.activation(dt_soft[:, half, :], f_bank[:, 0:T], ACT.Abs, bias=vec(B_DT + half))\
                       .then_inc(dt_abs_ready.sem, 1)
                act.preload_act_table_set(LN_EXP)
                wait(act, dt_abs_ready, b, 2)
                act.activation(dt_soft[:, :, :], dt_soft[:, :, :], ACT.Exp, scale=-1.0).then_inc(dt_exp_ready.sem, 1)
                wait(act, dt_exp_ready, b, 1)
                act.activation(dt_soft[:, :, :], dt_soft[:, :, :], ACT.Ln, bias=eps_col[:, 2:3])\
                   .then_inc(dt_ln_ready.sem, 1)

            def scan(b, i):
                wait(act, dt_ready, b, 1)
                for g in range(NG):
                    half = g // GROUPS
                    wait(act, state_ready, b, g - 1)
                    for k in range(GROUP):
                        at = half * STATES + g % GROUPS * GROUP + k
                        ins = act.activation(by_state(decay[g % 2])[:, k, 1:T], dt[i][:, half, 1:T], ACT.Exp,
                                             scale=neg_a[:, at:at + 1])
                    ins.then_inc(decay_ready.sem, 1)

            def norm(b, k, p_mean):
                wait_p_read(act, b, p_mean)
                act.activation(square[:, :], centered[:, :], ACT.Square).then_inc(squared.sem, 1)
                wait(act, p_mm, b, p_mean + 2)
                then_p_read(act.activation(rs[:, :], p_tile(p_mean + 1)[:, 0:T], ACT.Ln, bias=eps_col[:, 0:1]),
                            p_mean + 1)
                wait_p_read(act, b, p_mean + 1)
                act.activation(rs[:, :], rs[:, :], ACT.Exp, scale=-0.5).then_inc(rs_ready.sem, 1)

            def post(b, i):
                norm(b, 0, P_MEAN2)
                wait(act, gate_step, b, 2)
                act.activation(gate_tmp[:, 1:2], gate_tmp[:, 0:1], ACT.Exp).then_inc(gate_exp_ready.sem, 1)
                for j in range(2):
                    wait(act, expert_loaded[j], b, 16)
                    for m in range(H0T):
                        wait(act, p_mm, b, P_UP0[j] + m + 1)
                        if j and m == 0:
                            wait(act, p_mm, b, P_DOWN0[0] + 1)
                        then_p_read(act.activation(hid0[:, m, :], p_tile(P_UP0[j] + m)[:, 0:T], ACT.Gelu,
                                                   bias=expert[j][:, B1_AT + m:B1_AT + m + 1]), P_UP0[j] + m)
                act.preload_act_table_set(LN_EXP)
                norm(b, 1, P_MEAN3)
                wait(act, p_mm, b, P_Q + 1)
                then_p_read(act.activation(q_t[:, :], p_tile(P_Q)[:, 0:TP], ACT.Copy), P_Q)
                wait(act, p_mm, b, P_K + 1)
                then_p_read(act.activation(k_t[:, :], p_tile(P_K)[:, 0:T], ACT.Identity, accum_out=k_sum[:, :]), P_K)
                for s in range(3):
                    wait(act, bias_ready, b, s + 1)
                    then_p_read(act.activation(probs[:, s, :], p_tile(P_SCORE + s)[:, 0:T], ACT.Exp,
                                               scale=SCORE_SCALE, bias=s_bias[:, s:s + 1],
                                               accum_out=s_sum[:, s:s + 1]), P_SCORE + s)
                for s, (t0, n) in enumerate(TILES):
                    wait(act, p_mm, b, P_PROBS + s + 1)
                    then_p_read(act.activation(probs_t[0:n, s, :], p_tile(P_PROBS + s)[0:n, 0:TP], ACT.Copy),
                                P_PROBS + s)
                norm(b, 2, P_MEAN4)
                wait_p_read(act, b, P_ROUTER)
                act.activation(r_exp[:, :, :], r_cent[:, :, :], ACT.Exp).then_inc(router_exp_ready.sem, 1)
                wait(act, gates_kept, b - 1, 16)
                wait(act, p_mm, b, P_GATES + 1)
                then_p_read(act.activation(gates_t[:, :], p_tile(P_GATES)[0:E, 0:T], ACT.Copy), P_GATES)

            def batch(b, i):
                front(b, i)
                scan(b, i)
                post(b, i)

            per_batch(act, batch)

            act.wait_ge(mask_loaded, 48)
            act.activation(gates_parts, gates_e, ACT.Copy).then_inc(gates_hi, 1)
            act.wait_ge(gates_left, 1)
            act.activation(gates_parts[32:64, :], gates_rest[32:64, :], ACT.Copy)
            act.activation(gates_mid[64:96, :], gates_rest[64:96, :], ACT.Copy).then_inc(gates_mids, 1)

            def last_layer(b, i):
                for e in range(E):
                    wait(act, up_mm, b, e + 1)
                    wait(act, hid1_gated, b, e - 1)
                    for f in range(2):
                        k = MOE1_B1 + 2 * e + f
                        ins = act.activation(hid1[e % 2][:, f, :], c_rows[:, 2 * (e % 2) + f, 0:T], ACT.Gelu,
                                             bias=vec(k))
                    ins.then_inc(hid1_ready.sem, 1)

            per_batch(act, last_layer)

        @block.vector
        def _(dve):
            dve.memset(ssm_in[:, 0:CONV - 1], 0.0)
            dve.memset(eps_col[:, 0:1], EPS)
            dve.memset(eps_col[:, 1:2], EPS * EPS)
            dve.memset(eps_col[:, 2:3], 1.0)
            dve.memset(w_bc[:, :, :], 0.0).then_inc(weights_made, 1)
            dve.memset(xn3[:, T:TP], 0.0)
            dve.memset(xn4[:, T:TP], 0.0)
            dve.memset(keep_row[:, :], 1.0)
            dve.memset(ones_row[:, :], 1.0).then_inc(pads_ready, 1)
            for s in (state_ready, read_ready, y_read, hid1_gated, out_ready):
                grant(dve, s)

            dve.wait_ge(ssm_loaded, 80)
            dve.tensor_tensor(w_conv[:, :, :], conv_rows,
                              w_in_sb[:, 0:256].unsqueeze(1).to_broadcast([P, CONV, 256]), ALU.mult)\
               .then_inc(weights_made, 1)
            dve.wait_ge(weights_made, 2)
            for k in range(3):
                dve.tensor_copy(w_bc[:, :, 32 * k:32 * k + STATES], w_x_sb[:, :, RANK + STATES:])
            dve.tensor_copy(w_bc[:, :, STATES:2 * STATES], w_x_sb[:, :, RANK:RANK + STATES]).then_inc(weights_made, 1)
            for i in range(2):
                ins = dve.memset(by_state(decay[i])[:, :, 0:1], 0.0)
            ins.then_inc(weights_made, 1)
            dve.wait_ge(weights_made, 4)
            dve.wait_ge(a_exp, 1)
            dve.tensor_scalar(neg_a[:, :], neg_a[:, :], -1.0, None, ALU.mult).then_inc(a_ready, 1)

            for b in range(B):
                dve.wait_ge(tok_relu, b + 1)
                dve.bn_stats(bn_parts[:, b, :], tok_y[:, b * T:(b + 1) * T]).then_inc(bn_part, 1)
            dve.wait_ge(bn_part, B)
            dve.bn_aggr(bn[:, :], bn_parts[:, :, :]).then_inc(tok_step, 1)
            dve.wait_ge(tok_step, 1)
            dve.tensor_scalar(tok_rs[:, 0:1], bn[:, 1:2], EPS, None, ALU.add).then_inc(tok_step, 1)
            dve.wait_ge(tok_act, 2)
            dve.tensor_tensor(tok_rs[:, 3:4], tok_rs[:, 2:3], vec(GAMMA), ALU.mult).then_inc(tok_step, 1)
            dve.wait_ge(tok_step, 3)
            dve.tensor_tensor(tok_rs[:, 4:5], tok_rs[:, 3:4], bn[:, 0:1], ALU.mult).then_inc(tok_step, 1)
            dve.wait_ge(tok_step, 4)
            dve.tensor_tensor(tok_rs[:, 5:6], vec(BETA), tok_rs[:, 4:5], ALU.subtract).then_inc(tok_step, 1)
            dve.wait_ge(tok_step, 5)

            def front(b, i):
                dve.tensor_scalar(h0[i][:, :], cols(tok_y, b), tok_rs[:, 3:4], tok_rs[:, 5:6], ALU.mult, ALU.add)\
                   .then_inc(h0_ready.sem, 1)
                wait(dve, f_mm, b, F_MEAN + 1)
                wait(dve, h0_ready, b, 1)
                dve.tensor_tensor(f_centered[:, :], h0[i][:, :], f_bank[:, 0:T], ALU.subtract)\
                   .then_inc(f_read.sem, 1)
                wait(dve, f_rs_ready, b, 1)
                dve.scalar_tensor_tensor(f_centered[:, :], f_centered[:, :], vec(LN_G), f_rs,
                                         ALU.mult, ALU.mult).then_inc(f_scaled.sem, 1)
                wait(dve, f_scaled, b, 1)
                dve.tensor_scalar(ssm_in[:, CONV - 1:], f_centered[:, :], vec(LN_B), None, ALU.add)\
                   .then_inc(ssm_in_ready.sem, 1)
                wait(dve, bc_hi, b, 1)
                dve.tensor_copy(bc_f32[:, :], f_bank[0:32, 0:T]).then_inc(bc_copied.sem, 1)
                dve.tensor_tensor(bc_rest[:, :], f_bank[0:96, 0:T], bc_parts[i][:, :], ALU.subtract)\
                   .then_inc(f_read.sem, 1)
                wait(dve, bc_mids, b, 1)
                dve.tensor_tensor(bc_parts[i][64:96, :], bc_rest[64:96, :], bc_mid[64:96, :], ALU.subtract)\
                   .then_inc(bc_ready.sem, 1)
                for half in range(HALVES):
                    wait(dve, dt_abs_ready, b, half + 1)
                    dve.tensor_scalar(dt[i][:, half, :], f_bank[:, 0:T], vec(B_DT + half), 0.0, ALU.add, ALU.max)\
                       .then_inc(f_read.sem, 1)
                wait(dve, f_read, b, F_DT + 2)
                wait(dve, dt_ln_ready, b, 1)
                dve.tensor_tensor(dt[i][:, :, :], dt[i][:, :, :], dt_soft[:, :, :], ALU.add)\
                   .then_inc(dt_ready.sem, 1)

            def scan(b, i):
                def times_c(g):
                    for k in range(2):
                        wait(dve, c_ready, b, 2 * g + k + 1)
                        wait(dve, state_ready, b, g + 1)
                        wait(dve, read_summed, b, g - 1)
                        dve.tensor_tensor(by_state(read[g % 2])[:, 2 * k:2 * k + 2, :],
                                          by_state(state[g % 2])[:, 2 * k:2 * k + 2, :],
                                          c_rows[:, 2 * k:2 * k + 2, 0:T], ALU.mult).then_inc(read_ready.sem, 1)

                def gate(half):
                    wait(dve, y_mm, b, half + 1)
                    dve.scalar_tensor_tensor(y_gated[:, half, :], xc[i][:, half, :], vec(D_SKIP + half),
                                             y_bank[:, 0:T], ALU.mult, ALU.add).then_inc(y_read.sem, 1)
                    wait(dve, y_read, b, half + 1)
                    dve.tensor_tensor(y_gated[:, half, :], y_gated[:, half, :], zs[i][:, half, :], ALU.mult)\
                       .then_inc(y_gated_ready.sem, 1)

                for g in range(NG):
                    wait(dve, decay_ready, b, g + 1)
                    wait(dve, drive_ready, b, g + 1)
                    wait(dve, read_ready, b, 2 * (g - 1))
                    dve.tensor_tensor_scan(state[g % 2], decay[g % 2], drive[g % 2], 0.0, ALU.mult, ALU.add)\
                       .then_inc(state_ready.sem, 1)
                    if g:
                        times_c(g - 1)
                    if g == GROUPS + 1:
                        gate(0)
                times_c(NG - 1)
                gate(1)
                wait(dve, y_mm, b, 3)
                dve.tensor_tensor(h1[i][:, :], h0[i][:, :], y_bank[:, 0:T], ALU.add).then_inc(y_read.sem, 1)

            def center(b, h, p_mean):
                wait(dve, p_mm, b, p_mean + 1)
                then_p_read(dve.tensor_tensor(centered[:, :], h, p_tile(p_mean)[:, 0:T], ALU.subtract), p_mean)

            def post(b, i):
                wait(dve, y_read, b, 3)
                center(b, h1[i][:, :], P_MEAN2)
                wait(dve, rs_ready, b, 1)
                dve.scalar_tensor_tensor(xn2, centered[:, :], 1.0, rs[:, :], ALU.mult, ALU.mult,
                                         accum_out=pooled[:, :]).then_inc(xn2_ready.sem, 1)
                wait(dve, p_mm, b, P_GATE + 1)
                then_p_read(dve.scalar_tensor_tensor(gate_row[:, :], p_tile(P_GATE)[0:1, 0:E], 1.0 / T,
                                                     gate_b_sb[:, :], ALU.mult, ALU.add), P_GATE)
                wait_p_read(dve, b, P_GATE)
                dve.memset(spare[:, :], 0.0)
                dve.max(top_v[:, :], gate_row[:, :]).then_inc(gate_step.sem, 1)
                wait(dve, gate_step, b, 1)
                dve.memset(spare[:, :], 0.0)
                dve.max_index(top_i[:, :], top_v[:, :], gate_row[:, :]).then_inc(experts_known, 1)
                dve.tensor_tensor(gate_tmp[:, 0:1], top_v[:, 1:2], top_v[:, 0:1], ALU.subtract)\
                   .then_inc(gate_step.sem, 1)
                wait(dve, gate_exp_ready, b, 1)
                dve.tensor_scalar(gate_tmp[:, 2:3], gate_tmp[:, 1:2], 1.0, None, ALU.add).then_inc(gate_step.sem, 1)
                wait(dve, gate_step, b, 3)
                dve.reciprocal(w_pair[:, 0:1], gate_tmp[:, 2:3]).then_inc(gate_step.sem, 1)
                wait(dve, gate_step, b, 4)
                dve.tensor_tensor(w_pair[:, 1:2], gate_tmp[:, 1:2], w_pair[:, 0:1], ALU.mult)\
                   .then_inc(gate_step.sem, 1)
                wait(dve, p_mm, b, P_WCOL + 1)
                then_p_read(dve.tensor_copy(w_col[:, :], p_tile(P_WCOL)[:, 0:2]), P_WCOL)
                wait_p_read(dve, b, P_WCOL)
                for j in range(2):
                    wait(dve, expert_loaded[j], b, 16)
                dve.tensor_tensor(b2_mix[:, 0:1], expert[1][:, B2_AT:B2_AT + 1], w_col[:, 1:2], ALU.mult)\
                   .then_inc(b2_step.sem, 1)
                wait(dve, b2_step, b, 1)
                dve.scalar_tensor_tensor(b2_mix[:, 1:2], expert[0][:, B2_AT:B2_AT + 1], w_col[:, 0:1],
                                         b2_mix[:, 0:1], ALU.mult, ALU.add).then_inc(b2_step.sem, 1)
                wait(dve, b2_step, b, 2)
                dve.tensor_scalar(h2[:, :], h1[i][:, :], b2_mix[:, 1:2], None, ALU.add)\
                   .then_inc(b2_step.sem, 1)
                wait(dve, b2_step, b, 3)
                wait(dve, p_mm, b, P_DOWN0[0] + 1)
                then_p_read(dve.scalar_tensor_tensor(h2[:, :], p_tile(P_DOWN0[0])[:, 0:T], w_col[:, 0:1],
                                                     h2[:, :], ALU.mult, ALU.add), P_DOWN0[0])
                wait(dve, p_mm, b, P_DOWN0[1] + 1)
                wait_p_read(dve, b, P_DOWN0[0])
                then_p_read(dve.scalar_tensor_tensor(h2[:, :], p_tile(P_DOWN0[1])[:, 0:T], w_col[:, 1:2],
                                                     h2[:, :], ALU.mult, ALU.add), P_DOWN0[1])
                wait_p_read(dve, b, P_DOWN0[1])
                center(b, h2[:, :], P_MEAN3)
                wait(dve, rs_ready, b, 2)
                dve.tensor_tensor(xn3[:, 0:T], centered[:, :], rs[:, :], ALU.mult).then_inc(xn3_ready.sem, 1)
                wait(dve, p_mm, b, P_V + 1)
                then_p_read(dve.tensor_copy(v_sb[:, :, :], p_tile(P_V)[:, 0:TP].rearrange("p (s o) -> p s o", s=3)),
                            P_V)
                wait(dve, p_mm, b, P_LOW + 1)
                then_p_read(dve.tensor_scalar(low_row, p_tile(P_LOW)[0:1, 0:T], -1.0, None, ALU.mult), P_LOW)
                if i == 0:
                    with dve.If_eq(dve.to_reg(b), 0):
                        wait_p_read(dve, b, P_LOW)
                        dve.memset(spare[:, :], 0.0)
                        dve.max(low_v[:, :], low_row).then_inc(low_step, 1)
                        dve.wait_ge(low_step, 1)
                        dve.max_index(low_i[:, :], low_v[:, :], low_row).then_inc(low_step, 1)
                        dve.wait_ge(low_step, 2)
                        dve.tensor_copy(low_f[:, :], low_i[:, 0:1]).then_inc(low_step, 1)
                        dve.wait_ge(low_step, 3)
                        dve.wait_ge(index_step, 1)
                        dve.tensor_scalar(keep_row[:, 0:T], token_index[:, :], low_f[:, :], None, ALU.not_equal)\
                           .then_inc(low_step, 1)
                wait(dve, p_mm, b, P_KEEP + 1)
                then_p_read(dve.tensor_copy(keep[:, :], p_tile(P_KEEP)[:, 0:3]), P_KEEP)
                for s in range(3):
                    wait(dve, p_mm, b, P_SCORE + s + 1)
                    dve.reduce_max(s_max[:, s:s + 1], p_tile(P_SCORE + s)[:, 0:T], AX_X).then_inc(max_ready.sem, 1)
                    wait(dve, max_ready, b, s + 1)
                    dve.tensor_scalar(s_bias[:, s:s + 1], s_max[:, s:s + 1], -SCORE_SCALE, None, ALU.mult)\
                       .then_inc(bias_ready.sem, 1)
                for s in range(3):
                    wait_p_read(dve, b, P_SCORE + s)
                dve.reciprocal(s_inv[:, :], s_sum[:, :]).then_inc(scale_step.sem, 1)
                wait(dve, scale_step, b, 1)
                wait_p_read(dve, b, P_KEEP)
                dve.tensor_tensor(s_scale[:, :], s_inv[:, :], keep[:, :], ALU.mult).then_inc(scale_step.sem, 1)
                wait(dve, scale_step, b, 2)
                for s in range(3):
                    dve.tensor_scalar(probs[:, s, :], probs[:, s, :], s_scale[:, s:s + 1], None, ALU.mult)\
                       .then_inc(probs_scaled.sem, 1)
                wait(dve, p_mm, b, P_ATTN + 1)
                then_p_read(dve.tensor_tensor(cols(h3_all, b), h2[:, :], p_tile(P_ATTN)[:, 0:T], ALU.add), P_ATTN)
                wait_p_read(dve, b, P_ATTN)
                center(b, cols(h3_all, b), P_MEAN4)
                wait(dve, rs_ready, b, 3)
                wait(dve, xn4_kept, b - 1, 16)
                dve.tensor_tensor(xn4[:, 0:T], centered[:, :], rs[:, :], ALU.mult).then_inc(xn4_ready.sem, 1)
                logits = p_tile(P_ROUTER)[:, 0:3 * E].rearrange("p (s e) -> p s e", s=3)
                wait(dve, p_mm, b, P_ROUTER + 1)
                dve.reduce_max(r_max[:, :], logits, AX_X).then_inc(router_step.sem, 1)
                wait(dve, router_step, b, 1)
                then_p_read(dve.tensor_tensor(r_cent[:, :, :], logits,
                                              r_max[:, :].unsqueeze(2).to_broadcast([P, 3, E]), ALU.subtract),
                            P_ROUTER)
                wait(dve, router_exp_ready, b, 1)
                dve.reduce_sum(r_sum[:, :], r_exp[:, :, :], AX_X).then_inc(router_step.sem, 1)
                wait(dve, router_step, b, 2)
                dve.reciprocal(r_inv[:, :], r_sum[:, :]).then_inc(router_step.sem, 1)
                wait(dve, router_step, b, 3)
                dve.tensor_tensor(r_prob[:, :, :], r_exp[:, :, :],
                                  r_inv[:, :].unsqueeze(2).to_broadcast([P, 3, E]), ALU.mult)\
                   .then_inc(router_step.sem, 1)

            def batch(b, i):
                front(b, i)
                scan(b, i)
                post(b, i)

            per_batch(dve, batch)

            dve.wait_ge(gates_loaded, 16)
            now = top_in
            for r in range(TOP_ROUNDS):
                dve.max(top_8[:, :], now).then_inc(top_step, 1)
                dve.wait_ge(top_step, 2 * r + 1)
                if r == TOP_ROUNDS - 1 and TOP_TOKENS % 8:
                    dve.memset(top_8[:, TOP_TOKENS % 8:], -1.0).then_inc(top_step, 1)
                    dve.wait_ge(top_step, 2 * r + 2)
                then = top_work[r % 2]
                dve.match_replace(then, top_8[:, :], now, -1.0).then_inc(top_step, 1)
                now = then
                last = 2 * r + 2 + (1 if r == TOP_ROUNDS - 1 and TOP_TOKENS % 8 else 0)
                dve.wait_ge(top_step, last)
            dve.scalar_tensor_tensor(gates_masked, now, 0.0, top_in, ALU.is_lt, ALU.mult).then_inc(top_step, 1)
            dve.wait_ge(gates_hi, 1)
            dve.tensor_tensor(gates_rest, gates_e, gates_parts, ALU.subtract).then_inc(gates_left, 1)
            dve.wait_ge(gates_mids, 1)
            dve.tensor_tensor(gates_parts[64:96, :], gates_rest[64:96, :], gates_mid[64:96, :], ALU.subtract)\
               .then_inc(gates_split, 1)

            def last_layer(b, i):
                for e in range(E):
                    wait(dve, hid1_ready, b, e + 1)
                    wait(dve, gate_rows_mm, b, e + 1)
                    wait(dve, down_mm, b, e - 1)
                    gate_rows = (y_bank, f_bank)[e % 2][:, 0:T]
                    dve.tensor_tensor(hid1_g[e % 2], hid1[e % 2],
                                      gate_rows.unsqueeze(1).to_broadcast([P, 2, T]), ALU.mult)\
                       .then_inc(hid1_gated.sem, 1)
                wait(dve, down_mm, b, E)
                wait(dve, out_stored, b - 1, 16)
                dve.tensor_tensor(out_sb[i], cols(h3_all, b), p_bank[:, i, 0:T], ALU.add).then_inc(out_ready.sem, 1)

            per_batch(dve, last_layer)

        @block.tensor
        def _(pe):
            mm = nc.tensor.matmul
            for s in (read_summed, down_mm, f_read, *p_read):
                grant(pe, s)
            pe.wait_ge(x_loaded, 32)
            pe.wait_ge(tokw_loaded, 16)
            for b in range(B):
                if b >= 4:
                    pe.wait_ge(tok_relu, b - 3)
                y = c_rows[:, b % 4, 0:T]
                mm(y, tok_w_sb[:, 0, :], x2[:, b, 0:T], start=True, stop=False)
                mm(y, tok_w_sb[:, 1, :], x2[:, b, 2:2 + T], start=False, stop=False)
                mm(y, tok_w_sb[0:64, 2, :], x2[0:64, b, 4:4 + T], start=False, stop=True).then_inc(tok_mm, 1)
            pe.wait_ge(tok_relu, B)
            pe.wait_ge(ident_step, 3)
            pe.wait_ge(pick_step, 4)
            pe.wait_ge(weights_made, 3)
            pe.wait_ge(gate_loaded, 64)
            pe.wait_ge(pads_ready, 1)

            def front(b, i):
                f = f_bank[:, 0:T]

                def tile(n, *waits):
                    for s, k in waits:
                        wait(pe, s, b, k)
                    wait(pe, f_read, b, n)

                tile(F_MEAN, (h0_ready, 1))
                mm(f, mean_mat[:, :], h0[i][:, :], start=True, stop=True).then_inc(f_mm.sem, 1)
                tile(F_VAR, (f_squared, 1))
                mm(f, mean_mat[:, :], f_square, start=True, stop=True).then_inc(f_mm.sem, 1)
                for half in range(HALVES):
                    tile(F_XI + half, (ssm_in_ready, 1))
                    for j in range(CONV):
                        ins = mm(f, w_conv[:, j, P * half:P * (half + 1)], ssm_in[:, j:j + T],
                                 start=(j == 0), stop=(j == CONV - 1))
                    ins.then_inc(f_mm.sem, 1)
                for half in range(HALVES):
                    tile(F_Z + half)
                    mm(f, w_in_sb[:, 256 + P * half:256 + P * (half + 1)], ssm_in[:, CONV - 1:],
                       start=True, stop=True).then_inc(f_mm.sem, 1)
                tile(F_BC)
                for half in range(HALVES):
                    ins = mm(f_bank[0:96, 0:T], w_bc[:, half, :], xc[i][:, half, :], start=(half == 0),
                             stop=(half == 1))
                ins.then_inc(f_mm.sem, 1)
                tile(F_DT_LOW)
                for half in range(HALVES):
                    ins = mm(f_bank[0:RANK, 0:T], w_x_sb[:, half, 0:RANK], xc[i][:, half, :], start=(half == 0),
                             stop=(half == 1))
                ins.then_inc(f_mm.sem, 1)
                for half in range(HALVES):
                    tile(F_DT + half)
                    mm(f, w_dt_sb[:, P * half:P * (half + 1)], dt_low[:, :], start=True, stop=True)\
                        .then_inc(f_mm.sem, 1)

            def scan(b, i):
                wait(pe, bc_ready, b, 1)
                for g in range(NG + 1):
                    if g < NG:
                        for k in range(2):
                            wait(pe, read_ready, b, 2 * (g - 1) + k + 1)
                            for m in range(2):
                                s = g % GROUPS * GROUP + 2 * k + m
                                ins = mm(c_rows[:, 2 * k + m, 0:T], pick[:, s:s + 1].to_broadcast([96, P]),
                                         bc_parts[i][:, :], start=True, stop=True)
                            ins.then_inc(c_ready.sem, 1)
                    if g:
                        half, first = (g - 1) // GROUPS, (g - 1) % GROUPS == 0
                        if first:
                            wait(pe, y_read, b, half)
                        for k in range(GROUP):
                            if k % 2 == 0:
                                wait(pe, read_ready, b, 2 * (g - 1) + k // 2 + 1)
                            end = g % GROUPS == 0 and k == GROUP - 1
                            ins = mm(y_bank[:, 0:T], ident[:, :], by_state(read[(g - 1) % 2])[:, k, :],
                                     start=(first and k == 0), stop=end)
                        ins.then_inc(read_summed.sem, 1)
                        if g % GROUPS == 0:
                            pe.wait_ge(read_summed.sem, read_summed.at(b, g))
                            pe.sem_inc(y_mm.sem, 1)
                wait(pe, y_read, b, 2)
                for half in range(HALVES):
                    wait(pe, y_gated_ready, b, half + 1)
                    ins = mm(y_bank[:, 0:T], w_out_sb[:, half, :], y_gated[:, half, :], start=(half == 0),
                             stop=(half == 1))
                ins.then_inc(y_mm.sem, 1)

            def post(b, i):
                def tile(n, *waits):
                    for s, k in waits:
                        wait(pe, s, b, k)
                    wait(pe, p_read[n % 2], b, n // 2)
                    return p_tile(n)

                def norm(k, p_mean, h):
                    mm(tile(p_mean)[:, 0:T], mean_mat[:, :], h, start=True, stop=True).then_inc(p_mm.sem, 1)
                    mm(tile(p_mean + 1, (squared, k + 1))[:, 0:T], mean_mat[:, :], square[:, :],
                       start=True, stop=True).then_inc(p_mm.sem, 1)

                wait(pe, y_read, b, 3)
                norm(0, P_MEAN2, h1[i][:, :])
                mm(tile(P_GATE, (xn2_ready, 1))[0:1, 0:E], pooled[:, :], gate_w_sb[:, :], start=True, stop=True)\
                    .then_inc(p_mm.sem, 1)
                mm(tile(P_WCOL, (gate_step, 5))[:, 0:2], ones_row[:, :], w_pair[:, :], start=True, stop=True)\
                    .then_inc(p_mm.sem, 1)
                for j in range(2):
                    w = expert[j]
                    for m in range(H0T):
                        mm(tile(P_UP0[j] + m, (expert_loaded[j], 16))[:, 0:T], w[:, W1_AT + P * m:W1_AT + P * (m + 1)],
                           xn2, start=True, stop=True).then_inc(p_mm.sem, 1)
                    down = tile(P_DOWN0[j])
                    for m in range(H0T):
                        wait_p_read(pe, b, P_UP0[j] + m)
                        ins = mm(down[:, 0:T], w[:, W2_AT + P * m:W2_AT + P * (m + 1)], hid0[:, m, :],
                                 start=(m == 0), stop=(m == H0T - 1))
                    ins.then_inc(p_mm.sem, 1)
                wait_p_read(pe, b, P_DOWN0[1])
                norm(1, P_MEAN3, h2[:, :])
                mm(tile(P_Q, (xn3_ready, 1))[:, 0:TP], qkv_sb[:, 0, :], xn3[:, :], start=True, stop=True)\
                    .then_inc(p_mm.sem, 1)
                mm(tile(P_K)[:, 0:T], qkv_sb[:, 1, :], xn3[:, 0:T], start=True, stop=True).then_inc(p_mm.sem, 1)
                v = tile(P_V)
                for s in range(3):
                    ins = mm(v[:, P * s:P * (s + 1)], xn3[:, P * s:P * (s + 1)], qkv_sb[:, 2, :],
                             start=True, stop=True)
                ins.then_inc(p_mm.sem, 1)
                wait_p_read(pe, b, P_K)
                mm(tile(P_LOW)[0:1, 0:T], k_sum[:, :], q_t[:, 0:T], start=True, stop=True).then_inc(p_mm.sem, 1)
                pe.wait_ge(low_step, 4)
                kept = tile(P_KEEP)
                for s in range(3):
                    ins = mm(kept[:, s:s + 1], keep_row[0:1, P * s:P * (s + 1)], ones_row[0:1, 0:1],
                             start=True, stop=True)
                ins.then_inc(p_mm.sem, 1)
                for s in range(3):
                    mm(tile(P_SCORE + s)[:, 0:T], q_t[:, P * s:P * (s + 1)], k_t[:, :], start=True, stop=True)\
                        .then_inc(p_mm.sem, 1)
                wait(pe, probs_scaled, b, 3)
                for s, (t0, n) in enumerate(TILES):
                    turned = tile(P_PROBS + s)
                    for q in range(3):
                        ins = pe.transpose(turned[0:n, P * q:P * (q + 1)], probs[:, q, t0:t0 + n], ident[:, :])
                    ins.then_inc(p_mm.sem, 1)
                attn = tile(P_ATTN)
                for s, (t0, n) in enumerate(TILES):
                    wait_p_read(pe, b, P_PROBS + s)
                    ins = mm(attn[:, 0:T], v_sb[0:n, s, :], probs_t[0:n, s, 0:T], start=(s == 0), stop=(s == 2))
                ins.then_inc(p_mm.sem, 1)
                wait_p_read(pe, b, P_ATTN)
                norm(2, P_MEAN4, cols(h3_all, b))
                router = tile(P_ROUTER, (xn4_ready, 1))
                for s in range(3):
                    ins = mm(router[:, E * s:E * (s + 1)], xn4[:, P * s:P * (s + 1)], router_sb[:, :],
                             start=True, stop=True)
                ins.then_inc(p_mm.sem, 1)
                gates = tile(P_GATES, (router_step, 4))
                for s in range(3):
                    ins = pe.transpose(gates[0:E, P * s:P * (s + 1)], r_prob[:, s, :], ident[:, :])
                ins.then_inc(p_mm.sem, 1)

            def batch(b, i):
                front(b, i)
                scan(b, i)
                post(b, i)

            per_batch(pe, batch)

            wait(pe, p_read[1], B - 1, NPT // 2)
            wait(pe, xn4_kept, B - 1, 16)
            pe.wait_ge(moe1_loaded, 48)
            pe.wait_ge(gates_split, 1)

            def last_layer(b, i):
                acc = p_bank[:, i, 0:T]

                def down(e):
                    wait(pe, hid1_gated, b, e + 1)
                    for f in range(2):
                        ins = mm(acc, moe1_w2_sb[:, e, f, :], hid1_g[e % 2][:, f, :], start=False,
                                 stop=(e == E - 1 and f == 1))
                    ins.then_inc(down_mm.sem, 1)

                for e in range(E):
                    wait(pe, hid1_ready, b, e - 1)
                    for f in range(2):
                        ins = mm(c_rows[:, 2 * (e % 2) + f, 0:T], moe1_w1_sb[:, e, P * f:P * (f + 1)],
                                 cols(xn4_all, b), start=True, stop=True)
                    ins.then_inc(up_mm.sem, 1)
                    wait(pe, hid1_gated, b, e - 1)
                    mm((y_bank, f_bank)[e % 2][:, 0:T], pick[:, e:e + 1].to_broadcast([96, P]),
                       cols(gates_parts, b), start=True, stop=True).then_inc(gate_rows_mm.sem, 1)
                    if e == 0:
                        wait(pe, out_ready, b - 2, 1)
                        mm(acc, moe1_b2_sb[:, :], cols(gates_e[0:E, :], b), start=True, stop=False)
                    else:
                        down(e - 1)
                down(E - 1)

            per_batch(pe, last_layer)


def kernel(**inputs):
    import numpy as np
    import concourse.bacc as bacc
    from concourse.bass_utils import run_bass_kernel_spmd

    a = {name: np.asarray(v) for name, v in inputs.items()}
    batches, t_in, d_in = a["x"].shape
    tok_w = a["L0_tok_W"].T
    tok_tiles = np.zeros((P, 3, P), np.float32)
    tok_tiles[:, 0], tok_tiles[:, 1], tok_tiles[0:64, 2] = tok_w[0:128], tok_w[128:256], tok_w[256:320]

    def halves(v):
        return v.reshape(2, P, -1).transpose(1, 0, 2).reshape(P, -1)

    vectors = np.concatenate([
        a["L0_tok_b"][:, None], a["L0_tok_gamma"][:, None], a["L0_tok_beta"][:, None],
        a["L0_attn_ln_g"][:, None], a["L0_attn_ln_b"][:, None], halves(a["L0_attn_conv_b"]),
        halves(a["L0_attn_b_dt"]), halves(a["L0_attn_D"]), halves(a["L0_attn_A_log"]),
        a["L1_ffn_b1"].reshape(16, P).T,
    ], axis=1)
    moe0 = np.concatenate([
        a["L0_ffn_w1"],
        a["L0_ffn_w2"].reshape(8, 4, P, P).transpose(0, 2, 1, 3).reshape(8, P, 512),
        a["L0_ffn_b1"].reshape(8, 4, P).transpose(0, 2, 1), a["L0_ffn_b2"][:, :, None],
    ], axis=2)
    arrays = {
        "x_t": a["x"].transpose(2, 0, 1),
        "tok_w": tok_tiles,
        "vec_in": vectors,
        "conv_w": a["L0_attn_conv_w"][:, 0, :].T,
        "w_in": a["L0_attn_W_in"].T,
        "w_x": halves(a["L0_attn_W_x"].T).reshape(P, 2, -1),
        "w_dt": a["L0_attn_W_dt"].T,
        "w_out": halves(a["L0_attn_W_out"].T).reshape(P, 2, -1),
        "gate_w": a["L0_ffn_gate_w"],
        "gate_b": a["L0_ffn_gate_b"][None],
        "moe0": moe0,
        "qkv_w": a["L1_attn_kernel"].transpose(1, 0, 2),
        "router_w": a["L1_ffn_Wg"],
        "moe1_w1": a["L1_ffn_W1"].transpose(1, 0, 2),
        "moe1_w2": a["L1_ffn_W2"].reshape(8, 2, P, P).transpose(2, 0, 1, 3),
        "moe1_b2": a["L1_ffn_b2"],
    }
    arrays = {name: np.ascontiguousarray(v) for name, v in arrays.items()}
    t = t_in - 4
    nc = bacc.Bacc("TRN2", target_bir_lowering=False, num_devices=1)
    aps = {n: nc.dram_tensor(n, v.shape, F32, kind="ExternalInput").ap() for n, v in arrays.items()}
    aps["out"] = nc.dram_tensor("out", (P, batches * t), F32, kind="ExternalOutput").ap()
    aps["gates_dram"] = nc.dram_tensor("gates_dram", (batches, 8, t), F32).ap()
    aps["mask_dram"] = nc.dram_tensor("mask_dram", (batches, 8, t), F32).ap()
    aps["b_dram"] = nc.dram_tensor("b_dram", (2, 16, t), F32).ap()
    audio_tower(nc, **aps)
    got = run_bass_kernel_spmd(nc, [arrays], core_ids=[0]).results[0]["out"]
    return np.ascontiguousarray(got.reshape(P, batches, t).transpose(1, 2, 0))
```

```python
from contextlib import ExitStack

import concourse.bass as bass
from concourse import mybir

F32 = mybir.dt.float32
BF16 = mybir.dt.bfloat16
U32 = mybir.dt.uint32
I32 = mybir.dt.int32
ALU = mybir.AluOpType
ACT = mybir.ActivationFunctionType
AX_X = mybir.AxisListType.X
LN_EXP = "natural_log_exp_and_others"

P = 128
BANK = 512
EPS = 1e-5

TOK_B, GAMMA, BETA, LN_G, LN_B, CONV_B, B_DT, D_SKIP, A_LOG, MOE1_B1, N_VEC = 0, 1, 2, 3, 4, 5, 7, 9, 11, 43, 59


class Signal:

    def __init__(self, sem, per_batch, head):
        self.sem, self.per_batch, self.head = sem, per_batch, head

    def at(self, b, n):
        return b * self.per_batch + (n + self.head)


def audio_tower(nc, x_t, tok_w, vec_in, conv_w, w_in, w_x, w_dt, w_out, gate_w, gate_b, moe0, qkv_w,
                router_w, moe1_w1, moe1_w2, moe1_b2, out, gates_dram, mask_dram, b_dram):
    B, T_IN = x_t.shape[1:]
    TAPS = 5
    T = T_IN - TAPS + 1
    TP = 3 * P
    TILES = [(0, P), (P, P), (2 * P, T - 2 * P)]
    HALVES = 2
    STATES = 16
    GROUP = 4
    GROUPS = STATES // GROUP
    RANK = 8
    CONV = 4
    E = 8
    H0T = 4
    TOP_TOKENS = max(T * 2 // E, 1)
    TOP_ROUNDS = -(-TOP_TOKENS // 8)
    SCORE_SCALE = 1.0 / 8.0
    BT = B * T
    W1_AT, W2_AT, B1_AT, B2_AT, PACK = 0, 512, 1024, 1028, 1029

    with ExitStack() as ctx:
        def sb(name, shape, dt=F32):
            return ctx.enter_context(nc.sbuf_tensor(name, shape, dt))

        def sem(name):
            return ctx.enter_context(nc.semaphore(name))

        def signal(name, per_batch=1, head=0):
            return Signal(sem(name), per_batch, head)

        c_rows = ctx.enter_context(nc.psum_tensor("c_rows", [P, 4, BANK], F32))
        y_bank = ctx.enter_context(nc.psum_tensor("y_bank", [P, BANK], F32))
        f_bank = ctx.enter_context(nc.psum_tensor("f_bank", [P, BANK], F32))
        p_bank = ctx.enter_context(nc.psum_tensor("p_bank", [P, 2, BANK], F32))

        mean_mat = sb("mean_mat", [P, P])
        ident = sb("ident", [P, P])
        ones_row = sb("ones_row", [1, P])
        pick = sb("pick", [96, STATES], BF16)
        token_index = sb("token_index", [1, T])
        vecs = sb("vecs", [P, N_VEC])
        neg_a = sb("neg_a", [P, HALVES * STATES])
        eps_col = sb("eps_col", [P, 3])
        w_in_sb = sb("w_in_sb", [P, 512])
        w_conv = sb("w_conv", [P, CONV, 256])
        w_x_sb = sb("w_x_sb", [P, HALVES, RANK + 2 * STATES])
        w_bc = sb("w_bc", [P, HALVES, 96])
        w_dt_sb = sb("w_dt_sb", [RANK, 256])
        w_out_sb = sb("w_out_sb", [P, HALVES, P])
        gate_w_sb = sb("gate_w_sb", [P, E])
        gate_b_sb = sb("gate_b_sb", [1, E])
        qkv_sb = sb("qkv_sb", [P, 3, P])
        router_sb = sb("router_sb", [P, E])
        moe1_w1_sb = sb("moe1_w1_sb", [P, E, 256])
        moe1_w2_sb = sb("moe1_w2_sb", [P, E, 2, P])
        moe1_b2_sb = sb("moe1_b2_sb", [E, P])

        x_area = sb("x_area", [P, B * T_IN])
        x2 = x_area[:, :].rearrange("p (b t) -> p b t", b=B)
        xn4_all = x_area[:, 0:BT]
        tok_y = sb("tok_y", [P, BT])
        h3_all = tok_y
        bn_parts = sb("bn_parts", [P, B, 6])
        bn = sb("bn", [P, 2])
        tok_rs = sb("tok_rs", [P, 6])

        h0 = sb("h0", [P, T])
        f_centered = sb("f_centered", [P, T])
        ssm_in = sb("ssm_in", [P, CONV - 1 + T])
        xc = [sb(f"xc{i}", [P, HALVES, T]) for i in range(2)]
        zs = [sb(f"zs{i}", [P, HALVES, T]) for i in range(2)]
        bc_rest = sb("bc_rest", [96, T])
        bc_f32 = sb("bc_f32", [32, T])
        bc_mid = sb("bc_mid", [96, T], BF16)
        bc_parts = [sb(f"bc_parts{i}", [96, T], BF16) for i in range(2)]
        dt_low = sb("dt_low", [RANK, T])
        dt_soft = sb("dt_soft", [P, HALVES, T])
        f_square, f_rs = dt_soft[:, 0, :], dt_soft[:, 1, :]
        dt = [sb(f"dt{i}", [P, HALVES, T]) for i in range(2)]
        dtu = [sb(f"dtu{i}", [P, HALVES, T]) for i in range(2)]

        b_area = sb("b_area", [P, STATES * T])
        b_rows = b_area[:, :].rearrange("p (s t) -> p s t", s=STATES)
        tok_w_sb = b_area[:, 0:3 * P].rearrange("p (k o) -> p k o", k=3)
        scan_area = sb("scan_area", [P, 8, GROUP * T])
        decay, drive, state, read = ([scan_area[:, 2 * k + i, :] for i in range(2)] for k in range(4))
        y_gated = sb("y_gated", [P, HALVES, T])
        h1 = sb("h1", [P, T])
        conv_rows = scan_area[:, 0, 0:CONV * 256].rearrange("p (j d) -> p j d", j=CONV)

        def by_state(area):
            return area.rearrange("p (s t) -> p s t", s=GROUP)

        centered = sb("centered", [P, T])
        square = sb("square", [P, T])
        rs = sb("rs", [P, T])
        spare = sb("spare", [1, 1])
        pooled = sb("pooled", [P, 1])
        gate_row = sb("gate_row", [1, E])
        top_v = sb("top_v", [1, 8])
        top_i = sb("top_i", [1, 8], U32)
        gate_tmp = sb("gate_tmp", [1, 4])
        w_pair = sb("w_pair", [1, 2])
        w_col = sb("w_col", [P, 2])
        expert = [sb(f"expert{j}", [P, PACK]) for j in range(2)]
        b2_mix = sb("b2_mix", [P, 2])
        h2 = sb("h2", [P, T])
        hid0 = sb("hid0", [P, H0T, T])
        probs = hid0
        xn3 = sb("xn3", [P, TP])
        xn2 = xn3[:, 0:T]
        q_t = sb("q_t", [P, TP])
        k_t = sb("k_t", [P, T])
        k_sum = sb("k_sum", [P, 1])
        v_sb = sb("v_sb", [P, 3, P])
        low_row = square[0:1, :]
        low_v = sb("low_v", [1, 8])
        low_i = sb("low_i", [1, 8], U32)
        low_f = sb("low_f", [1, 1])
        keep_row = sb("keep_row", [1, TP])
        keep = sb("keep", [P, 3])
        s_max = sb("s_max", [P, 3])
        s_bias = sb("s_bias", [P, 3])
        s_sum = sb("s_sum", [P, 3])
        s_inv = sb("s_inv", [P, 3])
        s_scale = sb("s_scale", [P, 3])
        probs_t = sb("probs_t", [P, 3, TP])
        xn4 = sb("xn4", [P, TP])
        r_max = sb("r_max", [P, 3])
        r_cent = sb("r_cent", [P, 3, E])
        r_exp = sb("r_exp", [P, 3, E])
        r_sum = sb("r_sum", [P, 3])
        r_inv = sb("r_inv", [P, 3])
        r_prob = sb("r_prob", [P, 3, E])
        gates_t = sb("gates_t", [E, T])

        gates_e = scan_area[0:96, 0:2, :].rearrange("p a n -> p (a n)")
        gates_rest = scan_area[0:96, 2:4, :].rearrange("p a n -> p (a n)")
        gates_parts = scan_area[0:96, 4, :].bitcast(BF16)
        gates_mid = scan_area[0:96, 5, :].bitcast(BF16)
        top_in = scan_area[0:B * E, 6, 0:T]
        top_work = [scan_area[0:B * E, 6, T * (1 + i):T * (2 + i)] for i in range(2)]
        gates_masked = scan_area[0:B * E, 6, 3 * T:4 * T]
        top_8 = sb("top_8", [B * E, 8])
        hid1 = [b_area[:, 2 * T * i:2 * T * (i + 1)].rearrange("p (f t) -> p f t", f=2) for i in range(2)]
        hid1_g = [b_area[:, 2 * T * i:2 * T * (i + 1)].rearrange("p (f t) -> p f t", f=2) for i in (2, 3)]
        out_sb = [b_area[:, T * i:T * (i + 1)] for i in (8, 9)]

        x_loaded, tokw_loaded, vec_loaded, ssm_loaded, gate_loaded, moe1_loaded = (
            sem(n) for n in ("x_loaded", "tokw_loaded", "vec_loaded", "ssm_loaded", "gate_loaded", "moe1_loaded"))
        ident_step, pick_step, index_step, pads_ready, granted = (
            sem(n) for n in ("ident_step", "pick_step", "index_step", "pads_ready", "granted"))
        tok_mm, tok_relu, bn_part, tok_step, tok_act = (
            sem(n) for n in ("tok_mm", "tok_relu", "bn_part", "tok_step", "tok_act"))
        a_exp, a_ready, weights_made = sem("a_exp"), sem("a_ready"), sem("weights_made")

        F_MEAN, F_VAR, F_XI, F_Z, F_BC, F_DT_LOW, F_DT, NF = 0, 1, 2, 4, 6, 7, 8, 10
        f_mm = signal("f_mm", NF)
        f_read = signal("f_read", NF, head=1)
        h0_ready = signal("h0_ready")
        f_squared = signal("f_squared")
        f_rs_ready = signal("f_rs_ready")
        f_scaled = signal("f_scaled")
        ssm_in_ready = signal("ssm_in_ready")
        bc_hi = signal("bc_hi")
        bc_copied = signal("bc_copied")
        bc_mids = signal("bc_mids")
        bc_ready = signal("bc_ready")
        b_stored = signal("b_stored", 16)
        b_loaded = [signal(f"b_loaded{g}", 16) for g in range(GROUPS)]
        dt_abs_ready = signal("dt_abs_ready", 2)
        dt_exp_ready = signal("dt_exp_ready")
        dt_ln_ready = signal("dt_ln_ready")
        dt_ready = signal("dt_ready")
        dtu_ready = signal("dtu_ready")

        NG = HALVES * GROUPS
        decay_ready = signal("decay_ready", NG)
        drive_ready = signal("drive_ready", NG, head=4)
        state_ready = signal("state_ready", NG, head=2)
        c_ready = signal("c_ready", 2 * NG)
        read_ready = signal("read_ready", 2 * NG, head=3)
        read_summed = signal("read_summed", NG, head=2)
        pairs_added = signal("pairs_added", NG)
        y_read = signal("y_read", 2, head=1)
        y_gated_ready = signal("y_gated_ready", 2, head=3)

        P_OUT, P_MEAN2, P_VAR2, P_GATE, P_WCOL, P_UP0, P_DOWN0 = 0, 1, 2, 3, 4, (5, 10), (9, 14)
        P_MEAN3, P_VAR3, P_Q, P_K, P_V, P_LOW, P_SCORE = 15, 16, 17, 18, 19, 20, 21
        P_PROBS, P_ATTN, P_MEAN4, P_VAR4, P_ROUTER, P_GATES, NPT = 24, 27, 28, 29, 30, 31, 32
        KEEP_AT = 400
        p_mm = signal("p_mm", NPT)
        p_read = [signal(f"p_read{i}", NPT // 2, head=1) for i in range(2)]
        squared = signal("squared", 3)
        rs_ready = signal("rs_ready", 3)
        h1_begun = signal("h1_begun")
        xn2_ready = signal("xn2_ready")
        gate_step = signal("gate_step", 5)
        gate_exp_ready = signal("gate_exp_ready")
        experts_known = sem("experts_known")
        expert_loaded = [signal(f"expert_loaded{j}", 16) for j in range(2)]
        b2_step = signal("b2_step", 3)
        xn3_ready = signal("xn3_ready")
        low_step = sem("low_step")
        keep_ready = signal("keep_ready")
        max_ready = signal("max_ready", 3)
        bias_ready = signal("bias_ready", 3)
        scale_step = signal("scale_step", 2)
        probs_scaled = signal("probs_scaled", 3)
        xn4_ready = signal("xn4_ready")
        router_step = signal("router_step", 4)
        router_exp_ready = signal("router_exp_ready")
        xn4_kept = signal("xn4_kept", 16, head=16)
        gates_kept = signal("gates_kept", 16, head=16)

        gates_loaded, top_step, mask_stored, mask_loaded, zeroed = (
            sem(n) for n in ("gates_loaded", "top_step", "mask_stored", "mask_loaded", "zeroed"))
        gates_hi, gates_left, gates_mids, gates_split = (
            sem(n) for n in ("gates_hi", "gates_left", "gates_mids", "gates_split"))
        up_mm = signal("up_mm", E)
        gate_rows_mm = signal("gate_rows_mm", E)
        hid1_ready = signal("hid1_ready", E, head=2)
        hid1_gated = signal("hid1_gated", E, head=2)
        down_mm = signal("down_mm", E, head=2)
        out_ready = signal("out_ready", 1, head=2)
        out_stored = signal("out_stored", 16, head=16)

        def wait(eng, s, b, n):
            eng.wait_ge(s.sem, s.at(b, n))

        def grant(eng, s):
            eng.sem_inc(s.sem, s.head)

        def per_batch(eng, run):
            with eng.Fori(0, B // 2) as pair:
                run(pair * 2, 0)
                run(pair * 2 + 1, 1)

        SLOTS = 3 * NG
        FRONT_PARTS, POST_PARTS = 12, 31
        FRONT_FROM, POST_FROM = 1, 6

        def due(slot, first, parts):
            return max(0, (slot + 1 - first) * parts // (SLOTS - first))

        def turn(n, i, slot, front, post, ahead=True, behind=True):
            f, p = front(n + 1, 1 - i), post(n - 1, 1 - i)
            for at in range(SLOTS):
                slot(n, i, at, behind, ahead)
                if behind:
                    for _ in range(due(at, POST_FROM, POST_PARTS) - due(at - 1, POST_FROM, POST_PARTS)):
                        next(p, None)
                if ahead and FRONT_FROM <= at < FRONT_FROM + FRONT_PARTS:
                    next(f, None)

        def all_batches(eng, begin, slot, front, post, last_slots):
            for _ in front(0, 0):
                pass
            begin()
            turn(0, 0, slot, front, post, behind=False)
            with eng.Fori(0, (B - 2) // 2) as pair:
                turn(pair * 2 + 1, 1, slot, front, post)
                turn(pair * 2 + 2, 0, slot, front, post)
            turn(B - 1, 1, slot, front, post, ahead=False)
            for at in range(POST_FROM):
                last_slots(B, 0, at)
            for _ in post(B - 1, 1):
                pass

        def cols(area, b):
            return area[:, bass.ds(b * T, T)]

        def vec(k):
            return vecs[:, k:k + 1]

        def p_tile(n):
            return p_bank[:, n % 2, :]

        def wait_p_read(eng, b, n):
            wait(eng, p_read[n % 2], b, n // 2 + 1)

        def then_p_read(ins, n):
            ins.then_inc(p_read[n % 2].sem, 1)

        block = ctx.enter_context(nc.Block())

        @block.sync
        def _(sp):
            sp.dma_start(x2[0:64, :, :], x_t).then_inc(x_loaded, 16)
            sp.dma_start(x2[64:P, :, 0:T_IN - 1], x_t[:, :, 1:T_IN]).then_inc(x_loaded, 16)
            sp.dma_start(w_in_sb[:, :], w_in).then_inc(ssm_loaded, 16)
            sp.dma_start(conv_rows, conv_w.partition_broadcast(P)).then_inc(ssm_loaded, 16)
            sp.dma_start(w_x_sb[:, :, :], w_x).then_inc(ssm_loaded, 16)
            sp.dma_start(w_dt_sb[:, :], w_dt).then_inc(ssm_loaded, 16)
            sp.dma_start(w_out_sb[:, :, :], w_out).then_inc(ssm_loaded, 16)
            sp.dma_start(gate_w_sb[:, :], gate_w).then_inc(gate_loaded, 16)
            sp.dma_start(gate_b_sb[:, :], gate_b).then_inc(gate_loaded, 16)
            sp.dma_start(qkv_sb[:, :, :], qkv_w).then_inc(gate_loaded, 16)
            sp.dma_start(router_sb[:, :], router_w).then_inc(gate_loaded, 16)
            sp.dma_start(moe1_w1_sb[:, :, :], moe1_w1).then_inc(moe1_loaded, 16)
            sp.dma_start(moe1_w2_sb[:, :, :, :], moe1_w2).then_inc(moe1_loaded, 16)
            sp.dma_start(moe1_b2_sb[:, :], moe1_b2).then_inc(moe1_loaded, 16)
            grant(sp, xn4_kept)
            grant(sp, gates_kept)
            grant(sp, out_stored)

            def store_b(b, i):
                wait(sp, bc_copied, b, 1)
                sp.dma_start(b_dram[i], bc_f32[16:32, :]).then_inc(b_stored.sem, 16)

            def load_b(b, i):
                wait(sp, b_stored, b, 16)
                for g in range(GROUPS):
                    wait(sp, drive_ready, b - 1, GROUPS + g + 1)
                    sp.dma_start(b_rows[:, GROUP * g:GROUP * (g + 1), :],
                                 b_dram[i, GROUP * g:GROUP * (g + 1), :].partition_broadcast(P))\
                      .then_inc(b_loaded[g].sem, 16)

            def load_experts(b):
                sp.wait_ge(experts_known, 1)
                chosen = [sp.value_load(top_i[0:1, j:j + 1], min_val=0, max_val=E - 1) for j in range(2)]
                sp.sem_clear(experts_known)
                for j, e in enumerate(chosen):
                    sp.dma_start(expert[j][:, :], moe0[bass.ds(e, 1), :, :].rearrange("a p n -> p (a n)"))\
                      .then_inc(expert_loaded[j].sem, 16)

            def keep_rest(b):
                wait(sp, xn4_ready, b, 1)
                sp.dma_start(cols(xn4_all, b), xn4[:, 0:T]).then_inc(xn4_kept.sem, 16)
                wait_p_read(sp, b, P_GATES)
                sp.dma_start(gates_dram[bass.ds(b, 1), :, :].rearrange("a e t -> e (a t)"), gates_t[:, :])\
                  .then_inc(gates_kept.sem, 16)

            def both(n, i):
                store_b(n + 1, 1 - i)
                load_experts(n - 1)
                load_b(n + 1, 1 - i)
                keep_rest(n - 1)

            for b in range(2):
                store_b(b, b)
                load_b(b, b)
            with sp.Fori(0, (B - 2) // 2) as pair:
                both(pair * 2 + 1, 1)
                both(pair * 2 + 2, 0)
            for b in (B - 2, B - 1):
                load_experts(b)
                keep_rest(b)

            wait(sp, gates_kept, B - 1, 16)
            sp.dma_start(top_in, gates_dram.rearrange("b e t -> (b e) t")).then_inc(gates_loaded, 16)
            sp.wait_ge(top_step, 2 * TOP_ROUNDS + (2 if TOP_TOKENS % 8 else 1))
            sp.dma_start(mask_dram.rearrange("b e t -> (b e) t"), gates_masked).then_inc(mask_stored, 16)
            sp.wait_ge(mask_stored, 16)
            sp.wait_ge(zeroed, 1)
            for k in range(3):
                sp.dma_start(gates_e[32 * k:32 * k + E, :].rearrange("e (b t) -> e b t", b=B),
                             mask_dram.rearrange("b e t -> e b t")).then_inc(mask_loaded, 16)

            def result(b, i):
                wait(sp, out_ready, b, 1)
                sp.dma_start(cols(out, b), out_sb[i]).then_inc(out_stored.sem, 16)

            per_batch(sp, result)
            wait(sp, out_stored, B - 1, 16)
            wait(sp, xn4_kept, B - 1, 16)

        @block.gpsimd
        def _(pool):
            pool.memset(ident[:, :], 0.0).then_inc(ident_step, 1)
            pool.wait_ge(ident_step, 1)
            pool.affine_select(out=ident[:, :], in_=ident[:, :], compare_op=ALU.not_equal, fill=1.0, base=0,
                               pattern=[[-1, P]], channel_multiplier=1).then_inc(ident_step, 1)
            pool.memset(mean_mat[:, :], 1.0 / P).then_inc(ident_step, 1)
            pool.memset(pick[:, :], 0.0).then_inc(pick_step, 1)
            for k in range(3):
                pool.wait_ge(pick_step, k + 1)
                pool.affine_select(out=pick[:, :], in_=pick[:, :], compare_op=ALU.not_equal, fill=1.0,
                                   base=-32 * k, pattern=[[-1, STATES]], channel_multiplier=1).then_inc(pick_step, 1)
            pool.iota(token_index[:, :], pattern=[[1, T]], base=0, channel_multiplier=0,
                      allow_small_or_imprecise_dtypes=True).then_inc(index_step, 1)
            grant(pool, drive_ready)

            def front(b, i):
                for _ in range(FRONT_PARTS - 1):
                    yield
                wait(pool, f_read, b, F_XI + 2)
                wait(pool, dt_ready, b, 1)
                pool.tensor_tensor(dtu[i][:, :, :], dt[i][:, :, :], xc[i][:, :, :], ALU.mult)\
                    .then_inc(dtu_ready.sem, 1)

            def drive_group(b, i, g):
                half, states = g // GROUPS, g % GROUPS
                if g == 0:
                    wait(pool, dtu_ready, b, 1)
                if half == 0:
                    wait(pool, b_loaded[states], b, 16)
                wait(pool, state_ready, b, g - 1)
                pool.tensor_tensor(by_state(drive[g % 2]),
                                   dtu[i][:, half:half + 1, :].to_broadcast([P, GROUP, T]),
                                   b_rows[:, GROUP * states:GROUP * (states + 1), :], ALU.mult)\
                    .then_inc(drive_ready.sem, 1)

            def add_pairs(b, g):
                wait(pool, read_ready, b, 2 * (g + 1))
                r = by_state(read[g % 2])
                pool.tensor_tensor(r[:, 0:2, :], r[:, 0:2, :], r[:, 2:4, :], ALU.add).then_inc(pairs_added.sem, 1)

            def slot(n, i, at, behind, ahead):
                g = at // 3
                if at % 3 == 1 and g < NG - 1:
                    drive_group(n, i, g + 1)
                elif at % 3 == 1 and ahead:
                    drive_group(n + 1, 1 - i, 0)
                if at % 3 == 2 and g:
                    add_pairs(n, g - 1)
                elif at % 3 == 2 and behind:
                    add_pairs(n - 1, NG - 1)

            def last_slots(n, i, at):
                if at == 2:
                    add_pairs(n - 1, NG - 1)

            def post(b, i):
                yield

            all_batches(pool, lambda: drive_group(0, 0, 0), slot, front, post, last_slots)
            wait(pool, y_read, B - 1, 2)
            pool.memset(gates_e, 0.0).then_inc(zeroed, 1)

        @block.scalar
        def _(act):
            act.dma_start(tok_w_sb, tok_w).then_inc(tokw_loaded, 16)
            act.dma_start(vecs[:, :], vec_in).then_inc(vec_loaded, 16)
            grant(act, hid1_ready)
            act.preload_act_table_set(LN_EXP)
            act.wait_ge(vec_loaded, 16)
            act.activation(neg_a[:, :], vecs[:, A_LOG:A_LOG + HALVES * STATES], ACT.Exp).then_inc(a_exp, 1)
            for b in range(B):
                act.wait_ge(tok_mm, b + 1)
                act.activation(tok_y[:, b * T:(b + 1) * T], c_rows[:, b % 4, 0:T], ACT.Relu, bias=vec(TOK_B))\
                   .then_inc(tok_relu, 1)
            act.wait_ge(tok_step, 2)
            act.activation(tok_rs[:, 1:2], tok_rs[:, 0:1], ACT.Ln).then_inc(tok_act, 1)
            act.wait_ge(tok_act, 1)
            act.activation(tok_rs[:, 2:3], tok_rs[:, 1:2], ACT.Exp, scale=-0.5).then_inc(tok_act, 1)

            def front(b, i):
                yield
                wait(act, f_read, b, F_MEAN + 1)
                act.activation(f_square, f_centered[:, :], ACT.Square).then_inc(f_squared.sem, 1)
                yield
                act.preload_act_table_set(LN_EXP)
                wait(act, f_mm, b, F_VAR + 1)
                act.activation(f_rs, f_bank[:, 0:T], ACT.Ln, scale=1.0 + EPS, bias=eps_col[:, 1:2])\
                   .then_inc(f_read.sem, 1)
                wait(act, f_read, b, F_VAR + 1)
                act.activation(f_rs, f_rs, ACT.Exp, scale=-0.5).then_inc(f_rs_ready.sem, 1)
                yield
                yield
                wait(act, y_gated_ready, b - 2, 2)
                for half in range(HALVES):
                    wait(act, f_mm, b, F_XI + half + 1)
                    act.activation(xc[i][:, half, :], f_bank[:, 0:T], ACT.Silu, bias=vec(CONV_B + half))\
                       .then_inc(f_read.sem, 1)
                for half in range(HALVES):
                    wait(act, f_mm, b, F_Z + half + 1)
                    act.activation(zs[i][:, half, :], f_bank[:, 0:T], ACT.Silu).then_inc(f_read.sem, 1)
                act.preload_act_table_set(LN_EXP)
                yield
                wait(act, f_mm, b, F_BC + 1)
                act.activation(bc_parts[i][:, :], f_bank[0:96, 0:T], ACT.Copy).then_inc(bc_hi.sem, 1)
                yield
                wait(act, f_read, b, F_BC + 1)
                act.activation(bc_parts[i][32:64, :], bc_rest[32:64, :], ACT.Copy)
                act.activation(bc_mid[64:96, :], bc_rest[64:96, :], ACT.Copy).then_inc(bc_mids.sem, 1)
                wait(act, f_mm, b, F_DT_LOW + 1)
                act.activation(dt_low[:, :], f_bank[0:RANK, 0:T], ACT.Copy).then_inc(f_read.sem, 1)
                yield
                yield
                for half in range(HALVES):
                    wait(act, f_mm, b, F_DT + half + 1)
                    act.activation(dt_soft[:, half, :], f_bank[:, 0:T], ACT.Abs, bias=vec(B_DT + half))\
                       .then_inc(dt_abs_ready.sem, 1)
                    yield
                wait(act, dt_abs_ready, b, 2)
                act.activation(dt_soft[:, :, :], dt_soft[:, :, :], ACT.Exp, scale=-1.0).then_inc(dt_exp_ready.sem, 1)
                wait(act, dt_exp_ready, b, 1)
                act.activation(dt_soft[:, :, :], dt_soft[:, :, :], ACT.Ln, bias=eps_col[:, 2:3])\
                   .then_inc(dt_ln_ready.sem, 1)
                yield

            def decay_group(b, i, g):
                half = g // GROUPS
                if g == 0:
                    wait(act, dt_ready, b, 1)
                wait(act, state_ready, b, g - 1)
                for k in range(GROUP):
                    at = half * STATES + g % GROUPS * GROUP + k
                    ins = act.activation(by_state(decay[g % 2])[:, k, 1:T], dt[i][:, half, 1:T], ACT.Exp,
                                         scale=neg_a[:, at:at + 1])
                ins.then_inc(decay_ready.sem, 1)

            def slot(n, i, at, behind, ahead):
                g = at // 3
                if at % 3 == 1 and g < NG - 1:
                    decay_group(n, i, g + 1)
                elif at % 3 == 1 and ahead:
                    decay_group(n + 1, 1 - i, 0)

            def norm(b, k, p_mean):
                wait_p_read(act, b, p_mean)
                act.activation(square[:, :], centered[:, :], ACT.Square).then_inc(squared.sem, 1)
                yield
                wait(act, p_mm, b, p_mean + 2)
                then_p_read(act.activation(rs[:, :], p_tile(p_mean + 1)[:, 0:T], ACT.Ln, bias=eps_col[:, 0:1]),
                            p_mean + 1)
                wait_p_read(act, b, p_mean + 1)
                act.activation(rs[:, :], rs[:, :], ACT.Exp, scale=-0.5).then_inc(rs_ready.sem, 1)
                yield

            def post(b, i):
                yield
                yield from norm(b, 0, P_MEAN2)
                yield
                yield
                wait(act, gate_step, b, 2)
                act.activation(gate_tmp[:, 1:2], gate_tmp[:, 0:1], ACT.Exp).then_inc(gate_exp_ready.sem, 1)
                yield
                yield
                yield
                for j in range(2):
                    wait(act, expert_loaded[j], b, 16)
                    for m in range(H0T):
                        wait(act, p_mm, b, P_UP0[j] + m + 1)
                        if j and m == 0:
                            wait(act, p_mm, b, P_DOWN0[0] + 1)
                        then_p_read(act.activation(hid0[:, m, :], p_tile(P_UP0[j] + m)[:, 0:T], ACT.Gelu,
                                                   bias=expert[j][:, B1_AT + m:B1_AT + m + 1]), P_UP0[j] + m)
                    act.preload_act_table_set(LN_EXP)
                    yield
                    yield
                yield
                yield from norm(b, 1, P_MEAN3)
                yield
                wait(act, p_mm, b, P_Q + 1)
                then_p_read(act.activation(q_t[:, :], p_tile(P_Q)[:, 0:TP], ACT.Copy), P_Q)
                wait(act, p_mm, b, P_K + 1)
                then_p_read(act.activation(k_t[:, :], p_tile(P_K)[:, 0:T], ACT.Identity, accum_out=k_sum[:, :]), P_K)
                yield
                yield
                for s in range(3):
                    wait(act, bias_ready, b, s + 1)
                    then_p_read(act.activation(probs[:, s, :], p_tile(P_SCORE + s)[:, 0:T], ACT.Exp,
                                               scale=SCORE_SCALE, bias=s_bias[:, s:s + 1],
                                               accum_out=s_sum[:, s:s + 1]), P_SCORE + s)
                    if s == 0:
                        yield
                yield
                yield
                for s, (t0, n) in enumerate(TILES):
                    wait(act, p_mm, b, P_PROBS + s + 1)
                    then_p_read(act.activation(probs_t[0:n, s, :], p_tile(P_PROBS + s)[0:n, 0:TP], ACT.Copy),
                                P_PROBS + s)
                    if s:
                        yield
                yield
                yield from norm(b, 2, P_MEAN4)
                yield
                yield
                wait_p_read(act, b, P_ROUTER)
                act.activation(r_exp[:, :, :], r_cent[:, :, :], ACT.Exp).then_inc(router_exp_ready.sem, 1)
                yield
                yield
                wait(act, gates_kept, b - 1, 16)
                wait(act, p_mm, b, P_GATES + 1)
                then_p_read(act.activation(gates_t[:, :], p_tile(P_GATES)[0:E, 0:T], ACT.Copy), P_GATES)

            all_batches(act, lambda: decay_group(0, 0, 0), slot, front, post, lambda n, i, at: None)

            act.wait_ge(mask_loaded, 48)
            act.activation(gates_parts, gates_e, ACT.Copy).then_inc(gates_hi, 1)
            act.wait_ge(gates_left, 1)
            act.activation(gates_parts[32:64, :], gates_rest[32:64, :], ACT.Copy)
            act.activation(gates_mid[64:96, :], gates_rest[64:96, :], ACT.Copy).then_inc(gates_mids, 1)

            def last_layer(b, i):
                for e in range(E):
                    wait(act, up_mm, b, e + 1)
                    wait(act, hid1_gated, b, e - 1)
                    for f in range(2):
                        k = MOE1_B1 + 2 * e + f
                        ins = act.activation(hid1[e % 2][:, f, :], c_rows[:, 2 * (e % 2) + f, 0:T], ACT.Gelu,
                                             bias=vec(k))
                    ins.then_inc(hid1_ready.sem, 1)

            per_batch(act, last_layer)

        @block.vector
        def _(dve):
            dve.memset(ssm_in[:, 0:CONV - 1], 0.0)
            dve.memset(eps_col[:, 0:1], EPS)
            dve.memset(eps_col[:, 1:2], EPS * EPS)
            dve.memset(eps_col[:, 2:3], 1.0)
            dve.memset(w_bc[:, :, :], 0.0).then_inc(weights_made, 1)
            dve.memset(xn3[:, T:TP], 0.0)
            dve.memset(xn4[:, T:TP], 0.0)
            dve.memset(keep_row[:, :], 1.0)
            dve.memset(ones_row[:, :], 1.0).then_inc(pads_ready, 1)
            for s in (state_ready, read_ready, y_read, y_gated_ready, hid1_gated, out_ready):
                grant(dve, s)

            dve.wait_ge(ssm_loaded, 80)
            dve.tensor_tensor(w_conv[:, :, :], conv_rows,
                              w_in_sb[:, 0:256].unsqueeze(1).to_broadcast([P, CONV, 256]), ALU.mult)\
               .then_inc(weights_made, 1)
            dve.wait_ge(weights_made, 2)
            for k in range(3):
                dve.tensor_copy(w_bc[:, :, 32 * k:32 * k + STATES], w_x_sb[:, :, RANK + STATES:])
            dve.tensor_copy(w_bc[:, :, STATES:2 * STATES], w_x_sb[:, :, RANK:RANK + STATES]).then_inc(weights_made, 1)
            for i in range(2):
                ins = dve.memset(by_state(decay[i])[:, :, 0:1], 0.0)
            ins.then_inc(weights_made, 1)
            dve.wait_ge(weights_made, 4)
            dve.wait_ge(a_exp, 1)
            dve.tensor_scalar(neg_a[:, :], neg_a[:, :], -1.0, None, ALU.mult).then_inc(a_ready, 1)

            for b in range(B):
                dve.wait_ge(tok_relu, b + 1)
                dve.bn_stats(bn_parts[:, b, :], tok_y[:, b * T:(b + 1) * T]).then_inc(bn_part, 1)
            dve.wait_ge(bn_part, B)
            dve.bn_aggr(bn[:, :], bn_parts[:, :, :]).then_inc(tok_step, 1)
            dve.wait_ge(tok_step, 1)
            dve.tensor_scalar(tok_rs[:, 0:1], bn[:, 1:2], EPS, None, ALU.add).then_inc(tok_step, 1)
            dve.wait_ge(tok_act, 2)
            dve.tensor_tensor(tok_rs[:, 3:4], tok_rs[:, 2:3], vec(GAMMA), ALU.mult).then_inc(tok_step, 1)
            dve.wait_ge(tok_step, 3)
            dve.tensor_tensor(tok_rs[:, 4:5], tok_rs[:, 3:4], bn[:, 0:1], ALU.mult).then_inc(tok_step, 1)
            dve.wait_ge(tok_step, 4)
            dve.tensor_tensor(tok_rs[:, 5:6], vec(BETA), tok_rs[:, 4:5], ALU.subtract).then_inc(tok_step, 1)
            dve.wait_ge(tok_step, 5)

            def front(b, i):
                dve.tensor_scalar(h0[:, :], cols(tok_y, b), tok_rs[:, 3:4], tok_rs[:, 5:6], ALU.mult, ALU.add)\
                   .then_inc(h0_ready.sem, 1)
                yield
                wait(dve, h0_ready, b, 1)
                wait(dve, f_mm, b, F_MEAN + 1)
                dve.tensor_tensor(f_centered[:, :], h0[:, :], f_bank[:, 0:T], ALU.subtract)\
                   .then_inc(f_read.sem, 1)
                yield
                yield
                wait(dve, f_rs_ready, b, 1)
                dve.scalar_tensor_tensor(f_centered[:, :], f_centered[:, :], vec(LN_G), f_rs,
                                         ALU.mult, ALU.mult).then_inc(f_scaled.sem, 1)
                wait(dve, f_scaled, b, 1)
                dve.tensor_scalar(ssm_in[:, CONV - 1:], f_centered[:, :], vec(LN_B), None, ALU.add)\
                   .then_inc(ssm_in_ready.sem, 1)
                yield
                yield
                wait(dve, bc_hi, b, 1)
                dve.tensor_copy(bc_f32[:, :], f_bank[0:32, 0:T]).then_inc(bc_copied.sem, 1)
                dve.tensor_tensor(bc_rest[:, :], f_bank[0:96, 0:T], bc_parts[i][:, :], ALU.subtract)\
                   .then_inc(f_read.sem, 1)
                yield
                yield
                wait(dve, bc_mids, b, 1)
                dve.tensor_tensor(bc_parts[i][64:96, :], bc_rest[64:96, :], bc_mid[64:96, :], ALU.subtract)\
                   .then_inc(bc_ready.sem, 1)
                yield
                for half in range(HALVES):
                    wait(dve, dt_abs_ready, b, half + 1)
                    dve.tensor_scalar(dt[i][:, half, :], f_bank[:, 0:T], vec(B_DT + half), 0.0, ALU.add, ALU.max)\
                       .then_inc(f_read.sem, 1)
                    yield
                yield
                wait(dve, f_read, b, F_DT + 2)
                wait(dve, dt_ln_ready, b, 1)
                dve.tensor_tensor(dt[i][:, :, :], dt[i][:, :, :], dt_soft[:, :, :], ALU.add)\
                   .then_inc(dt_ready.sem, 1)

            def times_c(b, g, k):
                wait(dve, c_ready, b, 2 * g + k + 1)
                wait(dve, state_ready, b, g + 1)
                wait(dve, read_summed, b, g - 1)
                dve.tensor_tensor(by_state(read[g % 2])[:, 2 * k:2 * k + 2, :],
                                  by_state(state[g % 2])[:, 2 * k:2 * k + 2, :],
                                  c_rows[:, 2 * k:2 * k + 2, 0:T], ALU.mult).then_inc(read_ready.sem, 1)

            def gate(b, i, half):
                wait(dve, read_summed, b, GROUPS * (half + 1))
                dve.scalar_tensor_tensor(y_gated[:, half, :], xc[i][:, half, :], vec(D_SKIP + half),
                                         y_bank[:, 0:T], ALU.mult, ALU.add).then_inc(y_read.sem, 1)
                wait(dve, y_read, b, half + 1)
                dve.tensor_tensor(y_gated[:, half, :], y_gated[:, half, :], zs[i][:, half, :], ALU.mult)\
                   .then_inc(y_gated_ready.sem, 1)

            def slot(n, i, at, behind, ahead):
                g = at // 3
                if at % 3 == 0:
                    wait(dve, decay_ready, n, g + 1)
                    wait(dve, drive_ready, n, g + 1)
                    wait(dve, read_ready, n, 2 * (g - 1))
                    dve.tensor_tensor_scan(state[g % 2], decay[g % 2], drive[g % 2], 0.0, ALU.mult, ALU.add)\
                       .then_inc(state_ready.sem, 1)
                elif g:
                    times_c(n, g - 1, at % 3 - 1)
                elif behind:
                    times_c(n - 1, NG - 1, at % 3 - 1)
                if at == 3 * (GROUPS + 1) + 2:
                    gate(n, i, 0)
                if at == 5 and behind:
                    gate(n - 1, 1 - i, 1)

            def last_slots(n, i, at):
                if at in (1, 2):
                    times_c(n - 1, NG - 1, at - 1)
                if at == 5:
                    gate(n - 1, 1 - i, 1)

            def center(b, h, p_mean):
                wait(dve, p_mm, b, p_mean + 1)
                then_p_read(dve.tensor_tensor(centered[:, :], h, p_tile(p_mean)[:, 0:T], ALU.subtract), p_mean)

            def post(b, i):
                dve.tensor_scalar(h1[:, :], cols(tok_y, b), tok_rs[:, 3:4], tok_rs[:, 5:6], ALU.mult, ALU.add)\
                   .then_inc(h1_begun.sem, 1)
                wait(dve, h1_begun, b, 1)
                wait(dve, p_mm, b, P_OUT + 1)
                then_p_read(dve.tensor_tensor(h1[:, :], h1[:, :], p_tile(P_OUT)[:, 0:T], ALU.add), P_OUT)
                yield
                wait_p_read(dve, b, P_OUT)
                center(b, h1[:, :], P_MEAN2)
                yield
                yield
                wait(dve, rs_ready, b, 1)
                dve.scalar_tensor_tensor(xn2, centered[:, :], 1.0, rs[:, :], ALU.mult, ALU.mult,
                                         accum_out=pooled[:, :]).then_inc(xn2_ready.sem, 1)
                yield
                wait(dve, p_mm, b, P_GATE + 1)
                then_p_read(dve.scalar_tensor_tensor(gate_row[:, :], p_tile(P_GATE)[0:1, 0:E], 1.0 / T,
                                                     gate_b_sb[:, :], ALU.mult, ALU.add), P_GATE)
                wait_p_read(dve, b, P_GATE)
                dve.memset(spare[:, :], 0.0)
                dve.max(top_v[:, :], gate_row[:, :]).then_inc(gate_step.sem, 1)
                wait(dve, gate_step, b, 1)
                dve.memset(spare[:, :], 0.0)
                dve.max_index(top_i[:, :], top_v[:, :], gate_row[:, :]).then_inc(experts_known, 1)
                dve.tensor_tensor(gate_tmp[:, 0:1], top_v[:, 1:2], top_v[:, 0:1], ALU.subtract)\
                   .then_inc(gate_step.sem, 1)
                yield
                wait(dve, gate_exp_ready, b, 1)
                dve.tensor_scalar(gate_tmp[:, 2:3], gate_tmp[:, 1:2], 1.0, None, ALU.add).then_inc(gate_step.sem, 1)
                wait(dve, gate_step, b, 3)
                dve.reciprocal(w_pair[:, 0:1], gate_tmp[:, 2:3]).then_inc(gate_step.sem, 1)
                wait(dve, gate_step, b, 4)
                dve.tensor_tensor(w_pair[:, 1:2], gate_tmp[:, 1:2], w_pair[:, 0:1], ALU.mult)\
                   .then_inc(gate_step.sem, 1)
                yield
                wait(dve, p_mm, b, P_WCOL + 1)
                then_p_read(dve.tensor_copy(w_col[:, :], p_tile(P_WCOL)[:, 0:2]), P_WCOL)
                yield
                yield
                wait_p_read(dve, b, P_WCOL)
                for j in range(2):
                    wait(dve, expert_loaded[j], b, 16)
                dve.tensor_tensor(b2_mix[:, 0:1], expert[1][:, B2_AT:B2_AT + 1], w_col[:, 1:2], ALU.mult)\
                   .then_inc(b2_step.sem, 1)
                wait(dve, b2_step, b, 1)
                dve.scalar_tensor_tensor(b2_mix[:, 1:2], expert[0][:, B2_AT:B2_AT + 1], w_col[:, 0:1],
                                         b2_mix[:, 0:1], ALU.mult, ALU.add).then_inc(b2_step.sem, 1)
                wait(dve, b2_step, b, 2)
                dve.tensor_scalar(h2[:, :], h1[:, :], b2_mix[:, 1:2], None, ALU.add)\
                   .then_inc(b2_step.sem, 1)
                yield
                yield
                wait(dve, b2_step, b, 3)
                wait(dve, p_mm, b, P_DOWN0[0] + 1)
                then_p_read(dve.scalar_tensor_tensor(h2[:, :], p_tile(P_DOWN0[0])[:, 0:T], w_col[:, 0:1],
                                                     h2[:, :], ALU.mult, ALU.add), P_DOWN0[0])
                yield
                yield
                wait(dve, p_mm, b, P_DOWN0[1] + 1)
                wait_p_read(dve, b, P_DOWN0[0])
                then_p_read(dve.scalar_tensor_tensor(h2[:, :], p_tile(P_DOWN0[1])[:, 0:T], w_col[:, 1:2],
                                                     h2[:, :], ALU.mult, ALU.add), P_DOWN0[1])
                yield
                wait_p_read(dve, b, P_DOWN0[1])
                center(b, h2[:, :], P_MEAN3)
                yield
                yield
                wait(dve, rs_ready, b, 2)
                dve.tensor_tensor(xn3[:, 0:T], centered[:, :], rs[:, :], ALU.mult).then_inc(xn3_ready.sem, 1)
                yield
                yield
                wait(dve, p_mm, b, P_V + 1)
                then_p_read(dve.tensor_copy(v_sb[:, :, :], p_tile(P_V)[:, 0:TP].rearrange("p (s o) -> p s o", s=3)),
                            P_V)
                wait(dve, p_mm, b, P_LOW + 1)
                then_p_read(dve.tensor_scalar(low_row, p_tile(P_LOW)[0:1, 0:T], -1.0, None, ALU.mult), P_LOW)
                if i == 0 and not isinstance(b, int):
                    with dve.If_eq(dve.to_reg(b), 0):
                        wait_p_read(dve, b, P_LOW)
                        dve.memset(spare[:, :], 0.0)
                        dve.max(low_v[:, :], low_row).then_inc(low_step, 1)
                        dve.wait_ge(low_step, 1)
                        dve.max_index(low_i[:, :], low_v[:, :], low_row).then_inc(low_step, 1)
                        dve.wait_ge(low_step, 2)
                        dve.tensor_copy(low_f[:, :], low_i[:, 0:1]).then_inc(low_step, 1)
                        dve.wait_ge(low_step, 3)
                        dve.wait_ge(index_step, 1)
                        dve.tensor_scalar(keep_row[:, 0:T], token_index[:, :], low_f[:, :], None, ALU.not_equal)\
                           .then_inc(low_step, 1)
                yield
                for s in range(3):
                    wait(dve, p_mm, b, P_SCORE + s + 1)
                    if s == 0:
                        dve.tensor_copy(keep[:, :], p_tile(P_SCORE)[:, KEEP_AT:KEEP_AT + 3]).then_inc(keep_ready.sem, 1)
                    dve.reduce_max(s_max[:, s:s + 1], p_tile(P_SCORE + s)[:, 0:T], AX_X).then_inc(max_ready.sem, 1)
                    wait(dve, max_ready, b, s + 1)
                    dve.tensor_scalar(s_bias[:, s:s + 1], s_max[:, s:s + 1], -SCORE_SCALE, None, ALU.mult)\
                       .then_inc(bias_ready.sem, 1)
                    if s == 0:
                        yield
                yield
                for s in range(3):
                    wait_p_read(dve, b, P_SCORE + s)
                dve.reciprocal(s_inv[:, :], s_sum[:, :]).then_inc(scale_step.sem, 1)
                wait(dve, scale_step, b, 1)
                wait(dve, keep_ready, b, 1)
                dve.tensor_tensor(s_scale[:, :], s_inv[:, :], keep[:, :], ALU.mult).then_inc(scale_step.sem, 1)
                wait(dve, scale_step, b, 2)
                for s in range(3):
                    dve.tensor_scalar(probs[:, s, :], probs[:, s, :], s_scale[:, s:s + 1], None, ALU.mult)\
                       .then_inc(probs_scaled.sem, 1)
                for _ in range(3):
                    yield
                wait(dve, p_mm, b, P_ATTN + 1)
                then_p_read(dve.tensor_tensor(cols(h3_all, b), h2[:, :], p_tile(P_ATTN)[:, 0:T], ALU.add), P_ATTN)
                yield
                wait_p_read(dve, b, P_ATTN)
                center(b, cols(h3_all, b), P_MEAN4)
                yield
                yield
                wait(dve, rs_ready, b, 3)
                wait(dve, xn4_kept, b - 1, 16)
                dve.tensor_tensor(xn4[:, 0:T], centered[:, :], rs[:, :], ALU.mult).then_inc(xn4_ready.sem, 1)
                yield
                logits = p_tile(P_ROUTER)[:, 0:3 * E].rearrange("p (s e) -> p s e", s=3)
                wait(dve, p_mm, b, P_ROUTER + 1)
                dve.reduce_max(r_max[:, :], logits, AX_X).then_inc(router_step.sem, 1)
                wait(dve, router_step, b, 1)
                then_p_read(dve.tensor_tensor(r_cent[:, :, :], logits,
                                              r_max[:, :].unsqueeze(2).to_broadcast([P, 3, E]), ALU.subtract),
                            P_ROUTER)
                yield
                yield
                wait(dve, router_exp_ready, b, 1)
                dve.reduce_sum(r_sum[:, :], r_exp[:, :, :], AX_X).then_inc(router_step.sem, 1)
                wait(dve, router_step, b, 2)
                dve.reciprocal(r_inv[:, :], r_sum[:, :]).then_inc(router_step.sem, 1)
                wait(dve, router_step, b, 3)
                dve.tensor_tensor(r_prob[:, :, :], r_exp[:, :, :],
                                  r_inv[:, :].unsqueeze(2).to_broadcast([P, 3, E]), ALU.mult)\
                   .then_inc(router_step.sem, 1)

            all_batches(dve, lambda: None, slot, front, post, last_slots)

            dve.wait_ge(gates_loaded, 16)
            now = top_in
            for r in range(TOP_ROUNDS):
                dve.max(top_8[:, :], now).then_inc(top_step, 1)
                dve.wait_ge(top_step, 2 * r + 1)
                if r == TOP_ROUNDS - 1 and TOP_TOKENS % 8:
                    dve.memset(top_8[:, TOP_TOKENS % 8:], -1.0).then_inc(top_step, 1)
                    dve.wait_ge(top_step, 2 * r + 2)
                then = top_work[r % 2]
                dve.match_replace(then, top_8[:, :], now, -1.0).then_inc(top_step, 1)
                now = then
                last = 2 * r + 2 + (1 if r == TOP_ROUNDS - 1 and TOP_TOKENS % 8 else 0)
                dve.wait_ge(top_step, last)
            dve.scalar_tensor_tensor(gates_masked, now, 0.0, top_in, ALU.is_lt, ALU.mult).then_inc(top_step, 1)
            dve.wait_ge(gates_hi, 1)
            dve.tensor_tensor(gates_rest, gates_e, gates_parts, ALU.subtract).then_inc(gates_left, 1)
            dve.wait_ge(gates_mids, 1)
            dve.tensor_tensor(gates_parts[64:96, :], gates_rest[64:96, :], gates_mid[64:96, :], ALU.subtract)\
               .then_inc(gates_split, 1)

            def last_layer(b, i):
                for e in range(E):
                    wait(dve, hid1_ready, b, e + 1)
                    wait(dve, gate_rows_mm, b, e + 1)
                    wait(dve, down_mm, b, e - 1)
                    gate_rows = (y_bank, f_bank)[e % 2][:, 0:T]
                    dve.tensor_tensor(hid1_g[e % 2], hid1[e % 2],
                                      gate_rows.unsqueeze(1).to_broadcast([P, 2, T]), ALU.mult)\
                       .then_inc(hid1_gated.sem, 1)
                wait(dve, down_mm, b, E)
                wait(dve, out_stored, b - 1, 16)
                dve.tensor_tensor(out_sb[i], cols(h3_all, b), p_bank[:, i, 0:T], ALU.add).then_inc(out_ready.sem, 1)

            per_batch(dve, last_layer)

        @block.tensor
        def _(pe):
            mm = nc.tensor.matmul
            for s in (read_summed, down_mm, f_read, *p_read):
                grant(pe, s)
            pe.wait_ge(x_loaded, 32)
            pe.wait_ge(tokw_loaded, 16)
            for b in range(B):
                if b >= 4:
                    pe.wait_ge(tok_relu, b - 3)
                y = c_rows[:, b % 4, 0:T]
                mm(y, tok_w_sb[:, 0, :], x2[:, b, 0:T], start=True, stop=False)
                mm(y, tok_w_sb[:, 1, :], x2[:, b, 2:2 + T], start=False, stop=False)
                mm(y, tok_w_sb[0:64, 2, :], x2[0:64, b, 4:4 + T], start=False, stop=True).then_inc(tok_mm, 1)
            pe.wait_ge(tok_relu, B)
            pe.wait_ge(ident_step, 3)
            pe.wait_ge(pick_step, 4)
            pe.wait_ge(weights_made, 3)
            pe.wait_ge(gate_loaded, 64)
            pe.wait_ge(pads_ready, 1)

            def front(b, i):
                f = f_bank[:, 0:T]

                def tile(n, *waits):
                    for s, k in waits:
                        wait(pe, s, b, k)
                    wait(pe, f_read, b, n)

                yield
                tile(F_MEAN, (h0_ready, 1))
                mm(f, mean_mat[:, :], h0[:, :], start=True, stop=True).then_inc(f_mm.sem, 1)
                yield
                tile(F_VAR, (f_squared, 1))
                mm(f, mean_mat[:, :], f_square, start=True, stop=True).then_inc(f_mm.sem, 1)
                yield
                yield
                for half in range(HALVES):
                    tile(F_XI + half, (ssm_in_ready, 1))
                    for j in range(CONV):
                        ins = mm(f, w_conv[:, j, P * half:P * (half + 1)], ssm_in[:, j:j + T],
                                 start=(j == 0), stop=(j == CONV - 1))
                    ins.then_inc(f_mm.sem, 1)
                for half in range(HALVES):
                    tile(F_Z + half)
                    mm(f, w_in_sb[:, 256 + P * half:256 + P * (half + 1)], ssm_in[:, CONV - 1:],
                       start=True, stop=True).then_inc(f_mm.sem, 1)
                yield
                tile(F_BC)
                for half in range(HALVES):
                    ins = mm(f_bank[0:96, 0:T], w_bc[:, half, :], xc[i][:, half, :], start=(half == 0),
                             stop=(half == 1))
                ins.then_inc(f_mm.sem, 1)
                yield
                tile(F_DT_LOW)
                for half in range(HALVES):
                    ins = mm(f_bank[0:RANK, 0:T], w_x_sb[:, half, 0:RANK], xc[i][:, half, :], start=(half == 0),
                             stop=(half == 1))
                ins.then_inc(f_mm.sem, 1)
                yield
                yield
                for half in range(HALVES):
                    tile(F_DT + half)
                    mm(f, w_dt_sb[:, P * half:P * (half + 1)], dt_low[:, :], start=True, stop=True)\
                        .then_inc(f_mm.sem, 1)
                    yield
                yield

            def c_pair(b, i, g, k):
                if g == 0 and k == 0:
                    wait(pe, bc_ready, b, 1)
                wait(pe, read_ready, b, 2 * (g - 1) + k + 1)
                for m in range(2):
                    s = g % GROUPS * GROUP + 2 * k + m
                    ins = mm(c_rows[:, 2 * k + m, 0:T], pick[:, s:s + 1].to_broadcast([96, P]),
                             bc_parts[i][:, :], start=True, stop=True)
                ins.then_inc(c_ready.sem, 1)

            def add_states(b, g):
                half, first, last = g // GROUPS, g % GROUPS == 0, g % GROUPS == GROUPS - 1
                if first:
                    wait(pe, y_read, b, half)
                wait(pe, pairs_added, b, g + 1)
                for k in range(2):
                    ins = mm(y_bank[:, 0:T], ident[:, :], by_state(read[g % 2])[:, k, :],
                             start=(first and k == 0), stop=(last and k == 1))
                ins.then_inc(read_summed.sem, 1)

            def slot(n, i, at, behind, ahead):
                g = at // 3
                if at % 3 == 0 and g:
                    c_pair(n, i, g - 1, 1)
                elif at % 3 == 0 and behind:
                    c_pair(n - 1, 1 - i, NG - 1, 1)
                if at % 3 == 1 and g >= 2:
                    add_states(n, g - 2)
                elif at % 3 == 1 and behind:
                    add_states(n - 1, NG - 2 + g)
                if at % 3 == 2:
                    c_pair(n, i, g, 0)

            def last_slots(n, i, at):
                if at == 0:
                    c_pair(n - 1, 1 - i, NG - 1, 1)
                if at in (1, 4):
                    add_states(n - 1, NG - 2 + at // 3)

            def post(b, i):
                def tile(n, *waits):
                    for s, k in waits:
                        wait(pe, s, b, k)
                    wait(pe, p_read[n % 2], b, n // 2)
                    return p_tile(n)

                def norm(k, p_mean, h):
                    mm(tile(p_mean)[:, 0:T], mean_mat[:, :], h, start=True, stop=True).then_inc(p_mm.sem, 1)
                    yield
                    mm(tile(p_mean + 1, (squared, k + 1))[:, 0:T], mean_mat[:, :], square[:, :],
                       start=True, stop=True).then_inc(p_mm.sem, 1)
                    yield

                out_tile = tile(P_OUT, (y_gated_ready, 2))
                for half in range(HALVES):
                    ins = mm(out_tile[:, 0:T], w_out_sb[:, half, :], y_gated[:, half, :], start=(half == 0),
                             stop=(half == 1))
                ins.then_inc(p_mm.sem, 1)
                yield
                wait_p_read(pe, b, P_OUT)
                yield from norm(0, P_MEAN2, h1[:, :])
                yield
                mm(tile(P_GATE, (xn2_ready, 1))[0:1, 0:E], pooled[:, :], gate_w_sb[:, :], start=True, stop=True)\
                    .then_inc(p_mm.sem, 1)
                yield
                yield
                mm(tile(P_WCOL, (gate_step, 5))[:, 0:2], ones_row[:, :], w_pair[:, :], start=True, stop=True)\
                    .then_inc(p_mm.sem, 1)
                yield
                yield
                for j in range(2):
                    w = expert[j]
                    for m in range(H0T):
                        mm(tile(P_UP0[j] + m, (expert_loaded[j], 16))[:, 0:T], w[:, W1_AT + P * m:W1_AT + P * (m + 1)],
                           xn2, start=True, stop=True).then_inc(p_mm.sem, 1)
                    yield
                    down = tile(P_DOWN0[j])
                    for m in range(H0T):
                        wait_p_read(pe, b, P_UP0[j] + m)
                        ins = mm(down[:, 0:T], w[:, W2_AT + P * m:W2_AT + P * (m + 1)], hid0[:, m, :],
                                 start=(m == 0), stop=(m == H0T - 1))
                    ins.then_inc(p_mm.sem, 1)
                    yield
                yield
                wait_p_read(pe, b, P_DOWN0[1])
                yield from norm(1, P_MEAN3, h2[:, :])
                yield
                mm(tile(P_Q, (xn3_ready, 1))[:, 0:TP], qkv_sb[:, 0, :], xn3[:, :], start=True, stop=True)\
                    .then_inc(p_mm.sem, 1)
                mm(tile(P_K)[:, 0:T], qkv_sb[:, 1, :], xn3[:, 0:T], start=True, stop=True).then_inc(p_mm.sem, 1)
                yield
                v = tile(P_V)
                for s in range(3):
                    ins = mm(v[:, P * s:P * (s + 1)], xn3[:, P * s:P * (s + 1)], qkv_sb[:, 2, :],
                             start=True, stop=True)
                ins.then_inc(p_mm.sem, 1)
                wait_p_read(pe, b, P_K)
                mm(tile(P_LOW)[0:1, 0:T], k_sum[:, :], q_t[:, 0:T], start=True, stop=True).then_inc(p_mm.sem, 1)
                yield
                pe.wait_ge(low_step, 4)
                for s in range(3):
                    scores = tile(P_SCORE + s)
                    if s == 0:
                        for q in range(3):
                            mm(scores[:, KEEP_AT + q:KEEP_AT + q + 1], keep_row[0:1, P * q:P * (q + 1)],
                               ones_row[0:1, 0:1], start=True, stop=True)
                    mm(scores[:, 0:T], q_t[:, P * s:P * (s + 1)], k_t[:, :], start=True, stop=True)\
                        .then_inc(p_mm.sem, 1)
                    if s:
                        yield
                yield
                wait(pe, probs_scaled, b, 3)
                for s, (t0, n) in enumerate(TILES):
                    turned = tile(P_PROBS + s)
                    for q in range(3):
                        ins = pe.transpose(turned[0:n, P * q:P * (q + 1)], probs[:, q, t0:t0 + n], ident[:, :])
                    ins.then_inc(p_mm.sem, 1)
                    if s:
                        yield
                attn = tile(P_ATTN)
                for s, (t0, n) in enumerate(TILES):
                    wait_p_read(pe, b, P_PROBS + s)
                    ins = mm(attn[:, 0:T], v_sb[0:n, s, :], probs_t[0:n, s, 0:T], start=(s == 0), stop=(s == 2))
                ins.then_inc(p_mm.sem, 1)
                yield
                wait_p_read(pe, b, P_ATTN)
                yield from norm(2, P_MEAN4, cols(h3_all, b))
                yield
                router = tile(P_ROUTER, (xn4_ready, 1))
                for s in range(3):
                    ins = mm(router[:, E * s:E * (s + 1)], xn4[:, P * s:P * (s + 1)], router_sb[:, :],
                             start=True, stop=True)
                ins.then_inc(p_mm.sem, 1)
                for _ in range(3):
                    yield
                gates = tile(P_GATES, (router_step, 4))
                for s in range(3):
                    ins = pe.transpose(gates[0:E, P * s:P * (s + 1)], r_prob[:, s, :], ident[:, :])
                ins.then_inc(p_mm.sem, 1)

            def begin():
                pass

            all_batches(pe, begin, slot, front, post, last_slots)

            wait(pe, p_read[1], B - 1, NPT // 2)
            wait(pe, xn4_kept, B - 1, 16)
            pe.wait_ge(moe1_loaded, 48)
            pe.wait_ge(gates_split, 1)

            def last_layer(b, i):
                acc = p_bank[:, i, 0:T]

                def down(e):
                    wait(pe, hid1_gated, b, e + 1)
                    for f in range(2):
                        ins = mm(acc, moe1_w2_sb[:, e, f, :], hid1_g[e % 2][:, f, :], start=False,
                                 stop=(e == E - 1 and f == 1))
                    ins.then_inc(down_mm.sem, 1)

                for e in range(E):
                    wait(pe, hid1_ready, b, e - 1)
                    for f in range(2):
                        ins = mm(c_rows[:, 2 * (e % 2) + f, 0:T], moe1_w1_sb[:, e, P * f:P * (f + 1)],
                                 cols(xn4_all, b), start=True, stop=True)
                    ins.then_inc(up_mm.sem, 1)
                    wait(pe, hid1_gated, b, e - 1)
                    mm((y_bank, f_bank)[e % 2][:, 0:T], pick[:, e:e + 1].to_broadcast([96, P]),
                       cols(gates_parts, b), start=True, stop=True).then_inc(gate_rows_mm.sem, 1)
                    if e == 0:
                        wait(pe, out_ready, b - 2, 1)
                        mm(acc, moe1_b2_sb[:, :], cols(gates_e[0:E, :], b), start=True, stop=False)
                    else:
                        down(e - 1)
                down(E - 1)

            per_batch(pe, last_layer)


def kernel(**inputs):
    import numpy as np
    import concourse.bacc as bacc
    from concourse.bass_utils import run_bass_kernel_spmd

    a = {name: np.asarray(v) for name, v in inputs.items()}
    batches, t_in, d_in = a["x"].shape
    tok_w = a["L0_tok_W"].T
    tok_tiles = np.zeros((P, 3, P), np.float32)
    tok_tiles[:, 0], tok_tiles[:, 1], tok_tiles[0:64, 2] = tok_w[0:128], tok_w[128:256], tok_w[256:320]

    def halves(v):
        return v.reshape(2, P, -1).transpose(1, 0, 2).reshape(P, -1)

    vectors = np.concatenate([
        a["L0_tok_b"][:, None], a["L0_tok_gamma"][:, None], a["L0_tok_beta"][:, None],
        a["L0_attn_ln_g"][:, None], a["L0_attn_ln_b"][:, None], halves(a["L0_attn_conv_b"]),
        halves(a["L0_attn_b_dt"]), halves(a["L0_attn_D"]), halves(a["L0_attn_A_log"]),
        a["L1_ffn_b1"].reshape(16, P).T,
    ], axis=1)
    moe0 = np.concatenate([
        a["L0_ffn_w1"],
        a["L0_ffn_w2"].reshape(8, 4, P, P).transpose(0, 2, 1, 3).reshape(8, P, 512),
        a["L0_ffn_b1"].reshape(8, 4, P).transpose(0, 2, 1), a["L0_ffn_b2"][:, :, None],
    ], axis=2)
    arrays = {
        "x_t": a["x"].transpose(2, 0, 1),
        "tok_w": tok_tiles,
        "vec_in": vectors,
        "conv_w": a["L0_attn_conv_w"][:, 0, :].T,
        "w_in": a["L0_attn_W_in"].T,
        "w_x": halves(a["L0_attn_W_x"].T).reshape(P, 2, -1),
        "w_dt": a["L0_attn_W_dt"].T,
        "w_out": halves(a["L0_attn_W_out"].T).reshape(P, 2, -1),
        "gate_w": a["L0_ffn_gate_w"],
        "gate_b": a["L0_ffn_gate_b"][None],
        "moe0": moe0,
        "qkv_w": a["L1_attn_kernel"].transpose(1, 0, 2),
        "router_w": a["L1_ffn_Wg"],
        "moe1_w1": a["L1_ffn_W1"].transpose(1, 0, 2),
        "moe1_w2": a["L1_ffn_W2"].reshape(8, 2, P, P).transpose(2, 0, 1, 3),
        "moe1_b2": a["L1_ffn_b2"],
    }
    arrays = {name: np.ascontiguousarray(v) for name, v in arrays.items()}
    t = t_in - 4
    nc = bacc.Bacc("TRN2", target_bir_lowering=False, num_devices=1)
    aps = {n: nc.dram_tensor(n, v.shape, F32, kind="ExternalInput").ap() for n, v in arrays.items()}
    aps["out"] = nc.dram_tensor("out", (P, batches * t), F32, kind="ExternalOutput").ap()
    aps["gates_dram"] = nc.dram_tensor("gates_dram", (batches, 8, t), F32).ap()
    aps["mask_dram"] = nc.dram_tensor("mask_dram", (batches, 8, t), F32).ap()
    aps["b_dram"] = nc.dram_tensor("b_dram", (2, 16, t), F32).ap()
    audio_tower(nc, **aps)
    got = run_bass_kernel_spmd(nc, [arrays], core_ids=[0]).results[0]["out"]
    return np.ascontiguousarray(got.reshape(P, batches, t).transpose(1, 2, 0))
```

```python
from contextlib import ExitStack

import concourse.bass as bass
from concourse import mybir

F32 = mybir.dt.float32
F32R = mybir.dt.float32r
U32 = mybir.dt.uint32
ALU = mybir.AluOpType
ACT = mybir.ActivationFunctionType
AX_X = mybir.AxisListType.X
LN_EXP = "natural_log_exp_and_others"

P = 128
BANK = 512
EPS = 1e-5

TOK_B, GAMMA, BETA, LN_G, LN_B, CONV_B, B_DT, D_SKIP, A_LOG, MOE1_B1, N_VEC = 0, 1, 2, 3, 4, 5, 7, 9, 11, 43, 59


class Signal:

    def __init__(self, sem, per_batch, head):
        self.sem, self.per_batch, self.head = sem, per_batch, head

    def at(self, b, n):
        return b * self.per_batch + (n + self.head)


def audio_tower(nc, x_t, tok_w, vec_in, conv_w, w_in, w_x, w_dt, w_out, gate_w, gate_b, moe0, qkv_w,
                router_w, moe1_w1, moe1_w2, moe1_b2, out, gates_dram, mask_dram, b_dram):
    B, T_IN = x_t.shape[1:]
    TAPS = 5
    T = T_IN - TAPS + 1
    TP = 3 * P
    TE = T + 1
    TILES = [(0, P), (P, P), (2 * P, T - 2 * P)]
    HALVES = 2
    STATES = 16
    GROUP = 4
    GROUPS = STATES // GROUP
    RANK = 8
    CONV = 4
    E = 8
    H0T = 4
    TOP_TOKENS = max(T * 2 // E, 1)
    TOP_ROUNDS = -(-TOP_TOKENS // 8)
    SCORE_SCALE = 1.0 / 8.0
    BT = B * T
    W1_AT, W2_AT, B1_AT, B2_AT, PACK = 0, 512, 1024, 1028, 1029

    with ExitStack() as ctx:
        def sb(name, shape, dt=F32):
            return ctx.enter_context(nc.sbuf_tensor(name, shape, dt))

        def sem(name):
            return ctx.enter_context(nc.semaphore(name))

        def signal(name, per_batch=1, head=0):
            return Signal(sem(name), per_batch, head)

        psum = ctx.enter_context(nc.psum_tensor("psum", [P, 8, BANK], F32))
        c_rows, y_bank, f_bank = psum[:, 0:2, :], psum[:, 2, :], psum[:, 3, :]
        a_bank, p_bank = psum[:, 4:6, :], psum[:, 6:8, :]

        mean_mat = sb("mean_mat", [P, P])
        ident = sb("ident", [P, P])
        ones_row = sb("ones_row", [1, P])
        pick_raw = sb("pick_raw", [64, STATES])
        pick = sb("pick", [64, STATES])
        pick_gate_raw = sb("pick_gate_raw", [2 * E, E])
        pick_gate = sb("pick_gate", [2 * E, E])
        token_index = sb("token_index", [1, T])
        vecs = sb("vecs", [P, N_VEC])
        neg_a = sb("neg_a", [P, HALVES * STATES])
        eps_col = sb("eps_col", [P, 3])
        w_in_sb = sb("w_in_sb", [P, 512])
        w_conv = sb("w_conv", [P, CONV, 256])
        w_x_sb = sb("w_x_sb", [P, HALVES, RANK + 2 * STATES])
        w_bc = sb("w_bc", [P, HALVES, 64])
        w_dt_sb = sb("w_dt_sb", [RANK, 256])
        w_out_sb = sb("w_out_sb", [P, HALVES, P])
        gate_w_sb = sb("gate_w_sb", [P, E])
        gate_b_sb = sb("gate_b_sb", [1, E])
        qkv_sb = sb("qkv_sb", [P, 3, P])
        router_sb = sb("router_sb", [P, E])
        moe1_b2_sb = sb("moe1_b2_sb", [2 * E, P])

        x_area = sb("x_area", [P, B * T_IN])
        x2 = x_area[:, :].rearrange("p (b t) -> p b t", b=B)
        xn4_all = x_area[:, 0:BT]
        tok_y = sb("tok_y", [P, BT])
        h3_all = tok_y
        bn_parts = sb("bn_parts", [P, B, 6])
        bn = sb("bn", [P, 2])
        tok_rs = sb("tok_rs", [P, 6])

        bc_parts = [sb(f"bc_parts{i}", [64, TE]) for i in range(2)]

        y_gated = sb("y_gated", [P, HALVES, T])
        h1 = sb("h1", [P, T])
        def by_state(area):
            return area.rearrange("p (s t) -> p s t", s=GROUP)

        e_centered = sb("e_centered", [P, T])
        e_square = sb("e_square", [P, T])
        e_rs = sb("e_rs", [P, T])
        spare = sb("spare", [1, 1])
        pooled = sb("pooled", [P, 1])
        gate_row = sb("gate_row", [1, E])
        top_v = sb("top_v", [1, 8])
        top_i = sb("top_i", [1, 8], U32)
        gate_tmp = sb("gate_tmp", [1, 4])
        w_pair = sb("w_pair", [1, 2])
        w_col = sb("w_col", [P, 2])
        expert = [sb(f"expert{j}", [P, PACK]) for j in range(2)]
        b2_mix = sb("b2_mix", [P, 2])
        xn2 = sb("xn2", [P, T])
        h2 = [sb(f"h2_{i}", [P, T]) for i in range(2)]
        hid0 = sb("hid0", [P, H0T, T])

        a_centered = sb("a_centered", [P, T])
        a_square = sb("a_square", [P, T])
        a_rs = sb("a_rs", [P, T])
        xn3 = sb("xn3", [P, TP])
        q_t = sb("q_t", [P, TP])
        k_t = sb("k_t", [P, T])
        k_sum = sb("k_sum", [P, 1])
        v_sb = sb("v_sb", [P, 3, P])
        low_row = a_square[0:1, :]
        low_v = sb("low_v", [1, 8])
        low_i = sb("low_i", [1, 8], U32)
        low_f = sb("low_f", [1, 1])
        keep_row = sb("keep_row", [1, TP])
        keep = sb("keep", [P, 3])
        s_max = sb("s_max", [P, 3])
        s_bias = sb("s_bias", [P, 3])
        s_sum = sb("s_sum", [P, 3])
        s_inv = sb("s_inv", [P, 3])
        s_scale = sb("s_scale", [P, 3])
        probs = sb("probs", [P, 3, T])
        probs_t = sb("probs_t", [P, 3, TP])
        xn4 = sb("xn4", [P, TP])
        r_max = sb("r_max", [P, 3])
        r_cent = sb("r_cent", [P, 3, E])
        r_exp = sb("r_exp", [P, 3, E])
        r_sum = sb("r_sum", [P, 3])
        r_inv = sb("r_inv", [P, 3])
        r_prob = sb("r_prob", [P, 3, E])
        gates_t = sb("gates_t", [E, T])

        hid1_low_own = sb("hid1_low_own", [P, 2 * TE])
        SET = B // 2
        SE = SET * E
        top_8 = sb("top_8", [SE, 8])

        first_phase = ExitStack()

        def first_sb(name, shape):
            return first_phase.enter_context(nc.sbuf_tensor(name, shape, F32))

        front_area = first_sb("front_area", [P, 8 * T + CONV - 1])
        h0, f_centered = front_area[:, 0:T], front_area[:, T:2 * T]
        bc_f32 = front_area[0:32, 3 * T:4 * T]
        dt_low = front_area[0:RANK, 4 * T:5 * T]
        dt_soft = front_area[:, 5 * T:7 * T].rearrange("p (h t) -> p h t", h=HALVES)
        ssm_in = front_area[:, 7 * T:]
        carried = first_sb("carried", [P, 8 * HALVES * T])
        xc, zs, dt, dtu = ([carried[:, at + i * step:at + i * step + HALVES * T]
                            .rearrange("p (h t) -> p h t", h=HALVES) for i in range(2)]
                           for at, step in ((0, 4 * T), (2 * T, 4 * T), (8 * T, 2 * T), (12 * T, 2 * T)))
        f_square, f_rs = dt_soft[:, 0, :], dt_soft[:, 1, :]
        b_area = first_sb("b_area", [P, STATES * T])
        b_rows = b_area[:, :].rearrange("p (s t) -> p s t", s=STATES)
        tok_w_sb = b_area[:, 0:3 * P].rearrange("p (k o) -> p k o", k=3)
        scan_area = first_sb("scan_area", [P, 8, GROUP * T])
        decay, drive, state, read = ([scan_area[:, 2 * k + i, :] for i in range(2)] for k in range(4))
        conv_rows = scan_area[:, 0, 0:CONV * 256].rearrange("p (j d) -> p j d", j=CONV)
        first_phase.close()

        def pieces(area, n, width, at=0):
            return [area[:, at + width * k:at + width * (k + 1)] for k in range(n)]

        def by_f(areas):
            return [a.rearrange("p (f t) -> p f t", f=2) for a in areas]

        top_area = sb("top_area", [SE, 4 * T])
        top_in, *top_work, gates_masked = pieces(top_area, 4, T)
        top_parts = sb("top_parts", [SE, 2 * T])
        top_hi, top_low = pieces(top_parts, 2, T)
        HID = 4
        hid1_low_area = [sb("hid1_low_0", [P, 2 * TE])]
        gates_raw = sb("gates_raw", [2 * E, SET * T])
        gates_hl = [sb(f"gates_hl{k}", [2 * E, SET * T + 1]) for k in range(2)]
        hid1_low_pair = sb("hid1_low_pair", [P, 4 * TE])
        hid1_low_wide = by_f([hid1_low_area[0][:, :], *pieces(hid1_low_pair, 2, 2 * TE), hid1_low_own[:, :]])
        hid1_low = [a[:, :, 0:T] for a in hid1_low_wide]
        weights = sb("weights", [P, 2 * E * 256])
        moe1_w1_sb = weights[:, 0:E * 256].rearrange("p (e f) -> p e f", e=E)
        moe1_w2_sb = weights[:, E * 256:].rearrange("p (e f h) -> p e f h", e=E, f=2)
        hid1 = by_f(pieces(weights, 2, 2 * T))
        hid1_g = by_f(pieces(weights, 2, 2 * T, at=4 * T))
        out_sb = pieces(weights, 2, T, at=8 * T)
        x_parts = sb("x_parts", [P, 4 * TE])
        x_hi_wide, x_low_wide = pieces(x_parts, 2, TE), pieces(x_parts, 2, TE, at=2 * TE)
        x_hi, x_low = [a[:, 0:T] for a in x_hi_wide], [a[:, 0:T] for a in x_low_wide]
        between = (STATES * T * 4 + 16 * T * 4) - (4 * 5952 + 2 * E * 256 * 4 + 5952)
        sb("between", [P, between // 4])
        weights_hi, weights_low = sb("weights_hi", [P, 2 * E * 256]), sb("weights_low", [P, 2 * E * 256])
        hid1_hi_area = sb("hid1_hi_area", [P, 2 * TE * HID])
        hid1_hi_wide = by_f(pieces(hid1_hi_area, HID, 2 * TE))
        hid1_hi = [a[:, :, 0:T] for a in hid1_hi_wide]
        HALF = E * 256

        x_loaded, tokw_loaded, vec_loaded, ssm_loaded, gate_loaded, moe1_loaded = (
            sem(n) for n in ("x_loaded", "tokw_loaded", "vec_loaded", "ssm_loaded", "gate_loaded", "moe1_loaded"))
        ident_step, pick_step, index_step, pads_ready, granted = (
            sem(n) for n in ("ident_step", "pick_step", "index_step", "pads_ready", "granted"))
        tok_mm, tok_relu, bn_part, tok_step, tok_act = (
            sem(n) for n in ("tok_mm", "tok_relu", "bn_part", "tok_step", "tok_act"))
        a_exp, a_ready, weights_made = sem("a_exp"), sem("a_ready"), sem("weights_made")

        F_MEAN, F_VAR, F_XI, F_Z, F_BC, F_DT_LOW, F_DT, NF = 0, 1, 2, 4, 6, 7, 8, 10
        f_mm = signal("f_mm", NF)
        f_read = signal("f_read", NF, head=1)
        h0_ready = signal("h0_ready")
        f_squared = signal("f_squared")
        f_rs_ready = signal("f_rs_ready")
        f_scaled = signal("f_scaled")
        ssm_in_ready = signal("ssm_in_ready")
        bc_hi = signal("bc_hi")
        bc_copied = signal("bc_copied")
        b_stored = signal("b_stored", 16)
        b_loaded = [signal(f"b_loaded{g}", 16) for g in range(GROUPS)]
        dt_abs_ready = signal("dt_abs_ready", 2)
        dt_exp_ready = signal("dt_exp_ready")
        dt_ln_ready = signal("dt_ln_ready")
        dt_ready = signal("dt_ready")
        dtu_ready = signal("dtu_ready")

        NG = HALVES * GROUPS
        decay_ready = signal("decay_ready", NG)
        drive_ready = signal("drive_ready", NG, head=4)
        state_ready = signal("state_ready", NG, head=2)
        c_ready = signal("c_ready", 2 * NG)
        read_ready = signal("read_ready", 2 * NG, head=3)
        read_summed = signal("read_summed", NG, head=2)
        pairs_added = signal("pairs_added", NG)
        y_read = signal("y_read", 2, head=1)
        y_gated_ready = signal("y_gated_ready", 2, head=3)

        A_OUT, A_MEAN, A_VAR, A_GATE, A_WCOL, A_UP, A_DOWN, NA = 0, 1, 2, 3, 4, (5, 10), (9, 14), 15
        a_mm = signal("a_mm", NA)
        a_read = [signal(f"a_read{i}", (NA + 1 - i) // 2, head=1) for i in range(2)]
        a_squared = signal("a_squared")
        a_rs_ready = signal("a_rs_ready")
        h1_begun = signal("h1_begun")
        xn2_ready = signal("xn2_ready")
        gate_step = signal("gate_step", 5)
        gate_exp_ready = signal("gate_exp_ready")
        experts_known = sem("experts_known")
        expert_loaded = [signal(f"expert_loaded{j}", 16) for j in range(2)]
        b2_step = signal("b2_step", 3)

        P_MEAN3, P_VAR3, P_Q, P_K, P_V, P_LOW, P_SCORE = 0, 1, 2, 3, 4, 5, 6
        P_PROBS, P_ATTN, P_MEAN4, P_VAR4, P_ROUTER, P_GATES, NP = 9, 12, 13, 14, 15, 16, 17
        KEEP_AT = 400
        p_mm = signal("p_mm", NP)
        p_read = [signal(f"p_read{i}", (NP + 1 - i) // 2, head=1) for i in range(2)]
        p_squared = signal("p_squared", 2)
        p_rs_ready = signal("p_rs_ready", 2)
        xn3_ready = signal("xn3_ready")
        low_step = sem("low_step")
        keep_ready = signal("keep_ready")
        max_ready = signal("max_ready", 3)
        bias_ready = signal("bias_ready", 3)
        scale_step = signal("scale_step", 2)
        probs_scaled = signal("probs_scaled", 3)
        xn4_ready = signal("xn4_ready")
        router_step = signal("router_step", 4)
        router_exp_ready = signal("router_exp_ready")
        xn4_kept = signal("xn4_kept", 16, head=16)
        gates_kept = signal("gates_kept", 16, head=16)

        gates_loaded, top_step, mask_stored = (sem(n) for n in ("gates_loaded", "top_step", "mask_stored"))
        mask_loaded = [sem(f"mask_loaded{k}") for k in range(2)]
        gates_typed = sem("gates_typed")
        moe1_weights_loaded = sem("moe1_weights_loaded")
        TOP_STEPS = 2 * TOP_ROUNDS + (1 if TOP_TOKENS % 8 else 0) + 3
        up_mm = signal("up_mm", E)
        gate_rows_mm = signal("gate_rows_mm", E)
        hid1_ready = signal("hid1_ready", E, head=2)
        hid1_gated = signal("hid1_gated", E, head=2)
        hid1_rounded = signal("hid1_rounded", E)
        hid1_split = [signal(f"hid1_split{f}", E, head=2) for f in range(2)]
        x_rounded = signal("x_rounded")
        x_split = signal("x_split")
        pads_written = sem("pads_written")
        weights_rounded, weights_split = sem("weights_rounded"), sem("weights_split")
        down_mm = signal("down_mm", E, head=4)
        out_ready = signal("out_ready", 1, head=2)
        out_stored = signal("out_stored", 16, head=16)

        def wait(eng, s, b, n):
            eng.wait_ge(s.sem, s.at(b, n))

        def grant(eng, s):
            eng.sem_inc(s.sem, s.head)

        def late_batches(eng, run):
            with eng.Fori(SET // 2, B // 2) as pair:
                run(pair * 2)

        SLOTS = 3 * NG
        FRONT_AT = (0, 1, 2, 4, 7, 10, 11, 12, 12, 13, 15, 16, 17, 17, 19)
        EXPERTS_AT = (7, 8, 9, 10, 11, 13, 13, 14, 15, 16, 17, 18, 19, 21, 22)
        ATTENTION_AT = (1, 2, 3, 4, 5, 5, 7, 7, 8, 9, 10, 11, 12, 13, 14, 15, 16, 17, 18, 19, 20, 21, 22, 23)

        CHOICE_AT = (6, 6, 9, 10, 10, 11, 13, 13, 15, 16, 17, 18, 19)
        LAST_AT = ((8, 21), (3, 4, 5, 6, 7, 12, 13, 14, 15, 16, 17, 19, 20, 20, 22, 23))

        CHOOSE_FROM = 1

        def turn(n, i, slot, front, experts, attention, scan=True, ahead=True, behind=2, extra=None):
            i_next = 1 - i
            chains = []
            if behind == 2 or not behind and n > B:
                chains.append((ATTENTION_AT, attention(n - 2, i)))
            if behind:
                chains.append((EXPERTS_AT, experts(n - 1, i_next)))
            if ahead:
                chains.append((FRONT_AT, front(n + 1, i_next)))
            if extra:
                chains.append(extra)
            for at in range(SLOTS):
                slot(n, i, at, False, scan, behind > 0, ahead)
                for places, chain in chains:
                    for _ in range(places.count(at)):
                        next(chain, None)
                slot(n, i, at, True, scan, behind > 0, ahead)

        def all_batches(eng, begin, slot, front, experts, attention, choice, last_layer):
            for _ in front(0, 0):
                pass
            begin()
            run = (slot, front, experts, attention)
            turn(0, 0, *run, behind=0)
            turn(1, 1, *run, behind=1)
            with eng.Fori(0, (B - 4) // 2) as pair:
                turn(pair * 2 + 2, 0, *run)
                turn(pair * 2 + 3, 1, *run)
            turn(B - 2, 0, *run)
            turn(B - 1, 1, *run, ahead=False, extra=(CHOICE_AT, choice(0)))
            last = last_layer()
            turn(B, 0, *run, scan=False, ahead=False, extra=(LAST_AT[0], last))
            turn(B + 1, 1, *run, scan=False, ahead=False, behind=0, extra=(LAST_AT[1], last))
            for _ in last:
                pass

        def early_batches(part, prepare=(), after_part=lambda k: None):
            for k in range(2):
                if k < len(prepare):
                    prepare[k]()
                yield
            for b in range(SET):
                for e in range(E):
                    part(b, e)
                    if b >= SET - 2:
                        after_part((b - SET + 2) * E + e)
                    yield

        def cols(area, b):
            return area[:, bass.ds(b * T, T)]

        def vec(k):
            return vecs[:, k:k + 1]

        def a_tile(n):
            return a_bank[:, n % 2, :]

        def p_tile(n):
            return p_bank[:, n % 2, :]

        def early_sum(b):
            return f_bank if b < SET - 2 else p_bank[:, b % 2, :]

        def a_done(eng, b, n):
            wait(eng, a_read[n % 2], b, n // 2 + 1)

        def p_done(eng, b, n):
            wait(eng, p_read[n % 2], b, n // 2 + 1)

        block = ctx.enter_context(nc.Block())

        @block.sync
        def _(sp):
            sp.dma_start(x2[0:64, :, :], x_t).then_inc(x_loaded, 16)
            sp.dma_start(x2[64:P, :, 0:T_IN - 1], x_t[:, :, 1:T_IN]).then_inc(x_loaded, 16)
            sp.dma_start(w_in_sb[:, :], w_in).then_inc(ssm_loaded, 16)
            sp.dma_start(conv_rows, conv_w.partition_broadcast(P)).then_inc(ssm_loaded, 16)
            sp.dma_start(w_x_sb[:, :, :], w_x).then_inc(ssm_loaded, 16)
            sp.dma_start(w_dt_sb[:, :], w_dt).then_inc(ssm_loaded, 16)
            sp.dma_start(w_out_sb[:, :, :], w_out).then_inc(ssm_loaded, 16)
            sp.dma_start(gate_w_sb[:, :], gate_w).then_inc(gate_loaded, 16)
            sp.dma_start(gate_b_sb[:, :], gate_b).then_inc(gate_loaded, 16)
            sp.dma_start(qkv_sb[:, :, :], qkv_w).then_inc(gate_loaded, 16)
            sp.dma_start(router_sb[:, :], router_w).then_inc(gate_loaded, 16)
            for k in range(2):
                sp.dma_start(moe1_b2_sb[E * k:E * (k + 1), :], moe1_b2).then_inc(moe1_loaded, 16)
            grant(sp, xn4_kept)
            grant(sp, gates_kept)
            grant(sp, out_stored)

            def store_b(b, i):
                wait(sp, bc_copied, b, 1)
                sp.dma_start(b_dram[i], bc_f32[16:32, :]).then_inc(b_stored.sem, 16)

            def load_b(b, i):
                wait(sp, b_stored, b, 16)
                for g in range(GROUPS):
                    wait(sp, drive_ready, b - 1, GROUPS + g + 1)
                    sp.dma_start(b_rows[:, GROUP * g:GROUP * (g + 1), :],
                                 b_dram[i, GROUP * g:GROUP * (g + 1), :].partition_broadcast(P))\
                      .then_inc(b_loaded[g].sem, 16)

            def load_experts(b):
                sp.wait_ge(experts_known, 1)
                chosen = [sp.value_load(top_i[0:1, j:j + 1], min_val=0, max_val=E - 1) for j in range(2)]
                sp.sem_clear(experts_known)
                for j, e in enumerate(chosen):
                    sp.dma_start(expert[j][:, :], moe0[bass.ds(e, 1), :, :].rearrange("a p n -> p (a n)"))\
                      .then_inc(expert_loaded[j].sem, 16)

            def keep_rest(b):
                wait(sp, xn4_ready, b, 1)
                sp.dma_start(cols(xn4_all, b), xn4[:, 0:T]).then_inc(xn4_kept.sem, 16)
                p_done(sp, b, P_GATES)
                sp.dma_start(gates_dram[bass.ds(b, 1), :, :].rearrange("a e t -> e (a t)"), gates_t[:, :])\
                  .then_inc(gates_kept.sem, 16)

            def front_loads(n, i):
                store_b(n, i)
                load_b(n, i)

            def whole_turn(n, i):
                load_experts(n - 1)
                front_loads(n + 1, 1 - i)
                keep_rest(n - 2)

            front_loads(0, 0)
            front_loads(1, 1)
            load_experts(0)
            front_loads(2, 0)
            with sp.Fori(0, (B - 4) // 2) as pair:
                whole_turn(pair * 2 + 2, 0)
                whole_turn(pair * 2 + 3, 1)
            whole_turn(B - 2, 0)

            def load_gates(k):
                if k == 0:
                    wait(sp, dt_ready, B - 1, 1)
                wait(sp, gates_kept, SET if k == 0 else B - 1, 16)
                sp.dma_start(top_in, gates_dram[SET * k:SET * (k + 1), :, :].rearrange("b e t -> (b e) t"))\
                  .then_inc(gates_loaded, 16)

            def exchange_gates(k):
                sp.wait_ge(top_step, (k + 1) * TOP_STEPS)
                for part, rows in enumerate((top_hi, top_low)):
                    sp.dma_start(mask_dram[k, part].rearrange("b e t -> (b e) t"), rows).then_inc(mask_stored, 16)
                wait(sp, y_gated_ready, B - 2 + k, 2)
                sp.wait_ge(mask_stored, 32 * (k + 1))
                if k:
                    sp.wait_ge(gates_typed, 1)
                for part in range(2):
                    sp.dma_start(gates_raw[E * part:E * (part + 1), :].rearrange("e (b t) -> e b t", b=SET),
                                 mask_dram[k, part].rearrange("b e t -> e b t")).then_inc(mask_loaded[k], 16)

            def result(b, i):
                wait(sp, out_ready, b, 1)
                sp.dma_start(cols(out, b), out_sb[i]).then_inc(out_stored.sem, 16)

            load_gates(0)
            load_experts(B - 2)
            keep_rest(B - 3)
            wait(sp, state_ready, B - 1, NG)
            sp.dma_start(moe1_w1_sb, moe1_w1).then_inc(moe1_weights_loaded, 16)
            sp.dma_start(moe1_w2_sb, moe1_w2).then_inc(moe1_weights_loaded, 16)
            exchange_gates(0)
            load_experts(B - 1)
            keep_rest(B - 2)
            result(0, 0)
            keep_rest(B - 1)
            load_gates(1)
            result(1, 1)
            result(2, 0)
            exchange_gates(1)
            result(3, 1)
            def both_results(b):
                result(b, 0)
                result(b + 1, 1)

            late_batches(sp, both_results)
            wait(sp, out_stored, B - 1, 16)
            wait(sp, xn4_kept, B - 1, 16)

        @block.gpsimd
        def _(pool):
            pool.memset(ident[:, :], 0.0).then_inc(ident_step, 1)
            pool.wait_ge(ident_step, 1)
            pool.affine_select(out=ident[:, :], in_=ident[:, :], compare_op=ALU.not_equal, fill=1.0, base=0,
                               pattern=[[-1, P]], channel_multiplier=1).then_inc(ident_step, 1)
            pool.memset(mean_mat[:, :], 1.0 / P).then_inc(ident_step, 1)
            pool.memset(pick_raw[:, :], 0.0).then_inc(pick_step, 1)
            for k in range(2):
                pool.wait_ge(pick_step, k + 1)
                pool.affine_select(out=pick_raw[:, :], in_=pick_raw[:, :], compare_op=ALU.not_equal, fill=1.0,
                                   base=-32 * k, pattern=[[-1, STATES]], channel_multiplier=1).then_inc(pick_step, 1)
            pool.memset(pick_gate_raw[:, :], 0.0).then_inc(pick_step, 1)
            for k in range(2):
                pool.wait_ge(pick_step, 4 + k)
                pool.affine_select(out=pick_gate_raw[:, :], in_=pick_gate_raw[:, :], compare_op=ALU.not_equal, fill=1.0,
                                   base=-E * k, pattern=[[-1, E]], channel_multiplier=1).then_inc(pick_step, 1)
            pool.wait_ge(pick_step, 6)
            pool.tensor_copy(pick[:, :].bitcast(F32R), pick_raw[:, :]).then_inc(pick_step, 1)
            pool.tensor_copy(pick_gate[:, :].bitcast(F32R), pick_gate_raw[:, :]).then_inc(pick_step, 1)
            for i in range(2):
                pool.tensor_copy(bc_parts[i][:, T:TE].bitcast(F32R), pick_raw[:, 0:1]).then_inc(pick_step, 1)
            pool.iota(token_index[:, :], pattern=[[1, T]], base=0, channel_multiplier=0,
                      allow_small_or_imprecise_dtypes=True).then_inc(index_step, 1)
            grant(pool, drive_ready)

            def front(b, i):
                for _ in range(len(FRONT_AT) - 1):
                    yield
                wait(pool, f_read, b, F_XI + 2)
                wait(pool, dt_ready, b, 1)
                pool.tensor_tensor(dtu[i][:, :, :], dt[i][:, :, :], xc[i][:, :, :], ALU.mult)\
                    .then_inc(dtu_ready.sem, 1)

            def drive_group(b, i, g):
                half, states = g // GROUPS, g % GROUPS
                if g == 0:
                    wait(pool, dtu_ready, b, 1)
                if half == 0:
                    wait(pool, b_loaded[states], b, 16)
                wait(pool, state_ready, b, g - 1)
                pool.tensor_tensor(by_state(drive[g % 2]),
                                   dtu[i][:, half:half + 1, :].to_broadcast([P, GROUP, T]),
                                   b_rows[:, GROUP * states:GROUP * (states + 1), :], ALU.mult)\
                    .then_inc(drive_ready.sem, 1)

            def add_pairs(b, g):
                wait(pool, read_ready, b, 2 * (g + 1))
                r = by_state(read[g % 2])
                pool.tensor_tensor(r[:, 0:2, :], r[:, 0:2, :], r[:, 2:4, :], ALU.add).then_inc(pairs_added.sem, 1)

            def slot(n, i, at, after, scan, behind, ahead):
                g = at // 3
                if at % 3 == 1 and not after:
                    if scan and g < NG - 1:
                        drive_group(n, i, g + 1)
                    elif ahead and g == NG - 1:
                        drive_group(n + 1, 1 - i, 0)
                if at % 3 == 2 and not after:
                    if scan and g:
                        add_pairs(n, g - 1)
                    elif behind and g == 0:
                        add_pairs(n - 1, NG - 1)

            def round_weights():
                pool.wait_ge(moe1_weights_loaded, 32)
                wait(pool, y_gated_ready, B - 1, 2)
                for area, n in ((hid1_low_area[0], 2), (hid1_low_pair, 4), (hid1_low_own, 2), (x_parts, 4),
                                (hid1_hi_area, 2 * HID)):
                    pads = area[:, :].rearrange("p (k t) -> p k t", k=n)[:, :, T]
                    pool.tensor_copy(pads.bitcast(F32R), ident[:, 0:n]).then_inc(pads_written, 1)
                for k in range(2):
                    pool.tensor_copy(gates_hl[k][:, SET * T:].bitcast(F32R), pick_gate_raw[:, 0:1]).then_inc(pads_written, 1)
                for k in range(2):
                    half = slice(HALF * k, HALF * (k + 1))
                    pool.tensor_copy(weights_hi[:, half].bitcast(F32R), weights[:, half]).then_inc(weights_rounded, 1)

            def split_hidden(b, e):
                wait(pool, hid1_rounded, b, e + 1)
                g, low = hid1_g[e % 2][:, 1, :], hid1_low[e % HID][:, 1, :]
                pool.tensor_tensor(low.bitcast(F32R), g, hid1_hi[e % HID][:, 1, :], ALU.subtract).then_inc(hid1_split[1].sem, 1)

            def nothing(*_):
                yield

            def split_both(b, e):
                wait(pool, hid1_rounded, b, e + 1)
                for f in range(2):
                    g, low = hid1_g[e % 2][:, f, :], hid1_low[e % HID][:, f, :]
                    pool.tensor_tensor(low.bitcast(F32R), g, hid1_hi[e % HID][:, f, :], ALU.subtract).then_inc(hid1_split[f].sem, 1)

            all_batches(pool, lambda: drive_group(0, 0, 0), slot, front, nothing, nothing, nothing,
                        lambda: early_batches(split_both, (round_weights,)))

            def last_layer(b0):
                for k in range(2 * E):
                    split_hidden(b0 + k // E, k % E)

            late_batches(pool, last_layer)

        @block.scalar
        def _(act):
            act.dma_start(tok_w_sb, tok_w).then_inc(tokw_loaded, 16)
            act.dma_start(vecs[:, :], vec_in).then_inc(vec_loaded, 16)
            grant(act, hid1_ready)
            act.preload_act_table_set(LN_EXP)
            act.wait_ge(vec_loaded, 16)
            act.activation(neg_a[:, :], vecs[:, A_LOG:A_LOG + HALVES * STATES], ACT.Exp).then_inc(a_exp, 1)
            for b in range(B):
                act.wait_ge(tok_mm, b + 1)
                act.activation(tok_y[:, b * T:(b + 1) * T], psum[:, b, 0:T], ACT.Relu, bias=vec(TOK_B))\
                   .then_inc(tok_relu, 1)
            act.wait_ge(tok_step, 2)
            act.activation(tok_rs[:, 1:2], tok_rs[:, 0:1], ACT.Ln).then_inc(tok_act, 1)
            act.wait_ge(tok_act, 1)
            act.activation(tok_rs[:, 2:3], tok_rs[:, 1:2], ACT.Exp, scale=-0.5).then_inc(tok_act, 1)

            def front(b, i):
                yield
                yield
                wait(act, f_read, b, F_MEAN + 1)
                act.activation(f_square, f_centered, ACT.Square).then_inc(f_squared.sem, 1)
                yield
                wait(act, f_mm, b, F_VAR + 1)
                act.activation(f_rs, f_bank[:, 0:T], ACT.Ln, scale=1.0 + EPS, bias=eps_col[:, 1:2])\
                   .then_inc(f_read.sem, 1)
                wait(act, f_read, b, F_VAR + 1)
                act.activation(f_rs, f_rs, ACT.Exp, scale=-0.5).then_inc(f_rs_ready.sem, 1)
                yield
                yield
                wait(act, y_gated_ready, b - 2, 2)
                for half in range(HALVES):
                    wait(act, f_mm, b, F_XI + half + 1)
                    act.activation(xc[i][:, half, :], f_bank[:, 0:T], ACT.Silu, bias=vec(CONV_B + half))\
                       .then_inc(f_read.sem, 1)
                    yield
                for half in range(HALVES):
                    wait(act, f_mm, b, F_Z + half + 1)
                    act.activation(zs[i][:, half, :], f_bank[:, 0:T], ACT.Silu).then_inc(f_read.sem, 1)
                    if half == 0:
                        yield
                act.preload_act_table_set(LN_EXP)
                yield
                wait(act, f_mm, b, F_BC + 1)
                act.activation(bc_f32, f_bank[0:32, 0:T], ACT.Copy).then_inc(bc_copied.sem, 1)
                act.activation(bc_parts[i][:, 0:T].bitcast(F32R), f_bank[0:64, 0:T], ACT.Copy).then_inc(bc_hi.sem, 1)
                yield
                wait(act, f_mm, b, F_DT_LOW + 1)
                act.activation(dt_low, f_bank[0:RANK, 0:T], ACT.Copy).then_inc(f_read.sem, 1)
                yield
                for half in range(HALVES):
                    wait(act, f_mm, b, F_DT + half + 1)
                    act.activation(dt_soft[:, half, :], f_bank[:, 0:T], ACT.Abs, bias=vec(B_DT + half))\
                       .then_inc(dt_abs_ready.sem, 1)
                    act.activation(dt[i][:, half, :], f_bank[:, 0:T], ACT.Relu, bias=vec(B_DT + half))\
                       .then_inc(f_read.sem, 1)
                    yield
                wait(act, dt_abs_ready, b, 2)
                act.activation(dt_soft[:, :, :], dt_soft[:, :, :], ACT.Exp, scale=-1.0).then_inc(dt_exp_ready.sem, 1)
                wait(act, dt_exp_ready, b, 1)
                act.activation(dt_soft[:, :, :], dt_soft[:, :, :], ACT.Ln, bias=eps_col[:, 2:3])\
                   .then_inc(dt_ln_ready.sem, 1)
                yield

            def decay_group(b, i, g):
                half = g // GROUPS
                if g == 0:
                    wait(act, dt_ready, b, 1)
                wait(act, state_ready, b, g - 1)
                for k in range(GROUP):
                    at = half * STATES + g % GROUPS * GROUP + k
                    ins = act.activation(by_state(decay[g % 2])[:, k, 1:T], dt[i][:, half, 1:T], ACT.Exp,
                                         scale=neg_a[:, at:at + 1])
                ins.then_inc(decay_ready.sem, 1)

            def slot(n, i, at, after, scan, behind, ahead):
                g = at // 3
                if at % 3 == 1 and not after:
                    if scan and g < NG - 1:
                        decay_group(n, i, g + 1)
                    elif ahead and g == NG - 1:
                        decay_group(n + 1, 1 - i, 0)

            def experts(b, i):
                yield
                yield
                a_done(act, b, A_MEAN)
                act.activation(e_square[:, :], e_centered[:, :], ACT.Square).then_inc(a_squared.sem, 1)
                yield
                wait(act, a_mm, b, A_VAR + 1)
                act.activation(e_rs[:, :], a_tile(A_VAR)[:, 0:T], ACT.Ln, bias=eps_col[:, 0:1]).then_inc(a_read[A_VAR % 2].sem, 1)
                a_done(act, b, A_VAR)
                act.activation(e_rs[:, :], e_rs[:, :], ACT.Exp, scale=-0.5).then_inc(a_rs_ready.sem, 1)
                yield
                yield
                yield
                wait(act, gate_step, b, 2)
                act.activation(gate_tmp[:, 1:2], gate_tmp[:, 0:1], ACT.Exp).then_inc(gate_exp_ready.sem, 1)
                yield
                yield
                yield
                for j in range(2):
                    wait(act, expert_loaded[j], b, 16)
                    if j:
                        wait(act, a_mm, b, A_DOWN[0] + 1)
                    for m in range(H0T):
                        wait(act, a_mm, b, A_UP[j] + m + 1)
                        act.activation(hid0[:, m, :], a_tile(A_UP[j] + m)[:, 0:T], ACT.Gelu,
                                       bias=expert[j][:, B1_AT + m:B1_AT + m + 1]).then_inc(a_read[(A_UP[j] + m) % 2].sem, 1)
                        if m == 1:
                            yield
                    act.preload_act_table_set(LN_EXP)
                    yield
                    if j == 0:
                        yield

            def attention(b, i):
                def norm(k, p_mean):
                    yield
                    p_done(act, b, p_mean)
                    act.activation(a_square[:, :], a_centered[:, :], ACT.Square).then_inc(p_squared.sem, 1)
                    yield
                    wait(act, p_mm, b, p_mean + 2)
                    act.activation(a_rs[:, :], p_tile(p_mean + 1)[:, 0:T], ACT.Ln, bias=eps_col[:, 0:1]).then_inc(p_read[(p_mean + 1) % 2].sem, 1)
                    p_done(act, b, p_mean + 1)
                    act.activation(a_rs[:, :], a_rs[:, :], ACT.Exp, scale=-0.5).then_inc(p_rs_ready.sem, 1)
                    yield

                yield from norm(0, P_MEAN3)
                yield
                wait(act, p_mm, b, P_Q + 1)
                act.activation(q_t[:, :], p_tile(P_Q)[:, 0:TP], ACT.Copy).then_inc(p_read[P_Q % 2].sem, 1)
                yield
                wait(act, p_mm, b, P_K + 1)
                act.activation(k_t[:, :], p_tile(P_K)[:, 0:T], ACT.Identity, accum_out=k_sum[:, :]).then_inc(p_read[P_K % 2].sem, 1)
                yield
                yield
                yield
                yield
                for s in range(3):
                    wait(act, bias_ready, b, s + 1)
                    act.activation(probs[:, s, :], p_tile(P_SCORE + s)[:, 0:T], ACT.Exp, scale=SCORE_SCALE,
                                   bias=s_bias[:, s:s + 1], accum_out=s_sum[:, s:s + 1]).then_inc(p_read[(P_SCORE + s) % 2].sem, 1)
                    yield
                yield
                for s, (t0, n) in enumerate(TILES):
                    wait(act, p_mm, b, P_PROBS + s + 1)
                    act.activation(probs_t[0:n, s, :], p_tile(P_PROBS + s)[0:n, 0:TP], ACT.Copy).then_inc(p_read[(P_PROBS + s) % 2].sem, 1)
                    yield
                yield
                yield from norm(1, P_MEAN4)
                yield
                yield
                p_done(act, b, P_ROUTER)
                act.activation(r_exp[:, :, :], r_cent[:, :, :], ACT.Exp).then_inc(router_exp_ready.sem, 1)
                yield
                wait(act, gates_kept, b - 1, 16)
                wait(act, p_mm, b, P_GATES + 1)
                act.activation(gates_t[:, :], p_tile(P_GATES)[0:E, 0:T], ACT.Copy).then_inc(p_read[P_GATES % 2].sem, 1)

            def type_gates(k):
                wait(act, y_gated_ready, B - 1, 2)
                act.wait_ge(mask_loaded[k], 32)
                act.activation(gates_hl[k][:, 0:SET * T].bitcast(F32R), gates_raw[:, :], ACT.Copy).then_inc(gates_typed, 1)

            def round_x(b, i):
                act.activation(x_hi[i].bitcast(F32R), cols(xn4_all, b), ACT.Copy).then_inc(x_rounded.sem, 1)

            def gelu(b, e, banks):
                wait(act, up_mm, b, e + 1)
                wait(act, hid1_gated, b, e - 1)
                for f in range(2):
                    k = MOE1_B1 + 2 * e + f
                    ins = act.activation(hid1[e % 2][:, f, :], banks[:, f, 0:T], ACT.Gelu, bias=vec(k))
                ins.then_inc(hid1_ready.sem, 1)

            def round_hidden(b, e):
                wait(act, hid1_gated, b, e + 1)
                act.activation(hid1_hi[e % HID].bitcast(F32R), hid1_g[e % 2], ACT.Copy)\
                   .then_inc(hid1_rounded.sem, 1)

            def early_part(b, e):
                if e == 0:
                    if b == 0:
                        wait(act, y_gated_ready, B - 1, 2)
                    round_x(b, b % 2)
                gelu(b, e, (c_rows, a_bank)[e % 2])
                if e:
                    round_hidden(b, e - 1)
                elif b:
                    round_hidden(b - 1, E - 1)

            def nothing(*_):
                yield

            all_batches(act, lambda: decay_group(0, 0, 0), slot, front, experts, attention, nothing,
                        lambda: early_batches(early_part, (lambda: type_gates(0),)))
            round_hidden(SET - 1, E - 1)
            wait(act, xn4_kept, B - 1, 16)
            type_gates(1)

            def last_layer(b0):
                round_x(b0, 0)
                for k in range(2 * E):
                    b, e = b0 + k // E, k % E
                    gelu(b, e, (c_rows, a_bank)[e % 2])
                    if k:
                        round_hidden(b0 + (k - 1) // E, (k - 1) % E)
                    if k == E - 3:
                        round_x(b0 + 1, 1)
                round_hidden(b0 + 1, E - 1)

            late_batches(act, last_layer)

        @block.vector
        def _(dve):
            dve.memset(ssm_in[:, 0:CONV - 1], 0.0)
            dve.memset(eps_col[:, 0:1], EPS)
            dve.memset(eps_col[:, 1:2], EPS * EPS)
            dve.memset(eps_col[:, 2:3], 1.0)
            dve.memset(w_bc[:, :, :], 0.0).then_inc(weights_made, 1)
            dve.memset(xn3[:, T:TP], 0.0)
            dve.memset(xn4[:, T:TP], 0.0)
            dve.memset(keep_row[:, :], 1.0)
            dve.memset(ones_row[:, :], 1.0).then_inc(pads_ready, 1)
            for s in (state_ready, read_ready, y_read, y_gated_ready, hid1_gated, hid1_split[0], hid1_split[1], out_ready):
                grant(dve, s)

            dve.wait_ge(ssm_loaded, 80)
            dve.tensor_tensor(w_conv[:, :, :], conv_rows,
                              w_in_sb[:, 0:256].unsqueeze(1).to_broadcast([P, CONV, 256]), ALU.mult)\
               .then_inc(weights_made, 1)
            dve.wait_ge(weights_made, 2)
            for k in range(2):
                dve.tensor_copy(w_bc[:, :, 32 * k:32 * k + STATES], w_x_sb[:, :, RANK + STATES:])
            dve.tensor_copy(w_bc[:, :, STATES:2 * STATES], w_x_sb[:, :, RANK:RANK + STATES]).then_inc(weights_made, 1)
            for i in range(2):
                ins = dve.memset(by_state(decay[i])[:, :, 0:1], 0.0)
            ins.then_inc(weights_made, 1)
            dve.wait_ge(weights_made, 4)
            dve.wait_ge(a_exp, 1)
            dve.tensor_scalar(neg_a[:, :], neg_a[:, :], -1.0, None, ALU.mult).then_inc(a_ready, 1)

            for b in range(B):
                dve.wait_ge(tok_relu, b + 1)
                dve.bn_stats(bn_parts[:, b, :], tok_y[:, b * T:(b + 1) * T]).then_inc(bn_part, 1)
            dve.wait_ge(bn_part, B)
            dve.bn_aggr(bn[:, :], bn_parts[:, :, :]).then_inc(tok_step, 1)
            dve.wait_ge(tok_step, 1)
            dve.tensor_scalar(tok_rs[:, 0:1], bn[:, 1:2], EPS, None, ALU.add).then_inc(tok_step, 1)
            dve.wait_ge(tok_act, 2)
            dve.tensor_tensor(tok_rs[:, 3:4], tok_rs[:, 2:3], vec(GAMMA), ALU.mult).then_inc(tok_step, 1)
            dve.wait_ge(tok_step, 3)
            dve.tensor_tensor(tok_rs[:, 4:5], tok_rs[:, 3:4], bn[:, 0:1], ALU.mult).then_inc(tok_step, 1)
            dve.wait_ge(tok_step, 4)
            dve.tensor_tensor(tok_rs[:, 5:6], vec(BETA), tok_rs[:, 4:5], ALU.subtract).then_inc(tok_step, 1)
            dve.wait_ge(tok_step, 5)

            def front(b, i):
                dve.tensor_scalar(h0, cols(tok_y, b), tok_rs[:, 3:4], tok_rs[:, 5:6], ALU.mult, ALU.add)\
                   .then_inc(h0_ready.sem, 1)
                yield
                wait(dve, h0_ready, b, 1)
                wait(dve, f_mm, b, F_MEAN + 1)
                dve.tensor_tensor(f_centered, h0, f_bank[:, 0:T], ALU.subtract)\
                   .then_inc(f_read.sem, 1)
                yield
                yield
                yield
                wait(dve, f_rs_ready, b, 1)
                dve.scalar_tensor_tensor(f_centered, f_centered, vec(LN_G), f_rs,
                                         ALU.mult, ALU.mult).then_inc(f_scaled.sem, 1)
                wait(dve, f_scaled, b, 1)
                dve.tensor_scalar(ssm_in[:, CONV - 1:], f_centered, vec(LN_B), None, ALU.add)\
                   .then_inc(ssm_in_ready.sem, 1)
                for _ in range(5):
                    yield
                wait(dve, bc_hi, b, 1)
                dve.tensor_tensor(bc_parts[i][32:64, 0:T].bitcast(F32R), f_bank[32:64, 0:T], bc_parts[i][32:64, 0:T], ALU.subtract)\
                   .then_inc(f_read.sem, 1)
                yield
                yield
                yield
                yield
                yield
                wait(dve, f_read, b, F_DT + 2)
                wait(dve, dt_ln_ready, b, 1)
                dve.tensor_tensor(dt[i][:, :, :], dt[i][:, :, :], dt_soft[:, :, :], ALU.add)\
                   .then_inc(dt_ready.sem, 1)

            def times_c(b, g, k):
                wait(dve, c_ready, b, 2 * g + k + 1)
                wait(dve, state_ready, b, g + 1)
                wait(dve, read_summed, b, g - 1)
                dve.tensor_tensor(by_state(read[g % 2])[:, 2 * k:2 * k + 2, :],
                                  by_state(state[g % 2])[:, 2 * k:2 * k + 2, :],
                                  c_rows[:, :, 0:T], ALU.mult).then_inc(read_ready.sem, 1)

            def gate(b, i, half):
                wait(dve, read_summed, b, GROUPS * (half + 1))
                dve.scalar_tensor_tensor(y_gated[:, half, :], xc[i][:, half, :], vec(D_SKIP + half),
                                         y_bank[:, 0:T], ALU.mult, ALU.add).then_inc(y_read.sem, 1)
                wait(dve, y_read, b, half + 1)
                dve.tensor_tensor(y_gated[:, half, :], y_gated[:, half, :], zs[i][:, half, :], ALU.mult)\
                   .then_inc(y_gated_ready.sem, 1)

            def slot(n, i, at, after, scan, behind, ahead):
                g = at // 3
                if at % 3 == 0 and scan and not after:
                    wait(dve, decay_ready, n, g + 1)
                    wait(dve, drive_ready, n, g + 1)
                    wait(dve, read_ready, n, 2 * (g - 1))
                    dve.tensor_tensor_scan(state[g % 2], decay[g % 2], drive[g % 2], 0.0, ALU.mult, ALU.add)\
                       .then_inc(state_ready.sem, 1)
                if at % 3 and not after:
                    if scan and g:
                        times_c(n, g - 1, at % 3 - 1)
                    elif behind and g == 0:
                        times_c(n - 1, NG - 1, at % 3 - 1)
                if scan and after and at == 3 * (GROUPS + 2):
                    gate(n, i, 0)
                if behind and after and at == 6:
                    gate(n - 1, 1 - i, 1)

            def experts(b, i):
                dve.tensor_scalar(h1[:, :], cols(tok_y, b), tok_rs[:, 3:4], tok_rs[:, 5:6], ALU.mult, ALU.add)\
                   .then_inc(h1_begun.sem, 1)
                wait(dve, h1_begun, b, 1)
                wait(dve, a_mm, b, A_OUT + 1)
                dve.tensor_tensor(h1[:, :], h1[:, :], a_tile(A_OUT)[:, 0:T], ALU.add).then_inc(a_read[A_OUT % 2].sem, 1)
                yield
                a_done(dve, b, A_OUT)
                wait(dve, a_mm, b, A_MEAN + 1)
                dve.tensor_tensor(e_centered[:, :], h1[:, :], a_tile(A_MEAN)[:, 0:T], ALU.subtract).then_inc(a_read[A_MEAN % 2].sem, 1)
                for _ in range(3):
                    yield
                wait(dve, a_rs_ready, b, 1)
                dve.scalar_tensor_tensor(xn2[:, :], e_centered[:, :], 1.0, e_rs[:, :], ALU.mult, ALU.mult,
                                         accum_out=pooled[:, :]).then_inc(xn2_ready.sem, 1)
                yield
                wait(dve, a_mm, b, A_GATE + 1)
                dve.scalar_tensor_tensor(gate_row[:, :], a_tile(A_GATE)[0:1, 0:E], 1.0 / T, gate_b_sb[:, :],
                                         ALU.mult, ALU.add).then_inc(a_read[A_GATE % 2].sem, 1)
                a_done(dve, b, A_GATE)
                dve.memset(spare[:, :], 0.0)
                dve.max(top_v[:, :], gate_row[:, :]).then_inc(gate_step.sem, 1)
                wait(dve, gate_step, b, 1)
                dve.memset(spare[:, :], 0.0)
                dve.max_index(top_i[:, :], top_v[:, :], gate_row[:, :]).then_inc(experts_known, 1)
                dve.tensor_tensor(gate_tmp[:, 0:1], top_v[:, 1:2], top_v[:, 0:1], ALU.subtract)\
                   .then_inc(gate_step.sem, 1)
                yield
                wait(dve, gate_exp_ready, b, 1)
                dve.tensor_scalar(gate_tmp[:, 2:3], gate_tmp[:, 1:2], 1.0, None, ALU.add).then_inc(gate_step.sem, 1)
                wait(dve, gate_step, b, 3)
                dve.reciprocal(w_pair[:, 0:1], gate_tmp[:, 2:3]).then_inc(gate_step.sem, 1)
                wait(dve, gate_step, b, 4)
                dve.tensor_tensor(w_pair[:, 1:2], gate_tmp[:, 1:2], w_pair[:, 0:1], ALU.mult)\
                   .then_inc(gate_step.sem, 1)
                yield
                wait(dve, a_mm, b, A_WCOL + 1)
                dve.tensor_copy(w_col[:, :], a_tile(A_WCOL)[:, 0:2]).then_inc(a_read[A_WCOL % 2].sem, 1)
                yield
                yield
                a_done(dve, b, A_WCOL)
                for j in range(2):
                    wait(dve, expert_loaded[j], b, 16)
                dve.tensor_tensor(b2_mix[:, 0:1], expert[1][:, B2_AT:B2_AT + 1], w_col[:, 1:2], ALU.mult)\
                   .then_inc(b2_step.sem, 1)
                wait(dve, b2_step, b, 1)
                dve.scalar_tensor_tensor(b2_mix[:, 1:2], expert[0][:, B2_AT:B2_AT + 1], w_col[:, 0:1],
                                         b2_mix[:, 0:1], ALU.mult, ALU.add).then_inc(b2_step.sem, 1)
                wait(dve, b2_step, b, 2)
                dve.tensor_scalar(h2[i][:, :], h1[:, :], b2_mix[:, 1:2], None, ALU.add)\
                   .then_inc(b2_step.sem, 1)
                yield
                for j in range(2):
                    yield
                    wait(dve, a_mm, b, A_DOWN[j] + 1)
                    if j:
                        a_done(dve, b, A_DOWN[0])
                    else:
                        wait(dve, b2_step, b, 3)
                    dve.scalar_tensor_tensor(h2[i][:, :], a_tile(A_DOWN[j])[:, 0:T], w_col[:, j:j + 1], h2[i][:, :],
                                             ALU.mult, ALU.add).then_inc(a_read[A_DOWN[j] % 2].sem, 1)
                    if j == 0:
                        yield
                        yield

            def attention(b, i):
                a_done(dve, b, NA - 1)
                wait(dve, p_mm, b, P_MEAN3 + 1)
                dve.tensor_tensor(a_centered[:, :], h2[i][:, :], p_tile(P_MEAN3)[:, 0:T], ALU.subtract).then_inc(p_read[P_MEAN3 % 2].sem, 1)
                yield
                yield
                yield
                wait(dve, p_rs_ready, b, 1)
                dve.tensor_tensor(xn3[:, 0:T], a_centered[:, :], a_rs[:, :], ALU.mult).then_inc(xn3_ready.sem, 1)
                yield
                yield
                yield
                wait(dve, p_mm, b, P_V + 1)
                dve.tensor_copy(v_sb[:, :, :], p_tile(P_V)[:, 0:TP].rearrange("p (s o) -> p s o", s=3))\
                   .then_inc(p_read[P_V % 2].sem, 1)
                yield
                wait(dve, p_mm, b, P_LOW + 1)
                dve.tensor_scalar(low_row, p_tile(P_LOW)[0:1, 0:T], -1.0, None, ALU.mult).then_inc(p_read[P_LOW % 2].sem, 1)
                if i == 0 and not isinstance(b, int):
                    with dve.If_eq(dve.to_reg(b), 0):
                        p_done(dve, b, P_LOW)
                        dve.memset(spare[:, :], 0.0)
                        dve.max(low_v[:, :], low_row).then_inc(low_step, 1)
                        dve.wait_ge(low_step, 1)
                        dve.max_index(low_i[:, :], low_v[:, :], low_row).then_inc(low_step, 1)
                        dve.wait_ge(low_step, 2)
                        dve.tensor_copy(low_f[:, :], low_i[:, 0:1]).then_inc(low_step, 1)
                        dve.wait_ge(low_step, 3)
                        dve.wait_ge(index_step, 1)
                        dve.tensor_scalar(keep_row[:, 0:T], token_index[:, :], low_f[:, :], None, ALU.not_equal)\
                           .then_inc(low_step, 1)
                yield
                for s in range(3):
                    wait(dve, p_mm, b, P_SCORE + s + 1)
                    if s == 0:
                        dve.tensor_copy(keep[:, :], p_tile(P_SCORE)[:, KEEP_AT:KEEP_AT + 3]).then_inc(keep_ready.sem, 1)
                    dve.reduce_max(s_max[:, s:s + 1], p_tile(P_SCORE + s)[:, 0:T], AX_X).then_inc(max_ready.sem, 1)
                    wait(dve, max_ready, b, s + 1)
                    dve.tensor_scalar(s_bias[:, s:s + 1], s_max[:, s:s + 1], -SCORE_SCALE, None, ALU.mult)\
                       .then_inc(bias_ready.sem, 1)
                    yield
                yield
                p_done(dve, b, P_SCORE + 2)
                dve.reciprocal(s_inv[:, :], s_sum[:, :]).then_inc(scale_step.sem, 1)
                wait(dve, scale_step, b, 1)
                wait(dve, keep_ready, b, 1)
                dve.tensor_tensor(s_scale[:, :], s_inv[:, :], keep[:, :], ALU.mult).then_inc(scale_step.sem, 1)
                wait(dve, scale_step, b, 2)
                for s in range(3):
                    dve.tensor_scalar(probs[:, s, :], probs[:, s, :], s_scale[:, s:s + 1], None, ALU.mult)\
                       .then_inc(probs_scaled.sem, 1)
                for _ in range(4):
                    yield
                wait(dve, p_mm, b, P_ATTN + 1)
                dve.tensor_tensor(cols(h3_all, b), h2[i][:, :], p_tile(P_ATTN)[:, 0:T], ALU.add).then_inc(p_read[P_ATTN % 2].sem, 1)
                yield
                p_done(dve, b, P_ATTN)
                wait(dve, p_mm, b, P_MEAN4 + 1)
                dve.tensor_tensor(a_centered[:, :], cols(h3_all, b), p_tile(P_MEAN4)[:, 0:T], ALU.subtract)\
                   .then_inc(p_read[P_MEAN4 % 2].sem, 1)
                yield
                yield
                yield
                wait(dve, p_rs_ready, b, 2)
                wait(dve, xn4_kept, b - 1, 16)
                dve.tensor_tensor(xn4[:, 0:T], a_centered[:, :], a_rs[:, :], ALU.mult).then_inc(xn4_ready.sem, 1)
                yield
                logits = p_tile(P_ROUTER)[:, 0:3 * E].rearrange("p (s e) -> p s e", s=3)
                wait(dve, p_mm, b, P_ROUTER + 1)
                dve.reduce_max(r_max[:, :], logits, AX_X).then_inc(router_step.sem, 1)
                wait(dve, router_step, b, 1)
                dve.tensor_tensor(r_cent[:, :, :], logits, r_max[:, :].unsqueeze(2).to_broadcast([P, 3, E]),
                                  ALU.subtract).then_inc(p_read[P_ROUTER % 2].sem, 1)
                yield
                wait(dve, router_exp_ready, b, 1)
                dve.reduce_sum(r_sum[:, :], r_exp[:, :, :], AX_X).then_inc(router_step.sem, 1)
                wait(dve, router_step, b, 2)
                dve.reciprocal(r_inv[:, :], r_sum[:, :]).then_inc(router_step.sem, 1)
                wait(dve, router_step, b, 3)
                dve.tensor_tensor(r_prob[:, :, :], r_exp[:, :, :],
                                  r_inv[:, :].unsqueeze(2).to_broadcast([P, 3, E]), ALU.mult)\
                   .then_inc(router_step.sem, 1)
                yield

            def choice(k):
                base = k * TOP_STEPS
                dve.wait_ge(gates_loaded, 16 * (k + 1))
                now = top_in
                for r in range(TOP_ROUNDS):
                    last = r == TOP_ROUNDS - 1 and TOP_TOKENS % 8
                    if k and not r:
                        dve.wait_ge(mask_stored, 32)
                    dve.max(top_8[:, :], now).then_inc(top_step, 1)
                    dve.wait_ge(top_step, base + 2 * r + 1)
                    if last:
                        dve.memset(top_8[:, TOP_TOKENS % 8:], -1.0).then_inc(top_step, 1)
                        dve.wait_ge(top_step, base + 2 * r + 2)
                    then = top_work[r % 2]
                    dve.match_replace(then, top_8[:, :], now, -1.0).then_inc(top_step, 1)
                    now = then
                    dve.wait_ge(top_step, base + 2 * r + (3 if last else 2))
                    yield
                dve.scalar_tensor_tensor(gates_masked, now, 0.0, top_in, ALU.is_lt, ALU.mult).then_inc(top_step, 1)
                dve.wait_ge(top_step, base + TOP_STEPS - 2)
                dve.tensor_copy(top_hi.bitcast(F32R), gates_masked).then_inc(top_step, 1)
                dve.wait_ge(top_step, base + TOP_STEPS - 1)
                dve.tensor_tensor(top_low.bitcast(F32R), gates_masked, top_hi, ALU.subtract).then_inc(top_step, 1)
                yield

            def gate_hidden(b, e, gate_rows):
                wait(dve, hid1_ready, b, e + 1)
                wait(dve, gate_rows_mm, b, e + 1)
                wait(dve, down_mm, b, e + 1 - HID)
                for f in range(2):
                    wait(dve, hid1_split[f], b, e - 1)
                dve.tensor_tensor(hid1_g[e % 2], hid1[e % 2],
                                  gate_rows[:, 0:T].unsqueeze(1).to_broadcast([P, 2, T]), ALU.mult)\
                   .then_inc(hid1_gated.sem, 1)

            def finish(b, i, acc):
                wait(dve, down_mm, b, E)
                wait(dve, out_stored, b - 1, 16)
                dve.tensor_tensor(out_sb[i], cols(h3_all, b), acc[:, 0:T], ALU.add).then_inc(out_ready.sem, 1)

            def split_hidden(b, e):
                wait(dve, hid1_rounded, b, e + 1)
                g, low = hid1_g[e % 2][:, 0, :], hid1_low[e % HID][:, 0, :]
                dve.tensor_tensor(low.bitcast(F32R), g, hid1_hi[e % HID][:, 0, :], ALU.subtract).then_inc(hid1_split[0].sem, 1)

            def split_x(b, i):
                wait(dve, x_rounded, b, 1)
                dve.tensor_tensor(x_low[i].bitcast(F32R), cols(xn4_all, b), x_hi[i], ALU.subtract).then_inc(x_split.sem, 1)

            def early_part(b, e):
                if e == 0:
                    split_x(b, b % 2)
                if e == 3 and b:
                    finish(b - 1, (b - 1) % 2, early_sum(b - 1))
                gate_hidden(b, e, y_bank)

            def split_weights():
                for k in range(2):
                    half = slice(HALF * k, HALF * (k + 1))
                    dve.wait_ge(weights_rounded, k + 1)
                    dve.tensor_tensor(weights_low[:, half].bitcast(F32R), weights[:, half], weights_hi[:, half],
                                      ALU.subtract).then_inc(weights_split, 1)

            second_choice = choice(1)

            def choose_on(k):
                if k >= CHOOSE_FROM:
                    for _ in range(1 if k < 2 * E - 1 else TOP_ROUNDS):
                        next(second_choice, None)

            all_batches(dve, lambda: None, slot, front, experts, attention, choice,
                        lambda: early_batches(early_part, (lambda: None, split_weights), choose_on))
            finish(SET - 1, 1, early_sum(SET - 1))
            wait(dve, xn4_kept, B - 1, 16)

            def last_layer(b0):
                split_x(b0, 0)
                for k in range(2 * E):
                    b, e = b0 + k // E, k % E
                    gate_hidden(b, e, (y_bank, f_bank)[e % 2])
                    if k:
                        split_hidden(b0 + (k - 1) // E, (k - 1) % E)
                    if k == E - 3:
                        split_x(b0 + 1, 1)
                    if k == E + 3:
                        finish(b0, 0, p_bank[:, 0, :])
                split_hidden(b0 + 1, E - 1)
                finish(b0 + 1, 1, p_bank[:, 1, :])

            late_batches(dve, last_layer)

        @block.tensor
        def _(pe):
            mm = nc.tensor.matmul
            for s in (read_summed, down_mm, f_read, *a_read, *p_read):
                grant(pe, s)
            pe.wait_ge(x_loaded, 32)
            pe.wait_ge(tokw_loaded, 16)
            for b in range(B):
                y = psum[:, b, 0:T]
                mm(y, tok_w_sb[:, 0, :], x2[:, b, 0:T], start=True, stop=False)
                mm(y, tok_w_sb[:, 1, :], x2[:, b, 2:2 + T], start=False, stop=False)
                mm(y, tok_w_sb[0:64, 2, :], x2[0:64, b, 4:4 + T], start=False, stop=True).then_inc(tok_mm, 1)
            pe.wait_ge(tok_relu, B)
            pe.wait_ge(ident_step, 3)
            pe.wait_ge(pick_step, 10)
            pe.wait_ge(weights_made, 3)
            pe.wait_ge(gate_loaded, 64)
            pe.wait_ge(pads_ready, 1)

            def front(b, i):
                f = f_bank[:, 0:T]

                def tile(n, *waits):
                    for s, k in waits:
                        wait(pe, s, b, k)
                    wait(pe, f_read, b, n)

                yield
                tile(F_MEAN, (h0_ready, 1))
                mm(f, mean_mat[:, :], h0, start=True, stop=True).then_inc(f_mm.sem, 1)
                yield
                yield
                tile(F_VAR, (f_squared, 1))
                mm(f, mean_mat[:, :], f_square, start=True, stop=True).then_inc(f_mm.sem, 1)
                yield
                yield
                for half in range(HALVES):
                    tile(F_XI + half, (ssm_in_ready, 1))
                    for j in range(CONV):
                        ins = mm(f, w_conv[:, j, P * half:P * (half + 1)], ssm_in[:, j:j + T],
                                 start=(j == 0), stop=(j == CONV - 1))
                    ins.then_inc(f_mm.sem, 1)
                    yield
                for half in range(HALVES):
                    tile(F_Z + half)
                    mm(f, w_in_sb[:, 256 + P * half:256 + P * (half + 1)], ssm_in[:, CONV - 1:],
                       start=True, stop=True).then_inc(f_mm.sem, 1)
                    yield
                tile(F_BC)
                for half in range(HALVES):
                    ins = mm(f_bank[0:64, 0:T], w_bc[:, half, :], xc[i][:, half, :], start=(half == 0),
                             stop=(half == 1))
                ins.then_inc(f_mm.sem, 1)
                yield
                tile(F_DT_LOW)
                for half in range(HALVES):
                    ins = mm(f_bank[0:RANK, 0:T], w_x_sb[:, half, 0:RANK], xc[i][:, half, :], start=(half == 0),
                             stop=(half == 1))
                ins.then_inc(f_mm.sem, 1)
                yield
                for half in range(HALVES):
                    tile(F_DT + half)
                    mm(f, w_dt_sb[:, P * half:P * (half + 1)], dt_low, start=True, stop=True)\
                        .then_inc(f_mm.sem, 1)
                    yield
                yield

            def c_pair(b, i, g, k):
                if g == 0 and k == 0:
                    wait(pe, f_read, b, F_BC + 1)
                wait(pe, read_ready, b, 2 * g + k)
                for m in range(2):
                    s = g % GROUPS * GROUP + 2 * k + m
                    ins = mm(c_rows[:, m, 0:TE], pick[:, s:s + 1].to_broadcast([64, P]).bitcast(F32R),
                             bc_parts[i][:, :].bitcast(F32R), start=True, stop=True)
                ins.then_inc(c_ready.sem, 1)

            def add_states(b, g):
                half, first, last = g // GROUPS, g % GROUPS == 0, g % GROUPS == GROUPS - 1
                if first:
                    wait(pe, y_read, b, half)
                wait(pe, pairs_added, b, g + 1)
                for k in range(2):
                    ins = mm(y_bank[:, 0:T], ident[:, :], by_state(read[g % 2])[:, k, :],
                             start=(first and k == 0), stop=(last and k == 1))
                ins.then_inc(read_summed.sem, 1)

            def slot(n, i, at, after, scan, behind, ahead):
                g = at // 3
                if at % 3 == 0 and after:
                    if scan and g:
                        c_pair(n, i, g - 1, 0)
                    elif behind and g == 0:
                        c_pair(n - 1, 1 - i, NG - 1, 0)
                if at % 3 == 2 and not after:
                    if scan and g >= 2:
                        add_states(n, g - 2)
                    elif behind and g < 2:
                        add_states(n - 1, NG - 2 + g)
                if at % 3 == 1 and after:
                    if scan and g:
                        c_pair(n, i, g - 1, 1)
                    elif behind and g == 0:
                        c_pair(n - 1, 1 - i, NG - 1, 1)

            def experts(b, i):
                def tile(n, *waits):
                    for s, k in waits:
                        wait(pe, s, b, k)
                    wait(pe, a_read[n % 2], b, n // 2)
                    return a_tile(n)

                place = tile(A_OUT, (y_gated_ready, 2))
                for half in range(HALVES):
                    ins = mm(place[:, 0:T], w_out_sb[:, half, :], y_gated[:, half, :], start=(half == 0),
                             stop=(half == 1))
                ins.then_inc(a_mm.sem, 1)
                yield
                a_done(pe, b, A_OUT)
                place = tile(A_MEAN)
                mm(place[:, 0:T], mean_mat[:, :], h1[:, :], start=True, stop=True).then_inc(a_mm.sem, 1)
                yield
                yield
                place = tile(A_VAR, (a_squared, 1))
                mm(place[:, 0:T], mean_mat[:, :], e_square[:, :], start=True, stop=True).then_inc(a_mm.sem, 1)
                yield
                yield
                place = tile(A_GATE, (xn2_ready, 1))
                mm(place[0:1, 0:E], pooled[:, :], gate_w_sb[:, :], start=True, stop=True).then_inc(a_mm.sem, 1)
                yield
                yield
                place = tile(A_WCOL, (gate_step, 5))
                mm(place[:, 0:2], ones_row[:, :], w_pair[:, :], start=True, stop=True).then_inc(a_mm.sem, 1)
                yield
                yield
                for j in range(2):
                    w = expert[j]
                    wait(pe, expert_loaded[j], b, 16)
                    for m in range(H0T):
                        place = tile(A_UP[j] + m)
                        mm(place[:, 0:T], w[:, W1_AT + P * m:W1_AT + P * (m + 1)], xn2[:, :],
                           start=True, stop=True).then_inc(a_mm.sem, 1)
                        if m == 1:
                            yield
                    yield
                    a_done(pe, b, A_UP[j] + H0T - 1)
                    place = tile(A_DOWN[j])
                    for m in range(H0T):
                        ins = mm(place[:, 0:T], w[:, W2_AT + P * m:W2_AT + P * (m + 1)], hid0[:, m, :],
                                 start=(m == 0), stop=(m == H0T - 1))
                    ins.then_inc(a_mm.sem, 1)
                    yield

            def attention(b, i):
                def tile(n, *waits):
                    for s, k in waits:
                        wait(pe, s, b, k)
                    wait(pe, p_read[n % 2], b, n // 2)
                    return p_tile(n)

                a_done(pe, b, NA - 1)
                place = tile(P_MEAN3)
                mm(place[:, 0:T], mean_mat[:, :], h2[i][:, :], start=True, stop=True).then_inc(p_mm.sem, 1)
                yield
                yield
                place = tile(P_VAR3, (p_squared, 1))
                mm(place[:, 0:T], mean_mat[:, :], a_square[:, :], start=True, stop=True).then_inc(p_mm.sem, 1)
                yield
                yield
                place = tile(P_Q, (xn3_ready, 1))
                mm(place[:, 0:TP], qkv_sb[:, 0, :], xn3[:, :], start=True, stop=True).then_inc(p_mm.sem, 1)
                yield
                place = tile(P_K)
                mm(place[:, 0:T], qkv_sb[:, 1, :], xn3[:, 0:T], start=True, stop=True).then_inc(p_mm.sem, 1)
                yield
                place = tile(P_V)
                for s in range(3):
                    ins = mm(place[:, P * s:P * (s + 1)], xn3[:, P * s:P * (s + 1)], qkv_sb[:, 2, :],
                             start=True, stop=True)
                ins.then_inc(p_mm.sem, 1)
                yield
                place = tile(P_LOW)
                mm(place[0:1, 0:T], k_sum[:, :], q_t[:, 0:T], start=True, stop=True).then_inc(p_mm.sem, 1)
                yield
                for s in range(3):
                    place = tile(P_SCORE + s)
                    if s == 0:
                        pe.wait_ge(low_step, 4)
                        for q in range(3):
                            mm(place[:, KEEP_AT + q:KEEP_AT + q + 1], keep_row[0:1, P * q:P * (q + 1)],
                               ones_row[0:1, 0:1], start=True, stop=True)
                    mm(place[:, 0:T], q_t[:, P * s:P * (s + 1)], k_t[:, :], start=True, stop=True)\
                        .then_inc(p_mm.sem, 1)
                    yield
                yield
                yield
                for s, (t0, n) in enumerate(TILES):
                    place = tile(P_PROBS + s, (probs_scaled, 3))
                    for q in range(3):
                        ins = pe.transpose(place[0:n, P * q:P * (q + 1)], probs[:, q, t0:t0 + n], ident[:, :])
                    ins.then_inc(p_mm.sem, 1)
                    yield
                p_done(pe, b, P_PROBS + 2)
                place = tile(P_ATTN)
                for s, (t0, n) in enumerate(TILES):
                    ins = mm(place[:, 0:T], v_sb[0:n, s, :], probs_t[0:n, s, 0:T], start=(s == 0), stop=(s == 2))
                ins.then_inc(p_mm.sem, 1)
                yield
                p_done(pe, b, P_ATTN)
                place = tile(P_MEAN4)
                mm(place[:, 0:T], mean_mat[:, :], cols(h3_all, b), start=True, stop=True).then_inc(p_mm.sem, 1)
                yield
                yield
                place = tile(P_VAR4, (p_squared, 2))
                mm(place[:, 0:T], mean_mat[:, :], a_square[:, :], start=True, stop=True).then_inc(p_mm.sem, 1)
                yield
                yield
                place = tile(P_ROUTER, (xn4_ready, 1))
                for s in range(3):
                    ins = mm(place[:, E * s:E * (s + 1)], xn4[:, P * s:P * (s + 1)], router_sb[:, :],
                             start=True, stop=True)
                ins.then_inc(p_mm.sem, 1)
                yield
                yield
                place = tile(P_GATES, (router_step, 4))
                for s in range(3):
                    ins = pe.transpose(place[0:E, P * s:P * (s + 1)], r_prob[:, s, :], ident[:, :])
                ins.then_inc(p_mm.sem, 1)

            def in_parts(out, hi, low, w_hi, w_low, start, stop):
                for k, (w, x) in enumerate(((w_hi, hi), (w_low, hi), (w_hi, low))):
                    ins = mm(out, w.bitcast(F32R), x.bitcast(F32R), start=(start and k == 0), stop=(stop and k == 2))
                return ins

            def up(b, i, e, banks, between=lambda: None):
                for f in range(2):
                    at = slice(256 * e + P * f, 256 * e + P * (f + 1))
                    ins = in_parts(banks[:, f, 0:TE], x_hi_wide[i], x_low_wide[i], weights_hi[:, at], weights_low[:, at], True, True)
                    if f == 0:
                        between()
                ins.then_inc(up_mm.sem, 1)

            def set_cols(b, k):
                return bass.ds((b - SET * k) * T, TE)

            def gate_row(b, e, k, bank):
                mm(bank[:, 0:TE], pick_gate[:, e:e + 1].to_broadcast([2 * E, P]).bitcast(F32R),
                   gates_hl[k][:, set_cols(b, k)].bitcast(F32R), start=True, stop=True).then_inc(gate_rows_mm.sem, 1)

            def biases(b, k, acc):
                mm(acc[:, 0:TE], moe1_b2_sb[:, :], gates_hl[k][:, set_cols(b, k)], start=True, stop=False)

            def down(b, e, acc):
                for f in range(2):
                    wait(pe, hid1_split[f], b, e + 1)
                    at = slice(HALF + 256 * e + P * f, HALF + 256 * e + P * (f + 1))
                    ins = in_parts(acc[:, 0:TE], hid1_hi_wide[e % HID][:, f, :], hid1_low_wide[e % HID][:, f, :],
                                   weights_hi[:, at], weights_low[:, at], False, e == E - 1 and f == 1)
                ins.then_inc(down_mm.sem, 1)

            LAG = 3

            def early_part(b, e):
                if b == 0 and e == 0:
                    pe.wait_ge(moe1_loaded, 32)
                    pe.wait_ge(pads_written, 7)
                    pe.wait_ge(weights_split, 2)
                    pe.wait_ge(gates_typed, 1)
                if e == 0:
                    wait(pe, x_split, b, 1)
                wait(pe, hid1_ready, b, e - 1)
                up(b, b % 2, e, (c_rows, a_bank)[e % 2])
                if e == LAG:
                    if b < SET - 2:
                        wait(pe, out_ready, b - 1, 1)
                    else:
                        for n in (NP - 2, NP - 1):
                            p_done(pe, B - 1, n)
                    biases(b, 0, early_sum(b))
                if e >= LAG:
                    down(b, e - LAG, early_sum(b))
                elif b:
                    down(b - 1, e + E - LAG, early_sum(b - 1))
                wait(pe, hid1_gated, b, e)
                gate_row(b, e, 0, y_bank)

            def nothing(*_):
                yield

            all_batches(pe, lambda: None, slot, front, experts, attention, nothing,
                        lambda: early_batches(early_part))
            for e in range(E - LAG, E):
                down(SET - 1, e, early_sum(SET - 1))
            pe.wait_ge(gates_typed, 2)

            def last_layer(b0):
                for k in range(2 * E):
                    b, i, e = b0 + k // E, k // E, k % E
                    if e == 0:
                        wait(pe, x_split, b, 1)
                        wait(pe, out_ready, b - 2, 1)
                    wait(pe, hid1_ready, b, e - 1)
                    up(b, i, e, (c_rows, a_bank)[e % 2], lambda: wait(pe, hid1_gated, b, e - 1))
                    gate_row(b, e, 1, (y_bank, f_bank)[e % 2])
                    if e == 0:
                        biases(b, 1, p_bank[:, i, :])
                    if k >= LAG:
                        was = k - LAG
                        down(b0 + was // E, was % E, p_bank[:, was // E, :])
                for e in range(E - LAG, E):
                    down(b0 + 1, e, p_bank[:, 1, :])

            late_batches(pe, last_layer)


def kernel(**inputs):
    import numpy as np
    import concourse.bacc as bacc
    from concourse.bass_utils import run_bass_kernel_spmd

    a = {name: np.asarray(v) for name, v in inputs.items()}
    batches, t_in, d_in = a["x"].shape
    tok_w = a["L0_tok_W"].T
    tok_tiles = np.zeros((P, 3, P), np.float32)
    tok_tiles[:, 0], tok_tiles[:, 1], tok_tiles[0:64, 2] = tok_w[0:128], tok_w[128:256], tok_w[256:320]

    def halves(v):
        return v.reshape(2, P, -1).transpose(1, 0, 2).reshape(P, -1)

    vectors = np.concatenate([
        a["L0_tok_b"][:, None], a["L0_tok_gamma"][:, None], a["L0_tok_beta"][:, None],
        a["L0_attn_ln_g"][:, None], a["L0_attn_ln_b"][:, None], halves(a["L0_attn_conv_b"]),
        halves(a["L0_attn_b_dt"]), halves(a["L0_attn_D"]), halves(a["L0_attn_A_log"]),
        a["L1_ffn_b1"].reshape(16, P).T,
    ], axis=1)
    moe0 = np.concatenate([
        a["L0_ffn_w1"],
        a["L0_ffn_w2"].reshape(8, 4, P, P).transpose(0, 2, 1, 3).reshape(8, P, 512),
        a["L0_ffn_b1"].reshape(8, 4, P).transpose(0, 2, 1), a["L0_ffn_b2"][:, :, None],
    ], axis=2)
    arrays = {
        "x_t": a["x"].transpose(2, 0, 1),
        "tok_w": tok_tiles,
        "vec_in": vectors,
        "conv_w": a["L0_attn_conv_w"][:, 0, :].T,
        "w_in": a["L0_attn_W_in"].T,
        "w_x": halves(a["L0_attn_W_x"].T).reshape(P, 2, -1),
        "w_dt": a["L0_attn_W_dt"].T,
        "w_out": halves(a["L0_attn_W_out"].T).reshape(P, 2, -1),
        "gate_w": a["L0_ffn_gate_w"],
        "gate_b": a["L0_ffn_gate_b"][None],
        "moe0": moe0,
        "qkv_w": a["L1_attn_kernel"].transpose(1, 0, 2),
        "router_w": a["L1_ffn_Wg"],
        "moe1_w1": a["L1_ffn_W1"].transpose(1, 0, 2),
        "moe1_w2": a["L1_ffn_W2"].reshape(8, 2, P, P).transpose(2, 0, 1, 3),
        "moe1_b2": a["L1_ffn_b2"],
    }
    arrays = {name: np.ascontiguousarray(v) for name, v in arrays.items()}
    t = t_in - 4
    nc = bacc.Bacc("TRN2", target_bir_lowering=False, num_devices=1)
    aps = {n: nc.dram_tensor(n, v.shape, F32, kind="ExternalInput").ap() for n, v in arrays.items()}
    aps["out"] = nc.dram_tensor("out", (P, batches * t), F32, kind="ExternalOutput").ap()
    aps["gates_dram"] = nc.dram_tensor("gates_dram", (batches, 8, t), F32).ap()
    aps["mask_dram"] = nc.dram_tensor("mask_dram", (2, 2, batches // 2, 8, t), F32).ap()
    aps["b_dram"] = nc.dram_tensor("b_dram", (2, 16, t), F32).ap()
    audio_tower(nc, **aps)
    got = run_bass_kernel_spmd(nc, [arrays], core_ids=[0]).results[0]["out"]
    return np.ascontiguousarray(got.reshape(P, batches, t).transpose(1, 2, 0))
```
